# Optimizing a Trainium2 kernel written in Bass

```python
import numpy as np
import jax
import jax.numpy as jnp

def _softmax(x, axis=-1):
    return jax.nn.softmax(x, axis=axis)

def _gelu(x):
    return jax.nn.gelu(x, approximate=True)

def _silu(x):
    return jax.nn.silu(x)

def _sigmoid(x):
    return jax.nn.sigmoid(x)

def _layernorm(x, axis=-1, eps=1e-05):
    m = jnp.mean(x, axis=axis, keepdims=True)
    v = jnp.var(x, axis=axis, keepdims=True)
    return (x - m) / jnp.sqrt(v + eps)

def _scatter_add(tgt, idx, src, axis=0):
    return tgt.at[idx].add(src)

def _segment_sum(src, seg, n):
    return jax.ops.segment_sum(src, seg, n)
kernel_name = 'mk_metaformer_d1_conv_nchw128_r2_3658d8'

def setup_inputs(seed: int=0):
    np.random.seed(seed)
    _w = jnp.asarray

    def _rec_inputs():
        import jax
        import jax.numpy as jnp
        _gk = jax.random.key(seed)
        x = -0.0002023 + 1 * jax.random.normal(jax.random.fold_in(_gk, 1), (16, 64, 56, 56), jnp.float32)
        return x
    x = _rec_inputs()

    def _L0_conv_setup():
        import jax, jax.numpy as jnp
        import numpy as np
        DIM = 64
        QK = 64
        NWIN = 7
        HEADS = 8
        TOPK = 4
        SCALE = QK ** (-0.5)
        key = jax.random.key(seed)
        ks = jax.random.split(key, 6)
        N, H, W = (16, 56, 56)
        x = jax.random.normal(ks[0], (N, DIM, H, W), jnp.float32)
        qkv_w = jax.random.normal(ks[1], (DIM, 2 * QK + DIM), jnp.float32) * 0.02
        qkv_b = jnp.zeros((2 * QK + DIM,), jnp.float32)
        lepe_w = jax.random.normal(ks[2], (DIM, 1, 3, 3), jnp.float32) * 0.1
        wo_w = jax.random.normal(ks[3], (DIM, DIM), jnp.float32) * 0.02
        wo_b = jnp.zeros((DIM,), jnp.float32)
        return dict(x=x, qkv_w=qkv_w, qkv_b=qkv_b, lepe_w=lepe_w, wo_w=wo_w, wo_b=wo_b)
    _L0_conv_all = _L0_conv_setup()
    _L0_conv_in = {k: v for k, v in _L0_conv_all.items() if k in ('qkv_w', 'qkv_b', 'lepe_w', 'wo_w', 'wo_b')}
    del _L0_conv_all

    def _L0_ffn_setup():
        import jax, jax.numpy as jnp
        import numpy as np
        PADDED_SL = 4096
        TEMPERATURE = 1.0
        SIGMA_POW = 0.25

        def _stu_conv(phi, u, n):
            b, sl, d = u.shape
            sgn = jnp.where(jnp.arange(sl) % 2 == 0, 1.0, -1.0).astype(u.dtype)
            sgn3 = sgn[None, :, None]
            Vf = jnp.fft.rfft(phi, n=n, axis=0)
            Uf_p = jnp.fft.rfft(u, n=n, axis=1)
            Uf_m = jnp.fft.rfft(u * sgn3, n=n, axis=1)
            U_plus = jnp.fft.irfft(Vf[None, :, :, None] * Uf_p[:, :, None, :], n=n, axis=1)[:, :sl]
            U_minus = jnp.fft.irfft(Vf[None, :, :, None] * Uf_m[:, :, None, :], n=n, axis=1)[:, :sl]
            U_minus = U_minus * sgn[None, :, None, None]
            return (U_plus, U_minus)

        def _compute_spectral(u, sigma, phi, Mpp, Mpm):
            U_plus, U_minus = _stu_conv(phi, u, PADDED_SL)
            s = sigma ** SIGMA_POW
            out = jnp.einsum('btkd,k,kde->bte', U_plus, s, Mpp)
            out = out + jnp.einsum('btkd,k,kde->bte', U_minus, s, Mpm)
            return out

        def _compute_ar_u(Mu, u):
            sl = u.shape[1]
            out = jnp.zeros(u.shape[:2] + (Mu.shape[-1],), dtype=u.dtype)
            for i in range(Mu.shape[0]):
                ui = jnp.pad(u, ((0, 0), (i, 0), (0, 0)))[:, :sl]
                out = out + jnp.einsum('btd,de->bte', ui, Mu[i])
            return out

        def _stu(u, sigma, phi, Mu, Mpp, Mpm):
            return _compute_spectral(u, sigma, phi, Mpp, Mpm) + _compute_ar_u(Mu, u)
        key = jax.random.key(seed)
        ks = jax.random.split(key, 8)
        b, sl, d, K, k_u = (2, 2048, 64, 16, 3)
        x = jax.random.normal(ks[0], (b, sl, d), dtype=jnp.float32)
        sigma = jax.random.uniform(ks[1], (K,), dtype=jnp.float32, minval=0.001, maxval=1.0)
        phi = jax.random.normal(ks[2], (sl, K), dtype=jnp.float32) / np.sqrt(sl)
        M_u = jax.random.normal(ks[3], (4, k_u, d, d), dtype=jnp.float32) * 0.02
        M_phi_plus = jax.random.normal(ks[4], (4, K, d, d), dtype=jnp.float32) * 0.02
        M_phi_minus = jax.random.normal(ks[5], (4, K, d, d), dtype=jnp.float32) * 0.02
        log_weights = jnp.ones((4,), dtype=jnp.float32)
        u01 = jax.random.uniform(ks[6], (4,), dtype=jnp.float32, minval=1e-06, maxval=1.0 - 1e-06)
        gumbel = -jnp.log(-jnp.log(u01))
        return {'x': x, 'sigma': sigma, 'phi': phi, 'M_u': M_u, 'M_phi_plus': M_phi_plus, 'M_phi_minus': M_phi_minus, 'log_weights': log_weights, 'gumbel': gumbel}
    _L0_ffn_all = _L0_ffn_setup()
    _L0_ffn_in = {k: v for k, v in _L0_ffn_all.items() if k in ('sigma', 'phi', 'M_u', 'M_phi_plus', 'M_phi_minus', 'log_weights', 'gumbel')}
    del _L0_ffn_all
    return {'x': x, 'L0_conv_qkv_w': _L0_conv_in['qkv_w'], 'L0_conv_qkv_b': _L0_conv_in['qkv_b'], 'L0_conv_lepe_w': _L0_conv_in['lepe_w'], 'L0_conv_wo_w': _L0_conv_in['wo_w'], 'L0_conv_wo_b': _L0_conv_in['wo_b'], 'L0_ffn_sigma': _L0_ffn_in['sigma'], 'L0_ffn_phi': _L0_ffn_in['phi'], 'L0_ffn_M_u': _L0_ffn_in['M_u'], 'L0_ffn_M_phi_plus': _L0_ffn_in['M_phi_plus'], 'L0_ffn_M_phi_minus': _L0_ffn_in['M_phi_minus'], 'L0_ffn_log_weights': _L0_ffn_in['log_weights'], 'L0_ffn_gumbel': _L0_ffn_in['gumbel']}

def reference(x, L0_conv_qkv_w, L0_conv_qkv_b, L0_conv_lepe_w, L0_conv_wo_w, L0_conv_wo_b, L0_ffn_sigma, L0_ffn_phi, L0_ffn_M_u, L0_ffn_M_phi_plus, L0_ffn_M_phi_minus, L0_ffn_log_weights, L0_ffn_gumbel):
    import jax
    import jax.numpy as jnp

    def _L0_conv_ref(x, qkv_w, qkv_b, lepe_w, wo_w, wo_b):
        import jax, jax.numpy as jnp
        import numpy as np
        DIM = 64
        QK = 64
        NWIN = 7
        HEADS = 8
        TOPK = 4
        SCALE = QK ** (-0.5)
        N, C, H, W = x.shape
        hh, ww = (H // NWIN, W // NWIN)
        w2 = hh * ww
        P2 = NWIN * NWIN
        xh = jnp.transpose(x, (0, 2, 3, 1))
        xw = xh.reshape(N, NWIN, hh, NWIN, ww, C).transpose(0, 1, 3, 2, 4, 5).reshape(N, P2, hh, ww, C)
        qkv = xw @ qkv_w + qkv_b
        q = qkv[..., :QK]
        kv = qkv[..., QK:]
        q_pix = q.reshape(N, P2, w2, QK)
        kv_pix = kv.reshape(N, P2, w2, QK + DIM)
        q_win = q.mean((2, 3))
        k_win = kv[..., :QK].mean((2, 3))
        v = kv[..., QK:]
        v_full = v.reshape(N, NWIN, NWIN, hh, ww, DIM).transpose(0, 5, 1, 3, 2, 4).reshape(N, DIM, H, W)
        lepe = jax.lax.conv_general_dilated(v_full, lepe_w, (1, 1), 'SAME', feature_group_count=DIM, dimension_numbers=('NCHW', 'OIHW', 'NCHW'))
        lepe = jnp.transpose(lepe, (0, 2, 3, 1))
        qd = jax.lax.stop_gradient(q_win)
        kd = jax.lax.stop_gradient(k_win)
        logits = qd * SCALE @ jnp.swapaxes(kd, -1, -2)
        topk_logit, r_idx = jax.lax.top_k(logits, TOPK)
        r_weight = jax.nn.softmax(topk_logit, axis=-1)
        kv_sel = kv_pix[jnp.arange(N)[:, None, None], r_idx]
        k_sel = kv_sel[..., :QK]
        v_sel = kv_sel[..., QK:]
        hd = QK // HEADS
        hdv = DIM // HEADS
        qh = q_pix.reshape(N, P2, w2, HEADS, hd)
        kh = k_sel.reshape(N, P2, TOPK * w2, HEADS, hd)
        vh = v_sel.reshape(N, P2, TOPK * w2, HEADS, hdv)
        attn = jnp.einsum('npqhd,npkhd->nphqk', qh * SCALE, kh)
        attn = jax.nn.softmax(attn, axis=-1)
        out = jnp.einsum('nphqk,npkhd->npqhd', attn, vh).reshape(N, P2, w2, DIM)
        out = out.reshape(N, NWIN, NWIN, hh, ww, DIM).transpose(0, 1, 3, 2, 4, 5).reshape(N, H, W, DIM)
        out = out + lepe
        out = out @ wo_w + wo_b
        return jnp.transpose(out, (0, 3, 1, 2))

    def _L0_ffn_ref(x, sigma, phi, M_u, M_phi_plus, M_phi_minus, log_weights, gumbel):
        import jax, jax.numpy as jnp
        import numpy as np
        PADDED_SL = 4096
        TEMPERATURE = 1.0
        SIGMA_POW = 0.25

        def _stu_conv(phi, u, n):
            b, sl, d = u.shape
            sgn = jnp.where(jnp.arange(sl) % 2 == 0, 1.0, -1.0).astype(u.dtype)
            sgn3 = sgn[None, :, None]
            Vf = jnp.fft.rfft(phi, n=n, axis=0)
            Uf_p = jnp.fft.rfft(u, n=n, axis=1)
            Uf_m = jnp.fft.rfft(u * sgn3, n=n, axis=1)
            U_plus = jnp.fft.irfft(Vf[None, :, :, None] * Uf_p[:, :, None, :], n=n, axis=1)[:, :sl]
            U_minus = jnp.fft.irfft(Vf[None, :, :, None] * Uf_m[:, :, None, :], n=n, axis=1)[:, :sl]
            U_minus = U_minus * sgn[None, :, None, None]
            return (U_plus, U_minus)

        def _compute_spectral(u, sigma, phi, Mpp, Mpm):
            U_plus, U_minus = _stu_conv(phi, u, PADDED_SL)
            s = sigma ** SIGMA_POW
            out = jnp.einsum('btkd,k,kde->bte', U_plus, s, Mpp)
            out = out + jnp.einsum('btkd,k,kde->bte', U_minus, s, Mpm)
            return out

        def _compute_ar_u(Mu, u):
            sl = u.shape[1]
            out = jnp.zeros(u.shape[:2] + (Mu.shape[-1],), dtype=u.dtype)
            for i in range(Mu.shape[0]):
                ui = jnp.pad(u, ((0, 0), (i, 0), (0, 0)))[:, :sl]
                out = out + jnp.einsum('btd,de->bte', ui, Mu[i])
            return out

        def _stu(u, sigma, phi, Mu, Mpp, Mpm):
            return _compute_spectral(u, sigma, phi, Mpp, Mpm) + _compute_ar_u(Mu, u)
        T = x.shape[1]
        outs = []
        for i, frac in enumerate((1, 2, 4, 8)):
            xi = x[:, :T // frac]
            si = _stu(xi, sigma, phi, M_u[i], M_phi_plus[i], M_phi_minus[i])
            si = jnp.pad(si, ((0, 0), (0, T - si.shape[1]), (0, 0)))
            outs.append(si)
        y_soft = jax.nn.softmax((log_weights + gumbel) / TEMPERATURE)
        y_hard = jax.nn.one_hot(jnp.argmax(y_soft), 4, dtype=y_soft.dtype)
        weights = y_hard - jax.lax.stop_gradient(y_soft) + y_soft
        stacked = jnp.stack(outs, axis=-1)
        return jnp.sum(stacked * weights, axis=-1)

    def _gn(v, G=32, eps=1e-05):
        B_, C_, H_, W_ = v.shape
        g = v.reshape(B_, G, C_ // G, H_, W_)
        m = jnp.mean(g, axis=(2, 3, 4), keepdims=True)
        s = jnp.var(g, axis=(2, 3, 4), keepdims=True)
        return ((g - m) / jnp.sqrt(s + eps)).reshape(v.shape)

    def _ln_c(v, eps=1e-06):
        m = jnp.mean(v, axis=1, keepdims=True)
        s = jnp.var(v, axis=1, keepdims=True)
        return (v - m) / jnp.sqrt(s + eps)

    def _ln_t(v, eps=1e-05):
        m = jnp.mean(v, axis=-1, keepdims=True)
        s = jnp.var(v, axis=-1, keepdims=True)
        return (v - m) / jnp.sqrt(s + eps)

    def _to_tokens(v):
        B_, C_, H_, W_ = v.shape
        return v.reshape(B_, C_, H_ * W_).transpose(0, 2, 1)

    def _from_tokens(t, like):
        B_, C_, H_, W_ = like.shape
        return t.transpose(0, 2, 1).reshape(B_, C_, H_, W_)
    x = x + _L0_conv_ref(_ln_c(x), L0_conv_qkv_w, L0_conv_qkv_b, L0_conv_lepe_w, L0_conv_wo_w, L0_conv_wo_b)
    t = _to_tokens(x)
    t = t + _L0_ffn_ref(_ln_t(t), L0_ffn_sigma, L0_ffn_phi, L0_ffn_M_u, L0_ffn_M_phi_plus, L0_ffn_M_phi_minus, L0_ffn_log_weights, L0_ffn_gumbel)
    x = _from_tokens(t, x)
    return x

_drawn_inputs = setup_inputs


def setup_inputs(seed=0):
    import zlib

    import numpy as np

    out = dict(_drawn_inputs(seed))
    spreads = {'L0_conv_qkv_b': (0.0, 0.564),
     'L0_conv_wo_b': (0.0, 0.1),
     'L0_ffn_log_weights': (1.0, 0.2)}
    factors = {'L0_conv_qkv_w': 7.074, 'L0_conv_lepe_w': 6.183, 'L0_conv_wo_w': 3.966}
    for name, (base, spread) in spreads.items():
        noise = np.random.default_rng([zlib.crc32(name.encode()), seed]).standard_normal(out[name].shape)
        drawn = base * np.exp(spread * noise) if base else spread * noise
        out[name] = jnp.asarray(drawn.astype(out[name].dtype))
    for name, factor in factors.items():
        out[name] = (out[name] * factor).astype(out[name].dtype)
    return out
```

```python
from contextlib import ExitStack

import concourse.bass as bass
from concourse import mybir

F32 = mybir.dt.float32
BF16 = mybir.dt.bfloat16
I32 = mybir.dt.int32
U32 = mybir.dt.uint32
ALU = mybir.AluOpType
ACT = mybir.ActivationFunctionType
AX = mybir.AxisListType

C = 64
SIDE = 56
TOKENS = SIDE * SIDE
NWIN = 7
WINDOWS = NWIN * NWIN
WS = SIDE // NWIN
PX = WS * WS
ROW = NWIN * PX
HEADS, HD = 8, 8
HP = HEADS // 2
TOPK = 4
KEYS = TOPK * PX
PAD = SIDE + 2
TERMS = [(0, 0), (0, 1), (0, 2), (1, 0), (1, 1), (2, 0)]
TR = len(TERMS) * HD
QROWS = 2 * TR
SROWS = QROWS + 6
SCALE = float(C) ** -0.5
A_AT = [2, 1, 1, 1, 1, 1, 0]


NF = 4096
NA, NB = 49, 64
AL = 34
PAIRS = AL // 2
KPHI = 16
KAR = 3
KAP = 2 * KPHI + KAR
BRANCHES = 4
CLASSES = [(0, 8), (8, 8), (16, 16), (32, 32)]
CUTS = [(3, 0, 16), (3, 16, 16), (3, 32, 16), (3, 48, 16), (2, 0, 32), (2, 32, 32), (1, 0, 64), (0, 0, 64)]



def attention(nc, x, qkv_w, qkv_b, lepe_w, wo_w, wo_b, mats, x2_dram, u_dram):
    n_img = x.shape[0]
    duos = n_img // 2
    xv = x.rearrange("n c h w -> (n c) (h w)")
    with ExitStack() as ctx:
        def sb(name, shape, dt=F32):
            return ctx.enter_context(nc.sbuf_tensor(name, shape, dt))

        def sem(name):
            return ctx.enter_context(nc.semaphore(name))

        q_dram = nc.dram_tensor("q_dram", (2, 3, NWIN, C, ROW), BF16).ap()
        k_dram = nc.dram_tensor("k_dram", (2, 3, C, TOKENS), BF16).ap()

        ones64 = sb("ones64", [128, 128])
        ident = sb("ident", [128, 128])
        identb = sb("identb", [128, 128], BF16)
        pick = sb("pick", [128, 128])
        wqk = sb("wqk", [128, 2 * C])
        wraw = sb("wraw", [128, 2 * C])
        wv = sb("wv", [128, C])
        bqk = sb("bqk", [128, 1])
        bk0 = sb("bk0", [C, 1])
        bv = sb("bv", [128, 1])
        taps = sb("taps", [128, 9])
        wo = sb("wo", [128, C])
        woh = sb("woh", [128, 2, C])
        wob = sb("wob", [128, 1])
        X = sb("X", [128, TOKENS])
        Vimg = sb("Vimg", [128, PAD, PAD])
        Kexp = [sb(f"Kexp{m}", [SROWS, HP, TOKENS], BF16) for m in range(2)]
        Vpx = [sb(f"Vpx{m}", [128, WINDOWS, HEADS, HD + 1]) for m in range(2)]
        idxrow = sb("idxrow", [1, 2, WINDOWS * TOPK], I32)
        Cen = sb("Cen", [128, ROW])
        Sq = sb("Sq", [128, ROW])
        Std = sb("Std", [128, ROW])
        Rstd = sb("Rstd", [128, ROW])
        eps = sb("eps", [128, 2])
        Xn = sb("Xn", [128, ROW])
        Qk = sb("Qk", [128, ROW])
        Res = sb("Res", [128, ROW])
        Part = [sb(f"Part{m}", [128, 3, ROW], BF16) for m in range(2)]
        Vt = sb("Vt", [128, NWIN, 2, PX])
        xm = sb("xm", [128, WINDOWS])
        xms = sb("xms", [128, WINDOWS])
        qw = sb("qw", [C, 2, WINDOWS])
        kw = sb("kw", [C, 2, WINDOWS])
        lg = sb("lg", [WINDOWS, 2, WINDOWS])
        top = sb("top", [WINDOWS, 2, 8])
        idx = sb("idx", [WINDOWS, 2, 8], U32)
        Qbd = [sb(f"Qbd{m}", [SROWS, HP, NWIN, 2, PX], BF16) for m in range(2)]
        Ksel = [sb(f"Ksel{m}", [SROWS, NWIN, HP, TOPK, PX], BF16) for m in range(2)]
        Vsel = [sb(f"Vsel{m}", [128, NWIN, 2, HEADS, HD + 1]) for m in range(2)]
        Mx = [sb(f"Mx{m}", [128, HP, NWIN]) for m in range(2)]
        Mr = sb("Mr", [128, HP * NWIN])
        Mb = [sb(f"Mb{m}", [128, 3, HP * NWIN], BF16) for m in range(2)]
        MT = [sb(f"MT{m}", [3 * HP * NWIN, 2, PX], BF16) for m in range(2)]
        Pr = [sb(f"Pr{k}", [128, 2, HP, 2, PX]) for k in range(2)]
        Osb = [sb(f"Osb{k}", [128, 4, 2, PX]) for k in range(2)]
        On = [sb(f"On{m}", [128, NWIN, 2, PX]) for m in range(2)]
        Rc = sb("Rc", [128, 512])
        Lp = sb("Lp", [128, ROW])

        ps = ctx.enter_context(nc.psum_tensor("ps", [128, 8, 512], F32))
        ST0, OB, MISC = 2, 6, 7

        gate = {e: sem(f"gate_{e}") for e in ("pe", "act", "dve", "pool", "sp")}
        w_loaded = sem("w_loaded")
        init_done = sem("init_done")
        woh_loaded = sem("woh_loaded")
        x_loaded = sem("x_loaded")
        mean_ready = sem("mean_ready")
        cen_ready = sem("cen_ready")
        sq_ready = sem("sq_ready")
        var_ready = sem("var_ready")
        std_ready = sem("std_ready")
        rstd_ready = sem("rstd_ready")
        xn_ready = sem("xn_ready")
        xm_ready = sem("xm_ready")
        xms_ready = sem("xms_ready")
        qk_ready = sem("qk_ready")
        v_ready = sem("v_ready")
        qk_sb = sem("qk_sb")
        part1 = sem("part1")
        res1 = sem("res1")
        part2 = sem("part2")
        part3 = sem("part3")
        parts_stored = sem("parts_stored")
        vt_sb = sem("vt_sb")
        vT_ready = sem("vT_ready")
        vpx_done = sem("vpx_done")
        win_ready = sem("win_ready")
        win_sb = sem("win_sb")
        logits_ready = sem("logits_ready")
        lg_sb = sem("lg_sb")
        top_ready = sem("top_ready")
        idx_ready = sem("idx_ready")
        idx_stored = sem("idx_stored")
        k_loaded = sem("k_loaded")
        q_loaded = sem("q_loaded")
        m_loaded = sem("m_loaded")
        k_gathered = sem("k_gathered")
        v_gathered = sem("v_gathered")
        s_ready = sem("s_ready")
        max_done = sem("max_done")
        m_split = sem("m_split")
        st_ready = sem("st_ready")
        exp_done = sem("exp_done")
        pv_done = sem("pv_done")
        o_copied = sem("o_copied")
        misc_ready = sem("misc_ready")
        misc_free = sem("misc_free")
        on_ready = sem("on_ready")
        tap_done = sem("tap_done")
        x2_stored = sem("x2_stored")
        u_stored = sem("u_stored")

        block = ctx.enter_context(nc.Block())
        LAST = NWIN - 1
        N_W = 3 + 6 * HD + 12
        UNITS = 2 * NWIN
        MISC_DUO = 7 * NWIN

        def unit_of(d, i, m):
            return d * UNITS + i * 2 + m

        def misc_no(d, i, m, what, last=False):
            order = [(0, "sum0"), (0, "max"), (0, "sum1"), (1, "sum0")] + ([] if last else [(1, "max")]) \
                + [(1, "sum1"), (1, "out")]
            return d * MISC_DUO + i * 7 + (1 + order.index((m, what)))

        def hold(eng, name, s, value):
            eng.wait_ge(s, value)
            eng.sem_inc(gate[name], 1)

        @block.sync
        def _(sp):
            sp.dma_start(ones64[:, :], mats[0]).then_inc(w_loaded, 16)
            sp.dma_start(ident[:, :], mats[1]).then_inc(w_loaded, 16)
            sp.dma_start(pick[:, :], mats[2]).then_inc(w_loaded, 16)
            bias = qkv_b.rearrange("(s p h d) -> s h d p", s=3, p=HP, h=2)
            for h2 in range(2):
                q = HP * HD
                for out, s in ((bqk[q * h2:q * h2 + q, :], 0), (bqk[C + q * h2:C + q * h2 + q, :], 1),
                               (bk0[q * h2:q * h2 + q, :], 1)):
                    with nc.allow_non_contiguous_dma(reason="32 words"):
                        for e in range(HD):
                            sp.dma_start(out[HP * e:HP * e + HP], bias[s, h2, e:e + 1, :].rearrange("a p -> p a"))\
                              .then_inc(w_loaded, 16)
            for m in range(2):
                half = slice(C * m, C * m + C)
                sp.dma_start(wraw[half, :], qkv_w[:, 0:2 * C]).then_inc(w_loaded, 16)
                sp.dma_start(wv[half, :], qkv_w[:, 2 * C:3 * C]).then_inc(w_loaded, 16)
                sp.dma_start(bv[half, :], qkv_b[2 * C:3 * C].rearrange("(c a) -> c a", a=1)).then_inc(w_loaded, 16)
                sp.dma_start(taps[half, :], lepe_w.rearrange("c a i j -> c (a i j)")).then_inc(w_loaded, 16)
                sp.dma_start(wo[half, :], wo_w).then_inc(w_loaded, 16)
                sp.dma_start(wob[half, :], wo_b.rearrange("(c a) -> c a", a=1)).then_inc(w_loaded, 16)
            sp.wait_ge(init_done, 5)
            wo4 = wo_w.rearrange("(g j d) e -> j d g e", g=2, j=4)
            for j in range(4):
                sp.dma_start(woh[32 * j:32 * j + HD, :, :], wo4[j]).then_inc(woh_loaded, 16)

            def load_q(m, i, g):
                hold(sp, "sp", st_ready, g * NWIN + NWIN)
                for h2 in range(2):
                    for t, (part, _) in enumerate(TERMS):
                        r = TR * h2 + HD * t
                        src = q_dram[m, part].rearrange("i (h d p) (w x) -> i h d (p w) x", h=2, p=HP, x=PX)
                        sp.dma_start(Qbd[m][r:r + HD, :, :, h2, :].rearrange("d p w x -> d (p w) x"),
                                     src[bass.ds(i, 1), h2].rearrange("a d n x -> (a d) n x")).then_inc(q_loaded, 16)

            def load_max(m, no):
                hold(sp, "sp", misc_free, no + 2)
                for h2 in range(2):
                    for k in range(3):
                        r = QROWS + 3 * h2 + k
                        sp.dma_start(Qbd[m][r:r + 1, :, :, h2, :].rearrange("a p w x -> a (p w) x"),
                                     MT[m][HP * NWIN * k:HP * NWIN * (k + 1), h2, :]).then_inc(m_loaded, 16)

            with sp.Fori(0, duos) as d:
                hold(sp, "sp", x2_stored, d * (16 * NWIN) + 16)
                sp.dma_start(X[:, :], xv[bass.ds(d * 128, 128), :]).then_inc(x_loaded, 16)
                with sp.Fori(0, NWIN) as i:
                    for m in range(2):
                        hold(sp, "sp", part3, d * UNITS + i * 2 + (m + 1))
                        sp.dma_start(q_dram[m].rearrange("k i c x -> i c k x")[bass.ds(i, 1)]
                                     .rearrange("a c k x -> (a c) k x"), Part[m][0:C]).then_inc(parts_stored, 16)
                        sp.dma_start(k_dram[m].rearrange("k c x -> c k x")[:, :, bass.ds(i * ROW, ROW)],
                                     Part[m][C:2 * C]).then_inc(parts_stored, 16)
                hold(sp, "sp", parts_stored, d * (32 * UNITS) + 32 * UNITS + 16)
                for m in range(2):
                    for h2 in range(2):
                        for t, (_, part) in enumerate(TERMS):
                            r = TR * h2 + HD * t
                            src = k_dram[m, part].rearrange("(h d p) x -> h d (p x)", h=2, p=HP)[h2]
                            sp.dma_start(Kexp[m][r:r + HD].rearrange("d p x -> d (p x)"), src)\
                              .then_inc(k_loaded, 16)
                hold(sp, "sp", idx_ready, d * 2 + 2)
                for m in range(2):
                    sp.dma_start(idxrow[0:1, m, :].rearrange("a (w k) -> a w k", k=TOPK),
                                 idx[:, m, 0:TOPK].bitcast(I32)).then_inc(idx_stored, 16)
                load_q(0, 0, unit_of(d, 0, 0))
                load_max(0, d * MISC_DUO)

                def rows(i, last):
                    load_q(1, i, unit_of(d, i, 1))
                    load_max(1, misc_no(d, i, 0, "max"))
                    if not last:
                        load_q(0, i + 1, unit_of(d, i, 2))
                        load_max(0, misc_no(d, i, 1, "max"))

                with sp.Fori(0, LAST) as i:
                    rows(i, False)
                rows(LAST, True)
                with sp.Fori(0, NWIN) as i:
                    hold(sp, "sp", xn_ready, d * UNITS + i + (NWIN + 1))
                    sp.dma_start(x2_dram[bass.ds(d * 128, 128), bass.ds(i * ROW, ROW)],
                                 X[:, bass.ds(i * ROW, ROW)]).then_inc(x2_stored, 16)
                    sp.dma_start(u_dram[bass.ds(d * 128, 128), bass.ds(i * ROW, ROW)],
                                 Xn[:, :]).then_inc(u_stored, 16)
            sp.wait_ge(x2_stored, duos * 16 * NWIN + 16)
            sp.wait_ge(u_stored, duos * 16 * NWIN + 16)

        @block.gpsimd
        def _(pool):
            for m in range(2):
                nc.gpsimd.memset(Qbd[m][:], 0.0)
            nc.gpsimd.memset(eps[:, 0:1], 1e-6)
            nc.gpsimd.memset(eps[:, 1:2], 1e-5)
            nc.gpsimd.memset(Vimg[:], 0.0)
            nc.gpsimd.memset(woh[:], 0.0).then_inc(init_done, 1)
            pool.wait_ge(init_done, 5)
            regs = [pool.alloc_register(f"pool_win{k}") for k in range(TOPK)]

            with pool.Fori(0, duos) as d:
                hold(pool, "pool", k_loaded, d * (16 * 24) + 16 * 24)
                hold(pool, "pool", idx_stored, d * 32 + 32)
                with pool.Fori(0, NWIN) as i:
                    for m in range(2):
                        hold(pool, "pool", st_ready, unit_of(d, i, m) * NWIN + NWIN)
                        src = Kexp[m][:, :, :].bitcast(I32)
                        dst = Ksel[m][:, :, :, :, :].bitcast(I32)
                        for w in range(NWIN):
                            pool.load(regs, idxrow[0:1, m, bass.ds((i * NWIN + w) * TOPK, TOPK)])
                            win = [pool.snap(r, min_val=0, max_val=WINDOWS - 1) for r in regs]
                            for k in range(TOPK):
                                nc.gpsimd.tensor_copy(dst[:, w, :, k, :],
                                                      src[:, :, bass.ds(win[k] * (PX // 2), PX // 2)])\
                                    .then_inc(k_gathered, 1)

        @block.scalar
        def _(act):
            act.wait_ge(w_loaded, 16 * N_W)
            nc.scalar.activation(identb[:, :], ident[:, :], ACT.Copy).then_inc(init_done, 1)
            for k in range(2):
                nc.scalar.activation(wqk[:, C * k:C * k + C].rearrange("c (h d p) -> c h d p", h=2, p=HP),
                                     wraw[:, C * k:C * k + C].rearrange("c (p h d) -> c h d p", h=2, p=HP),
                                     ACT.Copy).then_inc(init_done, 1)
            act.wait_ge(init_done, 5)
            regs = [act.alloc_register(f"act_win{k}") for k in range(TOPK)]

            def deviation(tt, which):
                hold(act, "act", cen_ready, tt + 1)
                nc.scalar.activation(Sq[:, :], Cen[:, :], ACT.Square).then_inc(sq_ready, 1)
                hold(act, "act", var_ready, tt + 1)
                nc.scalar.activation(Std[:, :], ps[:, 1, 0:ROW], ACT.Sqrt, bias=eps[:, which:which + 1])\
                    .then_inc(std_ready, 1)

            def gather_v(m, i, w):
                act.load(regs, idxrow[0:1, m, bass.ds((i * NWIN + w) * TOPK, TOPK)])
                win = [act.snap(r, min_val=0, max_val=WINDOWS - 1) for r in regs]
                for k in range(TOPK):
                    half = slice(PX * (k % 2), PX * (k % 2) + PX)
                    nc.scalar.activation(Vsel[m][half, w, k // 2], Vpx[m][half, bass.ds(win[k], 1)],
                                         ACT.Copy).then_inc(v_gathered, 1)

            with act.Fori(0, duos) as d:
                with act.Fori(0, NWIN) as i:
                    t = d * NWIN + i
                    deviation(d * UNITS + i, 0)
                    for m in range(2):
                        hold(act, "act", qk_ready, t * 2 + (m + 1))
                        nc.scalar.activation(
                            Qk[:, :].rearrange("c (w a b) -> c w a b", w=NWIN, a=WS),
                            ps[:, 2 + m, 0:ROW].rearrange("c (a w b) -> c w a b", w=NWIN, a=WS),
                            ACT.Identity, bias=bqk[:, 0:1]).then_inc(qk_sb, 1)
                        hold(act, "act", qk_sb, t * 2 + (m + 1))
                        hold(act, "act", parts_stored, t * 64 + 16)
                        nc.scalar.activation(Part[m][:, 0, :], Qk[:, :], ACT.Copy).then_inc(part1, 1)
                        hold(act, "act", res1, t * 2 + (m + 1))
                        nc.scalar.activation(Part[m][:, 1, :], Res[:, :], ACT.Copy).then_inc(part2, 1)
                        hold(act, "act", part3, t * 2 + (m + 1))
                    hold(act, "act", v_ready, t + 1)
                    nc.scalar.activation(
                        Vimg[:, bass.ds(i * WS + 1, WS), 1:1 + SIDE],
                        ps[:, 4, 0:ROW].rearrange("c (a x) -> c a x", a=WS), ACT.Identity, bias=bv[:, 0:1])
                    for k in range(2):
                        nc.scalar.activation(Vt[:, :, k, :].rearrange("c w (a b) -> c w a b", a=WS),
                                             ps[:, 4, 0:ROW].rearrange("c (a w b) -> c w a b", w=NWIN, a=WS),
                                             ACT.Identity, bias=bv[:, 0:1]).then_inc(vt_sb, 1)
                    for m in range(2):
                        hold(act, "act", vT_ready, t * 2 + (m + 1))
                        nc.scalar.activation(Vpx[m][:, bass.ds(i * NWIN, NWIN), :, 0:HD],
                                             ps[:, 5 + 2 * m, 0:ROW].rearrange("q (w h e) -> q w h e", w=NWIN, h=HEADS),
                                             ACT.Copy).then_inc(vpx_done, 1)
                hold(act, "act", idx_stored, d * 32 + 32)
                hold(act, "act", vpx_done, d * UNITS + UNITS)
                for w in range(NWIN):
                    gather_v(0, 0, w)

                def unit(m, i, nxt, nm, ni, last):
                    g = unit_of(d, i, m)
                    if nxt:
                        hold(act, "act", pv_done, g * NWIN + 2)
                    for w in range(NWIN):
                        n = g * NWIN + w
                        k = (m * NWIN + w) % 2
                        hold(act, "act", st_ready, n + (1 + 14))
                        hold(act, "act", pv_done, n + 1)
                        nc.scalar.activation(Pr[k][:].rearrange("q c p h x -> q (c p h x)"),
                                             ps[:, ST0 + 2 * k:ST0 + 2 * k + 2, :].rearrange("q a b -> q (a b)"),
                                             ACT.Exp, scale=SCALE).then_inc(exp_done, 1)
                        if nxt:
                            gather_v(nm, ni, w)
                        if w in (4, LAST):
                            sub = w // 2 - 2
                            nw = 4 - sub
                            hold(act, "act", pv_done, g * NWIN + (2 + 4 + 3 * sub))
                            hold(act, "act", on_ready, g * 2 + (sub + 1))
                            nc.scalar.activation(Osb[sub][:, 0:nw].rearrange("c w a q -> c (w a q)"),
                                                 ps[:, OB, 0:nw * 128], ACT.Copy).then_inc(o_copied, 1)

                def rows(i, last):
                    unit(0, i, True, 1, i, last)
                    unit(1, i, not last, 0, i + 1, last)

                with act.Fori(0, LAST) as i:
                    rows(i, False)
                rows(LAST, True)
                with act.Fori(0, NWIN) as i:
                    deviation(d * UNITS + i + NWIN, 1)

        @block.vector
        def _(dve):
            for m in range(2):
                nc.vector.memset(Vpx[m][:], 1.0)
                last = nc.vector.memset(Kexp[m][QROWS:SROWS], -1.0)
            last.then_inc(init_done, 1)
            nc.vector.memset(ps[:, OB, :], 1.0).then_inc(o_copied, 1)
            nc.vector.memset(Mr[:, :], 0.0).then_inc(max_done, 2)
            nc.vector.memset(xm[:, :], 0.0).then_inc(exp_done, 2)
            nc.vector.memset(top[:], 0.0).then_inc(pv_done, 2)
            nc.vector.memset(lg[:], 0.0).then_inc(st_ready, 14)
            nc.vector.memset(Sq[:, 0:8], 0.0).then_inc(misc_free, 1)
            nc.vector.memset(Rc[:, 0:8], 0.0).then_inc(on_ready, 2)
            nc.vector.memset(Xn[:, 0:8], 0.0).then_inc(parts_stored, 16)
            nc.vector.memset(Res[:, 0:8], 0.0).then_inc(x2_stored, 16)
            nc.vector.memset(Cen[:, 0:8], 0.0).then_inc(u_stored, 16)
            dve.wait_ge(w_loaded, 16 * N_W)

            def norm(i, tt):
                hold(dve, "dve", mean_ready, tt + 1)
                nc.vector.tensor_tensor(Cen[:, :], X[:, bass.ds(i * ROW, ROW)], ps[:, 0, 0:ROW], ALU.subtract)\
                    .then_inc(cen_ready, 1)
                hold(dve, "dve", std_ready, tt + 1)
                nc.vector.reciprocal(Rstd[:, :], Std[:, :]).then_inc(rstd_ready, 1)
                hold(dve, "dve", rstd_ready, tt + 1)
                nc.vector.tensor_tensor(Xn[:, :], Cen[:, :], Rstd[:, :], ALU.mult).then_inc(xn_ready, 1)

            def row_max(m, w, g):
                for half in range(2):
                    hold(dve, "dve", s_ready, g * 14 + (2 * w + half + 1))
                    nc.vector.tensor_reduce(Mx[m][:, 2 * half:2 * half + 2, w],
                                            ps[:, half, :].rearrange("q (p k) -> q p k", p=2),
                                            AX.X, ALU.max).then_inc(max_done, 1)

            def split_max(m, g):
                flat = Mx[m][:].rearrange("q p w -> q (p w)")
                hold(dve, "dve", max_done, g * 14 + 16)
                nc.vector.tensor_copy(Mb[m][:, 0, :], flat).then_inc(m_split, 1)
                hold(dve, "dve", m_split, g * 4 + 1)
                nc.vector.tensor_tensor(Mr[:, :], flat, Mb[m][:, 0, :], ALU.subtract).then_inc(m_split, 1)
                hold(dve, "dve", m_split, g * 4 + 2)
                nc.vector.tensor_copy(Mb[m][:, 1, :], Mr[:, :]).then_inc(m_split, 1)
                hold(dve, "dve", m_split, g * 4 + 3)
                nc.vector.tensor_tensor(Mb[m][:, 2, :], Mr[:, :], Mb[m][:, 1, :], ALU.subtract).then_inc(m_split, 1)

            def copy_max(m, no):
                hold(dve, "dve", misc_ready, no + 1)
                nc.vector.tensor_copy(MT[m][:].rearrange("r h x -> r (h x)"),
                                      ps[:, MISC, :].bitcast(BF16)[0:3 * HP * NWIN, 0:128]).then_inc(misc_free, 1)

            def normalise(m, sub, on, no):
                nw = 4 - sub
                hold(dve, "dve", misc_ready, no + 1)
                hold(dve, "dve", on_ready, on + 2)
                nc.vector.reciprocal(Rc[:, 0:nw * 128], ps[:, MISC, 0:nw * 128]).then_inc(misc_free, 1)
                hold(dve, "dve", misc_free, no + 2)
                nc.vector.tensor_tensor(On[m][:, 4 * sub:4 * sub + nw].rearrange("c w a q -> c (w a q)"),
                                        Osb[sub][:, 0:nw].rearrange("c w a q -> c (w a q)"),
                                        Rc[:, 0:nw * 128], ALU.mult).then_inc(on_ready, 1)

            with dve.Fori(0, duos) as d:
                hold(dve, "dve", x_loaded, d * 16 + 16)
                with dve.Fori(0, NWIN) as i:
                    t = d * NWIN + i
                    tt = d * UNITS + i
                    hold(dve, "dve", u_stored, d * (16 * NWIN) + 16)
                    norm(i, tt)
                    hold(dve, "dve", xn_ready, tt + 1)
                    nc.vector.tensor_reduce(xm[:, bass.ds(i * NWIN, NWIN)],
                                            Xn[:, :].rearrange("c (a w b) -> c w a b", a=WS, w=NWIN),
                                            AX.XY, ALU.add).then_inc(xm_ready, 1)
                    for m in range(2):
                        hold(dve, "dve", part1, t * 2 + (m + 1))
                        nc.vector.tensor_tensor(Res[:, :], Qk[:, :], Part[m][:, 0, :], ALU.subtract).then_inc(res1, 1)
                        hold(dve, "dve", part2, t * 2 + (m + 1))
                        nc.vector.tensor_tensor(Part[m][:, 2, :], Res[:, :], Part[m][:, 1, :], ALU.subtract)\
                            .then_inc(part3, 1)
                hold(dve, "dve", xm_ready, d * NWIN + NWIN)
                nc.vector.tensor_scalar(xms[:, :], xm[:, :], 1.0 / PX, None, ALU.mult).then_inc(xms_ready, 1)
                hold(dve, "dve", win_ready, d + 1)
                for m in range(2):
                    bank = 2 + 2 * m
                    nc.vector.tensor_scalar(qw[:, m, :], ps[0:C, bank, 0:WINDOWS], bqk[0:C, 0:1], None, ALU.add)\
                        .then_inc(win_sb, 1)
                    nc.vector.tensor_scalar(kw[:, m, :], ps[0:C, bank, C:C + WINDOWS], bk0[:, 0:1], None,
                                            ALU.add).then_inc(win_sb, 1)
                hold(dve, "dve", logits_ready, d + 1)
                nc.vector.tensor_copy(lg[:], ps[0:WINDOWS, 3, 0:128].rearrange("a (m b) -> a m b", m=2)[:, :, 0:WINDOWS])\
                    .then_inc(lg_sb, 1)
                hold(dve, "dve", lg_sb, d + 1)
                for m in range(2):
                    nc.vector.max(top[:, m, :], lg[:, m, :]).then_inc(top_ready, 1)
                hold(dve, "dve", top_ready, d * 2 + 2)
                for m in range(2):
                    nc.vector.max_index(idx[:, m, :], top[:, m, :], lg[:, m, :]).then_inc(idx_ready, 1)

                g0 = unit_of(d, 0, 0)
                for w in range(NWIN):
                    row_max(0, w, g0)
                split_max(0, g0)
                copy_max(0, d * MISC_DUO)

                def tap(i, k):
                    done = (d * NWIN + i) * 9
                    a, b = k // 3, k % 3
                    src = Vimg[:, bass.ds(i * WS + a, WS), b:b + SIDE]
                    out = Lp[:, :].rearrange("c (y x) -> c y x", y=WS)
                    if k == 0:
                        nc.vector.tensor_scalar(out, src, taps[:, 0:1], None, ALU.mult).then_inc(tap_done, 1)
                    else:
                        hold(dve, "dve", tap_done, done + k)
                        nc.vector.scalar_tensor_tensor(out=out, in0=src, scalar=taps[:, k:k + 1], in1=out,
                                                       op0=ALU.mult, op1=ALU.add).then_inc(tap_done, 1)

                def unit(m, i, nxt, nm, last):
                    g = unit_of(d, i, m)
                    wa = 0
                    for w in range(NWIN):
                        if nxt:
                            for _ in range(A_AT[w]):
                                row_max(nm, wa, g + 1)
                                wa += 1
                        k = m * 5 + w
                        if w < 5 and k < 9:
                            tap(i, k)
                    if nxt:
                        split_max(nm, g + 1)
                    normalise(m, 0, g * 2, misc_no(d, i, m, "sum0", last))
                    if nxt:
                        copy_max(nm, misc_no(d, i, m, "max", last))
                    normalise(m, 1, g * 2 + 1, misc_no(d, i, m, "sum1", last))

                def rows(i, last):
                    unit(0, i, True, 1, last)
                    unit(1, i, not last, 0, last)
                    hold(dve, "dve", misc_ready, misc_no(d, i, 1, "out", last) + 1)
                    nc.vector.scalar_tensor_tensor(
                        out=X[:, bass.ds(i * ROW, ROW)], in0=ps[:, MISC, 0:ROW], scalar=wob[:, 0:1],
                        in1=X[:, bass.ds(i * ROW, ROW)], op0=ALU.add, op1=ALU.add).then_inc(misc_free, 1)

                with dve.Fori(0, LAST) as i:
                    rows(i, False)
                rows(LAST, True)
                with dve.Fori(0, NWIN) as i:
                    hold(dve, "dve", u_stored, d * (16 * NWIN) + i * 16 + 16)
                    norm(i, d * UNITS + i + NWIN)

        @block.tensor
        def _(pe):
            mm = nc.tensor.matmul
            pe.wait_ge(w_loaded, 16 * N_W)
            pe.wait_ge(woh_loaded, 16 * 4)
            pe.wait_ge(init_done, 5)

            def mean_var(i, tt):
                mm(ps[:, 0, 0:ROW], ones64[:, :], X[:, bass.ds(i * ROW, ROW)], start=True, stop=True)\
                    .then_inc(mean_ready, 1)
                hold(pe, "pe", sq_ready, tt + 1)
                mm(ps[:, 1, 0:ROW], ones64[:, :], Sq[:, :], start=True, stop=True).then_inc(var_ready, 1)

            def scores(m, w, g):
                hold(pe, "pe", k_gathered, (g * NWIN + w) * TOPK + TOPK)
                for half in range(2):
                    hold(pe, "pe", max_done, g * 14 + (2 * w + half + 1))
                    for p in (2 * half, 2 * half + 1):
                        last = mm(ps[:, half, (p % 2) * KEYS:(p % 2) * KEYS + KEYS], Qbd[m][0:QROWS, p, w, :, :].rearrange("r h x -> r (h x)"),
                                  Ksel[m][0:QROWS, w, p, :, :].rearrange("r k x -> r (k x)"), start=True, stop=True)
                    last.then_inc(s_ready, 1)

            def transpose_max(m, g, no):
                hold(pe, "pe", m_split, g * 4 + 4)
                hold(pe, "pe", misc_free, no + 1)
                nc.tensor.transpose(ps[:, MISC, :].bitcast(BF16)[0:3 * HP * NWIN, 0:128],
                                    Mb[m][:].rearrange("q k n -> q (k n)"), identb[:, :]).then_inc(misc_ready, 1)

            def scores_t(m, w, g):
                n = g * NWIN + w
                k = (m * NWIN + w) % 2
                if w == 0:
                    hold(pe, "pe", m_loaded, g * 96 + 96)
                hold(pe, "pe", exp_done, n + 1)
                for c in range(2):
                    for p in range(HP):
                        last = mm(ps[:, ST0 + 2 * k + c, p * 128:p * 128 + 128],
                                  Ksel[m][:, w, p, 2 * c:2 * c + 2, :].rearrange("r k x -> r (k x)"), Qbd[m][:, p, w, :, :].rearrange("r h x -> r (h x)"),
                                  start=True, stop=True)
                last.then_inc(st_ready, 1)

            def weighted(m, w, g):
                n = g * NWIN + w
                k = (m * NWIN + w) % 2
                if w == 0:
                    hold(pe, "pe", v_gathered, g * 28 + 28)
                if w in (0, 4):
                    hold(pe, "pe", o_copied, g * 2 + (w // 4 + 1))
                hold(pe, "pe", exp_done, n + 3)
                col = (w % 4) * 128
                for a in range(2):
                    for c in range(2):
                        for j in range(4):
                            h = 4 * a + j
                            last = mm(ps[32 * j:32 * j + HD + 1, OB, col + 64 * a:col + 64 * a + 64],
                                      Vsel[m][:, w, c, h, :], Pr[k][:, c, h // 2, h % 2, :],
                                      start=(c == 0), stop=(c == 1))
                last.then_inc(pv_done, 1)

            def sums(sub, g, no):
                hold(pe, "pe", o_copied, g * 2 + (sub + 2))
                hold(pe, "pe", misc_free, no + 1)
                nw = 4 - sub
                mm(ps[:, MISC, 0:nw * 128], pick[:, :], Osb[sub][:, 0:nw].rearrange("c w a q -> c (w a q)"),
                   start=True, stop=True).then_inc(misc_ready, 1)

            with pe.Fori(0, duos) as d:
                hold(pe, "pe", x_loaded, d * 16 + 16)
                with pe.Fori(0, NWIN) as i:
                    t = d * NWIN + i
                    mean_var(i, d * UNITS + i)
                    hold(pe, "pe", xn_ready, d * UNITS + i + 1)
                    for m in range(2):
                        half = slice(C * m, C * m + C)
                        last = mm(ps[half, 4, 0:ROW], wv[half, :], Xn[half, :], start=True, stop=True)
                    last.then_inc(v_ready, 1)
                    for m in range(2):
                        half = slice(C * m, C * m + C)
                        mm(ps[:, 2 + m, 0:ROW], wqk[half, :], Xn[half, :], start=True, stop=True).then_inc(qk_ready, 1)
                    hold(pe, "pe", vt_sb, t * 2 + 2)
                    for m in range(2):
                        half = slice(C * m, C * m + C)
                        for w in range(NWIN):
                            twice = Vt[half, w].rearrange("c k x -> c (k x)")
                            last = nc.tensor.transpose(ps[:, 5 + 2 * m, w * C:w * C + C], twice, ident[half, half])
                        last.then_inc(vT_ready, 1)
                hold(pe, "pe", xms_ready, d + 1)
                for m in range(2):
                    half = slice(C * m, C * m + C)
                    mm(ps[0:C, 2 + 2 * m, 0:WINDOWS], wqk[half, 0:C], xms[half, :], start=True, stop=True)
                    last = mm(ps[0:C, 2 + 2 * m, C:C + WINDOWS], wqk[half, C:2 * C], xms[half, :],
                              start=True, stop=True)
                last.then_inc(win_ready, 1)
                hold(pe, "pe", win_sb, d * 4 + 4)
                for m in range(2):
                    last = mm(ps[0:WINDOWS, 3, C * m:C * m + WINDOWS], qw[:, m, :], kw[:, m, :], start=True, stop=True)
                last.then_inc(logits_ready, 1)

                g0 = unit_of(d, 0, 0)
                hold(pe, "pe", vpx_done, d * UNITS + UNITS)
                hold(pe, "pe", lg_sb, d + 1)
                hold(pe, "pe", q_loaded, g0 * 192 + 192)
                for w in range(NWIN):
                    scores(0, w, g0)
                transpose_max(0, g0, d * MISC_DUO)

                def unit(m, i, nxt, nm, last):
                    g = unit_of(d, i, m)
                    wa = 0
                    for w in range(NWIN):
                        scores_t(m, w, g)
                        if nxt:
                            if w == 0:
                                hold(pe, "pe", q_loaded, g * 192 + 384)
                            for _ in range(A_AT[w]):
                                scores(nm, wa, g + 1)
                                wa += 1
                        if w > 0:
                            weighted(m, w - 1, g)
                    sums(0, g, misc_no(d, i, m, "sum0", last))
                    if nxt:
                        transpose_max(nm, g + 1, misc_no(d, i, m, "max", last))
                    weighted(m, LAST, g)
                    sums(1, g, misc_no(d, i, m, "sum1", last))

                def rows(i, last):
                    unit(0, i, True, 1, last)
                    unit(1, i, not last, 0, last)
                    no = misc_no(d, i, 1, "out", last)
                    hold(pe, "pe", misc_free, no + 1)
                    hold(pe, "pe", on_ready, (d * NWIN + i) * 4 + 6)
                    hold(pe, "pe", tap_done, (d * NWIN + i) * 9 + 9)
                    for m in range(2):
                        half = slice(C * m, C * m + C)
                        out = ps[half, MISC, 0:ROW]
                        for a in range(2):
                            mm(out, woh[:, a, :], On[m][:, :, a, :].rearrange("c w (y x) -> c y w x", y=WS),
                               start=(a == 0), stop=False)
                        last_mm = mm(out, wo[half, :], Lp[half, :], start=False, stop=True)
                    last_mm.then_inc(misc_ready, 1)

                with pe.Fori(0, LAST) as i:
                    rows(i, False)
                rows(LAST, True)
                hold(pe, "pe", misc_free, d * MISC_DUO + (MISC_DUO + 1))
                with pe.Fori(0, NWIN) as i:
                    mean_var(i, d * UNITS + i + NWIN)


def mixer(nc, u_dram, x2_dram, sigma, phi, m_u, m_plus, m_minus, log_weights, gumbel,
          dft, fwd, inv, idft, inmask, outmask, out_dram):
    n_img = u_dram.shape[0] // C
    COLS = n_img * C
    RA = 2 * AL
    s1_dram = nc.dram_tensor("s1_dram", (2, AL, NB, COLS), F32).ap()
    sp_dram = nc.dram_tensor("sp_dram", (2, AL, NB, KAP), F32).ap()
    z_dram = nc.dram_tensor("z_dram", (AL, n_img, 4, 16 * 2 * C), F32).ap()
    y1_dram = nc.dram_tensor("y1_dram", (2, AL, NB, COLS), F32).ap()

    with ExitStack() as outer:
        def sem(name):
            return outer.enter_context(nc.semaphore(name))

        gate = {e: sem(f"mgate_{e}") for e in ("pe", "act", "dve", "pool", "sp")}

        def hold(eng, name, s, value):
            eng.wait_ge(s, value)
            eng.sem_inc(gate[name], 1)

        def tensor(ctx, name, shape, dt=F32):
            return ctx.enter_context(nc.sbuf_tensor(name, shape, dt))

        ps = outer.enter_context(nc.psum_tensor("mps", [128, 8, 512], F32))
        E4 = tensor(outer, "E4", [RA, BRANCHES, NA])
        filters = outer.enter_context(ExitStack())
        Gs = tensor(filters, "Gs", [128, 2, 2, NB, C])
        Mbd = tensor(filters, "Mbd", [128, 2, C, C])

        with ExitStack() as ctx:
            D1 = tensor(ctx, "D1", [NA, RA])
            D4 = tensor(ctx, "D4", [NA, BRANCHES, RA])
            Ei = tensor(ctx, "Ei", [RA, NA])
            z8 = tensor(ctx, "z8", [128, 8])
            gum = tensor(ctx, "gum", [128, BRANCHES])
            top = tensor(ctx, "mtop", [128, 8])
            idx = tensor(ctx, "midx", [128, 8], U32)
            idf = tensor(ctx, "idf", [128, 1])
            ex = tensor(ctx, "ex", [128, BRANCHES])
            tot = tensor(ctx, "tot", [128, 1])
            rtot = tensor(ctx, "rtot", [128, 1])
            step = tensor(ctx, "step", [128, BRANCHES])
            one = tensor(ctx, "one", [128, BRANCHES])
            wgt = tensor(ctx, "wgt", [128, BRANCHES])
            dif = tensor(ctx, "dif", [128, BRANCHES])
            inm = tensor(ctx, "inm", [NA, BRANCHES, 4])
            inms = tensor(ctx, "inms", [NA, 4])
            outm = tensor(ctx, "outm", [RA, BRANCHES, 4 * NA])
            outs = tensor(ctx, "outs", [RA, 4 * NA])
            sig = tensor(ctx, "sig", [128, KPHI])
            sq1 = tensor(ctx, "sq1", [128, KPHI])
            sk = tensor(ctx, "sk", [128, KPHI])
            pht = tensor(ctx, "pht", [NA, NB, KPHI])
            U = [tensor(ctx, f"U{k}", [NA, C, NB]) for k in range(2)]
            S1 = [tensor(ctx, f"S1{k}", [RA, NB, 2, C]) for k in range(2)]

            fil = S1[0][0:NA].rearrange("a c b d -> a (c b d)")[:, 0:KAP * NB].rearrange("a (k c) -> a k c", k=KAP)
            Sp = S1[1][:].rearrange("r c b d -> r (c b d)")[:, 0:NB * KAP].rearrange("r (c k) -> r c k", k=KAP)

            ws_loaded = sem("ws_loaded")
            m_loaded = sem("mm_loaded")
            v_step = sem("v_step")
            sk_step = sem("sk_step")
            exp_ready = sem("exp_ready")
            fil_step = sem("fil_step")
            phi_mm = sem("phi_mm")
            phi_sb = sem("phi_sb")
            phi_stored = sem("phi_stored")
            mats_ready = sem("mats_ready")
            u_in = [sem(f"u_in{j}") for j in range(2)]
            s1_mm = sem("s1_mm")
            s1_act = sem("s1_act")
            s1_dve = sem("s1_dve")
            s1_stored = [sem(f"s1_stored{k}") for k in range(2)]
            cleared = sem("cleared")

            block = ctx.enter_context(nc.Block())
            N_WS = 8

            @block.sync
            def _(sp):
                sp.dma_start(z8[:, 0:BRANCHES], log_weights.partition_broadcast(128)).then_inc(ws_loaded, 16)
                sp.dma_start(gum[:, :], gumbel.partition_broadcast(128)).then_inc(ws_loaded, 16)
                sp.dma_start(sig[:, :], sigma.partition_broadcast(128)).then_inc(ws_loaded, 16)
                sp.dma_start(pht[0:32], phi.rearrange("(a c) k -> a c k", c=NB)).then_inc(ws_loaded, 16)
                sp.dma_start(D1[:, :], dft).then_inc(ws_loaded, 16)
                sp.dma_start(Ei[:, :], idft).then_inc(ws_loaded, 16)
                sp.dma_start(inm[:, :, :], inmask).then_inc(ws_loaded, 16)
                sp.dma_start(outm[:].rearrange("r i x -> r (i x)"), outmask.partition_broadcast(RA)).then_inc(ws_loaded, 16)
                raw = Gs[:].rearrange("p a r b e -> p (a r) (b e)")
                for r in (0, C):
                    sp.dma_start(raw[r:r + KPHI], m_plus.rearrange("i k d e -> k i (d e)")).then_inc(m_loaded, 16)
                    sp.dma_start(raw[r + KPHI:r + 2 * KPHI], m_minus.rearrange("i k d e -> k i (d e)")).then_inc(m_loaded, 16)
                    sp.dma_start(raw[r + 2 * KPHI:r + KAP], m_u.rearrange("i k d e -> k i (d e)")).then_inc(m_loaded, 16)
                sp.wait_ge(cleared, 2)

                def load(j, n):
                    hold(sp, "sp", s1_mm, n * 8 + 8)
                    sp.dma_start(U[j][:, :, :], u_dram[bass.ds(n * C, C), :].rearrange("d (a c) -> a d c", c=NB))\
                        .then_inc(u_in[j], 16)

                def store(k, p):
                    hold(sp, "sp", s1_act, p * 8 + 12)
                    hold(sp, "sp", s1_dve, p * 8 + 12)
                    sp.dma_start(s1_dram.rearrange("r a c x -> (r a) c x")[:, :, bass.ds(p * 2 * C, 2 * C)],
                                 S1[k][:].rearrange("r c b d -> r c (b d)")).then_inc(s1_stored[k], 16)

                load(0, 0)
                load(1, 1)
                sp.wait_ge(phi_sb, 5)
                sp.dma_start(sp_dram.rearrange("r a c k -> (r a) (c k)"), Sp.rearrange("r c k -> r (c k)"))\
                    .then_inc(phi_stored, 16)
                with sp.Fori(0, n_img // 4 - 1) as q:
                    for k in range(2):
                        load(0, q * 4 + (2 * k + 2))
                        load(1, q * 4 + (2 * k + 3))
                        store(k, q * 2 + k)
                load(0, n_img - 2)
                load(1, n_img - 1)
                store(0, n_img // 2 - 2)
                store(1, n_img // 2 - 1)
                for k in range(2):
                    sp.wait_ge(s1_stored[k], n_img // 4 * 16 + 16)
                sp.wait_ge(phi_stored, 16)

            @block.gpsimd
            def _(pool):
                nc.gpsimd.memset(Mbd[:], 0.0).then_inc(cleared, 1)
                nc.gpsimd.memset(fil, 0.0).then_inc(cleared, 1)

            @block.scalar
            def _(act):
                act.wait_ge(ws_loaded, 16 * N_WS)
                nc.scalar.activation(sq1[:, :], sig[:, :], ACT.Sqrt).then_inc(sk_step, 1)
                act.wait_ge(sk_step, 1)
                nc.scalar.activation(sk[:, :], sq1[:, :], ACT.Sqrt).then_inc(sk_step, 1)
                act.wait_ge(v_step, 3)
                nc.scalar.activation(ex[:, :], z8[:, 4:8], ACT.Exp).then_inc(exp_ready, 1)
                for n in range(5):
                    k0, nk = 8 * n, min(8, KAP - 8 * n)
                    act.wait_ge(phi_mm, n + 1)
                    nc.scalar.activation(Sp[:, :, k0:k0 + nk].rearrange("r c k -> r k c"),
                                         ps[0:RA, n, 0:nk * NB].rearrange("r (k c) -> r k c", k=nk),
                                         ACT.Copy).then_inc(phi_sb, 1)

                def evacuate(k, j, q):
                    n = q * 4 + (2 * k + j)
                    for m in range(0, 8, 2):
                        cls, d0, nd = CUTS[m]
                        c0, w = CLASSES[cls]
                        hold(act, "act", s1_mm, n * 8 + (m + 17))
                        if m == 0:
                            hold(act, "act", s1_stored[k], q * 16 + 16)
                        nc.scalar.activation(S1[k][:, c0:c0 + w, j, d0:d0 + nd].rearrange("r c d -> r d c"),
                                             ps[0:RA, m, :].rearrange("r (d c) -> r d c", c=w),
                                             ACT.Copy).then_inc(s1_act, 1)

                act.wait_ge(phi_stored, 16)
                with act.Fori(0, n_img // 4) as q:
                    for k in range(2):
                        for j in range(2):
                            evacuate(k, j, q)

            @block.vector
            def _(dve):
                nc.vector.memset(dif[:, :], 0.0).then_inc(s1_mm, 16)
                nc.vector.memset(top[:, :], 0.0).then_inc(s1_act, 4)
                nc.vector.memset(ex[:, :], 0.0).then_inc(s1_dve, 4)
                nc.vector.memset(idf[:, :], 0.0).then_inc(s1_stored[0], 16)
                nc.vector.memset(rtot[:, :], 0.0).then_inc(s1_stored[1], 16)
                for i in range(BRANCHES):
                    nc.vector.memset(step[:, i:i + 1], float(i))
                dve.wait_ge(ws_loaded, 16 * N_WS)
                count = 0

                def step_done(ins):
                    nonlocal count
                    ins.then_inc(v_step, 1)
                    count += 1
                    dve.wait_ge(v_step, count)

                step_done(nc.vector.tensor_tensor(gum[:, :], gum[:, :], z8[:, 0:4], ALU.add))
                step_done(nc.vector.tensor_reduce(tot[:, :], gum[:, :], AX.X, ALU.max))
                step_done(nc.vector.tensor_scalar(z8[:, 4:8], gum[:, :], tot[:, 0:1], None, ALU.subtract))
                dve.wait_ge(exp_ready, 1)
                step_done(nc.vector.tensor_reduce(tot[:, :], ex[:, :], AX.X, ALU.add))
                step_done(nc.vector.reciprocal(rtot[:, :], tot[:, :]))
                step_done(nc.vector.tensor_scalar(z8[:, 0:4], ex[:, :], rtot[:, 0:1], None, ALU.mult))
                step_done(nc.vector.memset(z8[:, 4:8], -1.0))
                step_done(nc.vector.max(top[:, :], z8[:, :]))
                step_done(nc.vector.max_index(idx[:, :], top[:, :], z8[:, :]))
                step_done(nc.vector.tensor_copy(idf[:, :], idx[:, 0:1]))
                step_done(nc.vector.tensor_scalar(one[:, :], step[:, :], idf[:, 0:1], None, ALU.is_equal))
                step_done(nc.vector.tensor_tensor(dif[:, :], one[:, :], z8[:, 0:4], ALU.subtract))
                step_done(nc.vector.tensor_tensor(wgt[:, :], dif[:, :], z8[:, 0:4], ALU.add))
                dve.wait_ge(cleared, 2)
                dve.wait_ge(sk_step, 2)
                for k in range(KPHI):
                    last = nc.vector.tensor_scalar(fil[0:32, k, :], pht[0:32, :, k], sk[0:32, k:k + 1], None, ALU.mult)
                step_done(last)
                even = fil[0:32].rearrange("a k (c s) -> a k c s", s=2)
                nc.vector.tensor_scalar(even[:, KPHI:2 * KPHI, :, 0], even[:, 0:KPHI, :, 0], 1.0, None, ALU.mult)
                nc.vector.tensor_scalar(even[:, KPHI:2 * KPHI, :, 1], even[:, 0:KPHI, :, 1], -1.0, None, ALU.mult)
                for i in range(KAR):
                    last = nc.vector.memset(fil[0:1, 2 * KPHI + i, i:i + 1], 1.0)
                last.then_inc(fil_step, 1)
                for src, dst in ((inm, inms), (outm, outs)):
                    p = dst.shape[0]
                    step_done(nc.vector.tensor_scalar(dst[:, :], src[:, 0, :], one[0:p, 0:1], None, ALU.mult))
                    for i in range(1, BRANCHES):
                        step_done(nc.vector.scalar_tensor_tensor(out=dst[:, :], in0=src[:, i, :], scalar=one[0:p, i:i + 1],
                                                                 in1=dst[:, :], op0=ALU.mult, op1=ALU.add))
                for cls in range(4):
                    nc.vector.tensor_scalar(D4[:, cls, :], D1[:, :], inms[:, cls:cls + 1], None, ALU.mult)
                    last = nc.vector.tensor_tensor(E4[:, cls, :], Ei[:, :], outs[:, cls * NA:cls * NA + NA], ALU.mult)
                last.then_inc(mats_ready, 1)
                raw = Gs[:].rearrange("p a r b e -> p (a r) (b e)")
                dve.wait_ge(m_loaded, 16 * 6)
                for h in range(2):
                    rows = slice(C * h, C * h + KAP)
                    dst = Mbd[rows, h].rearrange("p d e -> p (d e)")
                    step_done(nc.vector.tensor_scalar(dst, raw[rows, 0, :], wgt[rows, 0:1], None, ALU.mult))
                    for i in range(1, BRANCHES):
                        step_done(nc.vector.scalar_tensor_tensor(out=dst, in0=raw[rows, i, :], scalar=wgt[rows, i:i + 1],
                                                                 in1=dst, op0=ALU.mult, op1=ALU.add))

                def evacuate(k, j, q):
                    n = q * 4 + (2 * k + j)
                    for m in range(1, 8, 2):
                        cls, d0, nd = CUTS[m]
                        c0, w = CLASSES[cls]
                        hold(dve, "dve", s1_mm, n * 8 + (m + 17))
                        if m == 1:
                            hold(dve, "dve", s1_stored[k], q * 16 + 16)
                        nc.vector.tensor_copy(S1[k][:, c0:c0 + w, j, d0:d0 + nd].rearrange("r c d -> r d c"),
                                              ps[0:RA, m, :].rearrange("r (d c) -> r d c", c=w)).then_inc(s1_dve, 1)

                dve.wait_ge(phi_stored, 16)
                with dve.Fori(0, n_img // 4) as q:
                    for k in range(2):
                        for j in range(2):
                            evacuate(k, j, q)

            @block.tensor
            def _(pe):
                mm = nc.tensor.matmul
                pe.wait_ge(fil_step, 1)
                for n in range(5):
                    k0, nk = 8 * n, min(8, KAP - 8 * n)
                    mm(ps[0:RA, n, 0:nk * NB], D1[:, :], fil[:, k0:k0 + nk, :].rearrange("a k c -> a (k c)"),
                       start=True, stop=True).then_inc(phi_mm, 1)
                pe.wait_ge(phi_sb, 5)
                pe.wait_ge(mats_ready, 1)
                with pe.Fori(0, n_img // 2) as q:
                    for j in range(2):
                        n = q * 2 + j
                        hold(pe, "pe", u_in[j], q * 16 + 16)
                        for m, (cls, d0, nd) in enumerate(CUTS):
                            c0, w = CLASSES[cls]
                            hold(pe, "pe", s1_dve if m % 2 else s1_act, n * 4 + (m // 2 + 1))
                            mm(ps[0:RA, m, :], D4[:, cls, :], U[j][:, d0:d0 + nd, c0:c0 + w],
                               start=True, stop=True).then_inc(s1_mm, 1)

        with ExitStack() as ctx:
            Fw = tensor(ctx, "Fw", [128, 2, 3 * NB])
            Iv = tensor(ctx, "Iv", [128, 2, 2 * NB])
            Sf = tensor(ctx, "Sf", [128, 2, KAP])
            Sin = tensor(ctx, "Sin", [128, 2, COLS])
            Uh = [tensor(ctx, f"Uh{k}", [128, n_img, NB]) for k in range(2)]
            Vh = tensor(ctx, "Vh", [128, 2, 2 * NB])
            Zs = [tensor(ctx, f"Zs{k}", [128, 4, 4 * 2 * C]) for k in range(2)]
            Zr = [tensor(ctx, f"Zr{k}", [128, n_img, C]) for k in range(2)]
            Ys = [tensor(ctx, f"Ys{k}", [128, COLS]) for k in range(2)]
            nil = tensor(ctx, "nil", [1, 16])

            in_loaded = sem("in_loaded")
            iv_loaded = sem("iv_loaded")
            v_mm = sem("v_mm")
            v_sb = sem("v_sb")
            g_mm = sem("g_mm")
            g_act = sem("g_act")
            g_dve = sem("g_dve")
            uh_mm = sem("uh_mm")
            uh_act = sem("uh_act")
            uh_dve = sem("uh_dve")
            z_mm = sem("z_mm")
            z_act = sem("z_act")
            z_dve = sem("z_dve")
            z_stored = [sem(f"z_stored{k}") for k in range(2)]
            z_loaded = [sem(f"z_loaded{k}") for k in range(2)]
            i_mm = sem("i_mm")
            i_act = sem("i_act")
            i_dve = sem("i_dve")
            y_stored = [sem(f"y_stored{k}") for k in range(2)]
            b_init = sem("b_init")

            block = ctx.enter_context(nc.Block())
            Z_BANK, I_BANK = 4, 6

            @block.sync
            def _(sp):
                def load_in(p):
                    for r in range(2):
                        half = slice(NB * r, NB * r + NB)
                        sp.dma_start(Sin[half], s1_dram[r].rearrange("a c x -> c a x")[:, bass.ds(p * 2, 2), :])\
                            .then_inc(in_loaded, 16)
                        sp.dma_start(Sf[half], sp_dram[r].rearrange("a c k -> c a k")[:, bass.ds(p * 2, 2), :])\
                            .then_inc(in_loaded, 16)
                    sp.dma_start(Fw[:], fwd[:, bass.ds(p * 2, 2), :]).then_inc(in_loaded, 16)

                def load_inverse(p):
                    sp.dma_start(Iv[:], inv[:, bass.ds(p * 2, 2), :]).then_inc(iv_loaded, 16)

                def store_inverse(p):
                    for k in range(2):
                        hold(sp, "sp", i_act, p * 2 + (k + 2))
                        hold(sp, "sp", i_dve, p * 2 + (k + 2))
                        for r in range(2):
                            half = slice(NB * r, NB * r + NB)
                            sp.dma_start(y1_dram[r].rearrange("a c x -> c a x")[:, bass.ds(p * 2 + k, 1), :]
                                         .rearrange("c a x -> c (a x)"), Ys[k][half, :]).then_inc(y_stored[k], 16)

                def turn(p):
                    for k in range(2):
                        hold(sp, "sp", z_act, p * 4 + (2 * k + 3))
                        hold(sp, "sp", z_dve, p * 4 + (2 * k + 3))
                        for q in range(4):
                            sp.dma_start(z_dram.rearrange("a b q x -> q a b x")[q][bass.ds(p * 2 + k, 1)]
                                         .rearrange("a b x -> (a b) x"),
                                         Zs[k][32 * q:32 * q + n_img].rearrange("b j x -> b (j x)")).then_inc(z_stored[k], 16)
                    for k in range(2):
                        hold(sp, "sp", z_stored[k], p * 64 + 80)
                        hold(sp, "sp", i_mm, p * 4 + 4)
                        sp.dma_start(Zr[k][:, :, :], z_dram[bass.ds(p * 2 + k, 1)]
                                     .rearrange("a b q (j e) -> (a q j) b e", e=C)).then_inc(z_loaded[k], 16)

                sp.wait_ge(b_init, 1)
                load_in(0)
                load_inverse(0)
                sp.wait_ge(uh_mm, 4)
                load_in(1)
                turn(0)

                def step(p, last):
                    store_inverse(p - 1)
                    load_inverse(p)
                    if not last:
                        hold(sp, "sp", uh_mm, p * 4 + 4)
                        load_in(p + 1)
                    turn(p)

                with sp.Fori(1, PAIRS - 1) as p:
                    step(p, False)
                step(PAIRS - 1, True)
                store_inverse(PAIRS - 1)
                for k in range(2):
                    sp.wait_ge(y_stored[k], PAIRS * 32 + 16)

            def copy_g(eng, name, copy, s, odd, p):
                hold(eng, name, z_mm, p * 8 + 1)
                for n in range(odd, 32, 2):
                    hold(eng, name, g_mm, p * 32 + (n + 1))
                    copy(Gs[:, :, :, :, 2 * n:2 * n + 2].rearrange("p a r b e -> p (a r) b e"),
                         ps[:, n % 4, :].rearrange("p (e x b) -> p x b e", e=2, b=NB)).then_inc(s, 1)

            def copy_uh(eng, name, copy, s, odd, p):
                for k in range(2):
                    hold(eng, name, uh_mm, p * 4 + (2 * k + odd + 1))
                    copy(Uh[k][:, 8 * odd:8 * odd + 8].rearrange("p b x -> p (b x)"), ps[:, 2 * k + odd, :]).then_inc(s, 1)

            def copy_z(eng, name, copy, s, odd, p):
                for t in range(odd, 8, 2):
                    if t < 4:
                        hold(eng, name, z_stored[0], p * 64 + 16)
                    else:
                        hold(eng, name, z_stored[1], p * 64 + 16)
                    hold(eng, name, z_mm, p * 8 + (t + 2))
                    copy(Zs[t // 4][:, t % 4, :], ps[:, Z_BANK + odd, :]).then_inc(s, 1)

            def copy_inverse(eng, name, copy, s, odd, p):
                for k in range(2):
                    hold(eng, name, i_mm, p * 4 + (2 * k + odd + 5))
                    hold(eng, name, y_stored[k], p * 32 + 16)
                    copy(Ys[k][:, 512 * odd:512 * odd + 512], ps[:, I_BANK + odd, :]).then_inc(s, 1)

            @block.scalar
            def _(act):
                def copy(out, in_):
                    return nc.scalar.activation(out, in_, ACT.Copy)

                act.wait_ge(b_init, 1)

                def step(p, first):
                    hold(act, "act", v_mm, p + 1)
                    copy(Vh[0:KAP].rearrange("k a x -> k (a x)"), ps[0:KAP, I_BANK, 0:256]).then_inc(v_sb, 1)
                    copy_g(act, "act", copy, g_act, 0, p)
                    if not first:
                        copy_inverse(act, "act", copy, i_act, 0, p - 1)
                    copy_uh(act, "act", copy, uh_act, 0, p)
                    copy_z(act, "act", copy, z_act, 0, p)

                step(0, True)
                with act.Fori(1, PAIRS) as p:
                    step(p, False)
                copy_inverse(act, "act", copy, i_act, 0, PAIRS - 1)

            @block.vector
            def _(dve):
                copy = nc.vector.tensor_copy
                nc.vector.memset(ps[:, Z_BANK:Z_BANK + 2, :], 0.0)
                nc.vector.memset(Vh[:], 0.0)
                for n, (s, credit) in enumerate([(g_act, 2), (g_dve, 2), (z_mm, 1), (z_act, 1), (z_dve, 1), (i_mm, 4),
                                                 (i_act, 1), (i_dve, 1), (z_stored[0], 16), (z_stored[1], 16),
                                                 (y_stored[0], 16), (y_stored[1], 16), (b_init, 1)]):
                    nc.vector.memset(nil[:, n:n + 1], 0.0).then_inc(s, credit)

                def step(p, first):
                    hold(dve, "dve", v_mm, p + 1)
                    copy(Vh[C:C + KAP].rearrange("k a x -> k (a x)"), ps[C:C + KAP, I_BANK, 0:256]).then_inc(v_sb, 1)
                    copy_g(dve, "dve", copy, g_dve, 1, p)
                    if not first:
                        copy_inverse(dve, "dve", copy, i_dve, 1, p - 1)
                    copy_uh(dve, "dve", copy, uh_dve, 1, p)
                    copy_z(dve, "dve", copy, z_dve, 1, p)

                dve.wait_ge(b_init, 1)
                step(0, True)
                with dve.Fori(1, PAIRS) as p:
                    step(p, False)
                copy_inverse(dve, "dve", copy, i_dve, 1, PAIRS - 1)

            @block.tensor
            def _(pe):
                mm = nc.tensor.matmul
                pe.wait_ge(b_init, 1)

                def inverse(p):
                    hold(pe, "pe", iv_loaded, p * 16 + 16)
                    for k in range(2):
                        hold(pe, "pe", z_loaded[k], p * 16 + 16)
                        for h in range(2):
                            hold(pe, "pe", i_dve if h else i_act, p * 2 + (k + 1))
                            mm(ps[:, I_BANK + h, :], Iv[:, k, :], Zr[k][:, 8 * h:8 * h + 8, :].rearrange("x b e -> x (b e)"),
                               start=True, stop=True).then_inc(i_mm, 1)

                def step(p, first):
                    hold(pe, "pe", in_loaded, p * 80 + 80)
                    if not first:
                        hold(pe, "pe", i_act, p * 2 - 1)
                    for k in range(2):
                        mm(ps[0:KAP, I_BANK, 128 * k:128 * k + 128], Sf[:, k, :], Fw[:, k, NB:3 * NB], start=True, stop=True)
                        last = mm(ps[C:C + KAP, I_BANK, 128 * k:128 * k + 128], Sf[:, k, :], Fw[:, k, 0:2 * NB],
                                  start=True, stop=True)
                    last.then_inc(v_mm, 1)
                    hold(pe, "pe", v_sb, p * 2 + 2)
                    for n in range(32):
                        hold(pe, "pe", g_dve if n % 2 else g_act, p * 16 + (n // 2 + 1))
                        for e in range(2):
                            last = mm(ps[:, n % 4, 256 * e:256 * e + 256],
                                      Mbd[:, :, :, 2 * n + e].rearrange("k h d -> k (h d)"),
                                      Vh[:].rearrange("k a x -> k (a x)"), start=True, stop=True)
                        last.then_inc(g_mm, 1)
                    if not first:
                        inverse(p - 1)
                    hold(pe, "pe", g_act, p * 16 + 18)
                    hold(pe, "pe", g_dve, p * 16 + 18)
                    for k in range(2):
                        for b in range(n_img):
                            bank, col = 2 * k + b // 8, (b % 8) * NB
                            mm(ps[0:C, bank, col:col + NB], Sin[:, k, b * C:b * C + C], Fw[:, k, NB:2 * NB],
                               start=True, stop=True)
                            last = mm(ps[C:2 * C, bank, col:col + NB], Sin[:, k, b * C:b * C + C], Fw[:, k, 2 * NB:3 * NB],
                                      start=True, stop=True)
                            if b % 8 == 7:
                                last.then_inc(uh_mm, 1)
                    for k in range(2):
                        hold(pe, "pe", uh_act, p * 2 + (k + 1))
                        hold(pe, "pe", uh_dve, p * 2 + (k + 1))
                        for jj in range(4):
                            t = 4 * k + jj
                            hold(pe, "pe", z_dve if t % 2 else z_act, p * 4 + (t // 2 + 1))
                            for j in range(4):
                                for q in range(4):
                                    be = 16 * q + 4 * jj + j
                                    last = mm(ps[32 * q:32 * q + n_img, Z_BANK + t % 2, 128 * j:128 * j + 128],
                                              Uh[k][:, :, be], Gs[:, k, :, be, :], start=True, stop=True)
                            last.then_inc(z_mm, 1)

                step(0, True)
                with pe.Fori(1, PAIRS) as p:
                    step(p, False)
                inverse(PAIRS - 1)

        filters.close()

        with ExitStack() as ctx:
            Y1 = [tensor(ctx, f"Y1{k}", [RA, NB, 2, C]) for k in range(2)]
            Xr = [tensor(ctx, f"Xr{k}", [NA, C, NB]) for k in range(4)]
            nil = tensor(ctx, "nil2", [1, 5])
            c_in = [sem(f"c_in{k}") for k in range(2)]
            c_mm = sem("c_mm")
            c_dve = sem("c_dve")
            c_stored = [sem(f"c_stored{k}") for k in range(2)]
            c_init = sem("c_init")
            block = ctx.enter_context(nc.Block())

            @block.sync
            def _(sp):
                sp.wait_ge(c_init, 1)

                def load(k, q):
                    p = q * 2 + k
                    hold(sp, "sp", c_mm, p * 16 + 16)
                    sp.dma_start(Y1[k][:].rearrange("r c b e -> r c (b e)"),
                                 y1_dram.rearrange("r a c x -> (r a) c x")[:, :, bass.ds(p * 2 * C, 2 * C)])\
                        .then_inc(c_in[k], 16)
                    hold(sp, "sp", c_stored[k], q * 32 + 16)
                    for j in range(2):
                        sp.dma_start(Xr[2 * k + j][:], x2_dram[bass.ds((p * 2 + j) * C, C), :]
                                     .rearrange("e (a c) -> a e c", c=NB)).then_inc(c_in[k], 16)

                def store(k, q):
                    for j in range(2):
                        n = q * 4 + (2 * k + j)
                        hold(sp, "sp", c_dve, n * 8 + 16)
                        sp.dma_start(out_dram[bass.ds(n * C, C), :].rearrange("e (a c) -> a e c", c=NB),
                                     Xr[2 * k + j][:]).then_inc(c_stored[k], 16)

                load(0, 0)
                with sp.Fori(0, n_img // 4 - 1) as q:
                    load(1, q)
                    store(0, q)
                    load(0, q + 1)
                    store(1, q)
                load(1, n_img // 4 - 1)
                store(0, n_img // 4 - 1)
                store(1, n_img // 4 - 1)
                for k in range(2):
                    sp.wait_ge(c_stored[k], n_img // 4 * 32 + 16)

            @block.vector
            def _(dve):
                for n, (s, credit) in enumerate([(c_mm, 32), (c_dve, 8), (c_stored[0], 16), (c_stored[1], 16)]):
                    nc.vector.memset(nil[:, n:n + 1], 0.0).then_inc(s, credit)
                nc.vector.memset(nil[:, 4:5], 0.0).then_inc(c_init, 1)
                with dve.Fori(0, n_img // 4) as q:
                    for k in range(2):
                        hold(dve, "dve", c_in[k], q * 48 + 48)
                        for j in range(2):
                            n = q * 4 + (2 * k + j)
                            for m, (cls, e0, ne) in enumerate(CUTS):
                                c0, w = CLASSES[cls]
                                part = Xr[2 * k + j][:, e0:e0 + ne, c0:c0 + w]
                                hold(dve, "dve", c_mm, n * 8 + (m + 33))
                                nc.vector.tensor_tensor(part, ps[0:NA, m, :].rearrange("a (e c) -> a e c", c=w), part,
                                                        ALU.add).then_inc(c_dve, 1)

            @block.tensor
            def _(pe):
                pe.wait_ge(c_init, 1)
                with pe.Fori(0, n_img // 4) as q:
                    for k in range(2):
                        hold(pe, "pe", c_in[k], q * 48 + 48)
                        for j in range(2):
                            n = q * 4 + (2 * k + j)
                            for m, (cls, e0, ne) in enumerate(CUTS):
                                c0, w = CLASSES[cls]
                                hold(pe, "pe", c_dve, n * 8 + (m + 1))
                                nc.tensor.matmul(ps[0:NA, m, :], E4[:, cls, :],
                                                 Y1[k][:, c0:c0 + w, j, e0:e0 + ne].rearrange("r c e -> r e c"),
                                                 start=True, stop=True).then_inc(c_mm, 1)


def dft_mats():
    import numpy as np
    al = np.arange(AL)
    a, c, be = np.arange(NB), np.arange(NB), np.arange(NB)
    t1 = 2 * np.pi * ((a[:NA, None] * al[None, :]) % NB) / NB
    dft = np.concatenate([np.cos(t1), -np.sin(t1)], 1)
    t2 = 2 * np.pi * ((c[:, None, None] * (al[None, :, None] + NB * be[None, None, :])) % NF) / NF
    re, im = np.cos(t2), -np.sin(t2)
    fwd = np.concatenate([np.concatenate([-im, re, im], 2), np.concatenate([-re, -im, re], 2)], 0)
    ce, se = np.cos(t2), np.sin(t2)
    inv = np.empty((NB, 2, AL, 2, NB))
    inv[:, 0, :, 0], inv[:, 1, :, 0] = ce.transpose(2, 1, 0), -se.transpose(2, 1, 0)
    inv[:, 0, :, 1], inv[:, 1, :, 1] = se.transpose(2, 1, 0), ce.transpose(2, 1, 0)
    weight = np.where((al == 0) | (al == 32), 1.0, 2.0) * (al < 33) / NF
    idft = np.concatenate([np.cos(t1) * weight, -np.sin(t1) * weight], 1).T
    cut = TOKENS // 2 ** np.arange(BRANCHES)
    first = np.array([c0 for c0, _ in CLASSES])
    inside = NB * a[:NA, None, None] + first[None, None, :] < cut[None, :, None]
    inmask = inside
    outmask = inside.transpose(1, 2, 0).reshape(-1)
    return [np.ascontiguousarray(m, np.float32) for m in (dft, fwd, inv.reshape(2 * NB, AL, 2 * NB), idft, inmask, outmask)]


def const_mats():
    import numpy as np
    mats = np.zeros((3, 128, 128), np.float32)
    for m in range(2):
        mats[0, C * m:C * m + C, C * m:C * m + C] = 1.0 / C
    mats[1] = np.eye(128, dtype=np.float32)
    for j in range(4):
        mats[2, 32 * j + HD, 32 * j:32 * j + 32] = 1.0
    return mats


_INPUTS = ["x", "L0_conv_qkv_w", "L0_conv_qkv_b", "L0_conv_lepe_w", "L0_conv_wo_w", "L0_conv_wo_b",
           "L0_ffn_sigma", "L0_ffn_phi", "L0_ffn_M_u", "L0_ffn_M_phi_plus", "L0_ffn_M_phi_minus",
           "L0_ffn_log_weights", "L0_ffn_gumbel"]


def kernel(**inputs):
    import numpy as np
    import concourse.bacc as _bacc
    from concourse import mybir as _mybir
    from concourse.bass_utils import run_bass_kernel_spmd as _run
    nc = _bacc.Bacc("TRN2", target_bir_lowering=False, num_devices=1)
    arrays = {}

    def given(name, array):
        arrays[name] = np.ascontiguousarray(array)
        return nc.dram_tensor(name, arrays[name].shape, _mybir.dt.from_np(arrays[name].dtype),
                              kind="ExternalInput").ap()

    x, qkv_w, qkv_b, lepe_w, wo_w, wo_b, *ffn = [given(f"in_{n}", inputs[n]) for n in _INPUTS]
    mats = given("att_mats", const_mats())
    dfts = [given(f"dft_mats{n}", m) for n, m in enumerate(dft_mats())]
    out = nc.dram_tensor("out0", x.shape, F32, kind="ExternalOutput").ap()
    rows = x.shape[0] * C
    x2_dram = nc.dram_tensor("x2_dram", (rows, TOKENS), F32).ap()
    u_dram = nc.dram_tensor("u_dram", (rows, TOKENS), F32).ap()
    attention(nc, x, qkv_w, qkv_b, lepe_w, wo_w, wo_b, mats, x2_dram, u_dram)
    mixer(nc, u_dram, x2_dram, *ffn, *dfts, out.rearrange("n c h w -> (n c) (h w)"))
    result = _run(nc, [arrays], core_ids=[0])
    return result.results[0]["out0"]
```

```python
from contextlib import ExitStack

import concourse.bass as bass
from concourse import mybir

F32 = mybir.dt.float32
BF16 = mybir.dt.bfloat16
I32 = mybir.dt.int32
U32 = mybir.dt.uint32
ALU = mybir.AluOpType
ACT = mybir.ActivationFunctionType
AX = mybir.AxisListType

C = 64
SIDE = 56
TOKENS = SIDE * SIDE
NWIN = 7
WINDOWS = NWIN * NWIN
WS = SIDE // NWIN
PX = WS * WS
ROW = NWIN * PX
HEADS, HD = 8, 8
HP = HEADS // 2
TOPK = 4
KEYS = TOPK * PX
PAD = SIDE + 2
TERMS = [(0, 0), (0, 1), (0, 2), (1, 0), (1, 1), (2, 0)]
TR = len(TERMS) * HD
QROWS = 2 * TR
NMAX = 3 * HP * NWIN
SCALE = float(C) ** -0.5
A_AT = [0, 2, 2, 1, 1, 1, 0]


NF = 4096
NA, NB = 49, 64
AL = 34
PAIRS = AL // 2
KPHI = 16
KAR = 3
KAP = 2 * KPHI + KAR
BRANCHES = 4
CLASSES = [(0, 8), (8, 8), (16, 16), (32, 32)]
CUTS = [(3, 0, 16), (3, 16, 16), (3, 32, 16), (3, 48, 16), (2, 0, 32), (2, 32, 32), (1, 0, 64), (0, 0, 64)]



def attention(nc, x, qkv_w, qkv_b, lepe_w, wo_w, wo_b, mats, x2_dram, u_dram):
    n_img = x.shape[0]
    duos = n_img // 2
    xv = x.rearrange("n c h w -> (n c) (h w)")
    with ExitStack() as ctx:
        def sb(name, shape, dt=F32):
            return ctx.enter_context(nc.sbuf_tensor(name, shape, dt))

        def sem(name):
            return ctx.enter_context(nc.semaphore(name))

        q_dram = nc.dram_tensor("q_dram", (2, NWIN, 2, len(TERMS), HD * HP, ROW), BF16).ap()
        k_dram = nc.dram_tensor("k_dram", (2, 3, C, TOKENS), BF16).ap()

        ones64 = sb("ones64", [128, 128])
        ident = sb("ident", [128, 128])
        identb = sb("identb", [128, 128], BF16)
        pick = sb("pick", [128, 128])
        each = sb("each", [NMAX, HP * NWIN])
        less = sb("less", [NMAX, HP * NWIN, 2 * PX], BF16)
        wqk = sb("wqk", [128, 2 * C])
        wraw = sb("wraw", [128, 2 * C])
        wv = sb("wv", [128, C])
        bqk = sb("bqk", [128, 1])
        bk0 = sb("bk0", [C, 1])
        bv = sb("bv", [128, 1])
        taps = sb("taps", [128, 9])
        wo = sb("wo", [128, C])
        woh = sb("woh", [128, 2, C])
        wob = sb("wob", [128, 1])
        X = sb("X", [128, TOKENS])
        Vimg = sb("Vimg", [128, PAD, PAD])
        Kexp = [sb(f"Kexp{m}", [QROWS, HP, TOKENS], BF16) for m in range(2)]
        Vpx = [sb(f"Vpx{m}", [128, WINDOWS, HEADS, HD + 1]) for m in range(2)]
        idxrow = sb("idxrow", [1, 2, WINDOWS * TOPK], I32)
        Rc = sb("Rc", [128, 512])
        Lp = sb("Lp", [128, ROW])
        nil = sb("nil", [1, 16])
        eps = sb("eps", [128, 2])
        Xn = [sb(f"Xn{k}", [128, ROW]) for k in range(2)]
        Qk = sb("Qk", [128, ROW])
        Res = sb("Res", [128, ROW])
        Part = [sb(f"Part{m}", [128, 3, ROW], BF16) for m in range(2)]
        Vt = sb("Vt", [128, NWIN, 2, PX])
        xm = sb("xm", [128, WINDOWS])
        xms = sb("xms", [128, WINDOWS])
        qw = sb("qw", [C, 2, WINDOWS])
        kw = sb("kw", [C, 2, WINDOWS])
        lg = sb("lg", [WINDOWS, 2, WINDOWS])
        top = sb("top", [WINDOWS, 2, 8])
        idx = sb("idx", [WINDOWS, 2, 8], U32)
        Qbd = [sb(f"Qbd{m}", [QROWS, HP, NWIN, 2, PX], BF16) for m in range(2)]
        Ksel = [sb(f"Ksel{m}", [QROWS, NWIN, HP, TOPK, PX], BF16) for m in range(2)]
        Vsel = [sb(f"Vsel{m}", [128, NWIN, 2, HEADS, HD + 1]) for m in range(2)]
        Mx = [sb(f"Mx{m}", [128, HP, NWIN]) for m in range(2)]
        Mr = sb("Mr", [128, HP * NWIN])
        Mb = [sb(f"Mb{m}", [128, 3, HP * NWIN], BF16) for m in range(2)]
        MT = [sb(f"MT{m}", [NMAX, 2, PX], BF16) for m in range(2)]
        Pr = [sb(f"Pr{k}", [128, 2, HP, 2, PX]) for k in range(2)]
        Osb = [sb(f"Osb{k}", [128, 4, 2, PX]) for k in range(2)]
        On = [sb(f"On{m}", [128, NWIN, 2, PX]) for m in range(2)]
        Cen = [On[k][:].rearrange("c w a q -> c (w a q)")[:, 0:ROW] for k in range(2)]
        Sq = [Osb[k][:].rearrange("c w a q -> c (w a q)")[:, 0:ROW] for k in range(2)]
        Std = [Pr[k][:].rearrange("q c p h x -> q (c p h x)")[:, 0:ROW] for k in range(2)]
        Rstd = [Pr[k][:].rearrange("q c p h x -> q (c p h x)")[:, 512:512 + ROW] for k in range(2)]

        ps = ctx.enter_context(nc.psum_tensor("ps", [128, 8, 512], F32))
        ST0, OB, MISC = 2, 6, 7

        gate = {e: sem(f"gate_{e}") for e in ("pe", "act", "dve", "pool", "sp")}
        w_loaded = sem("w_loaded")
        less_step = sem("less_step")
        ob_set = sem("ob_set")
        init_done = sem("init_done")
        woh_loaded = sem("woh_loaded")
        x_loaded = sem("x_loaded")
        mean_ready = sem("mean_ready")
        cen_ready = sem("cen_ready")
        sq_ready = sem("sq_ready")
        var_ready = sem("var_ready")
        std_ready = sem("std_ready")
        rstd_ready = sem("rstd_ready")
        xn_ready = sem("xn_ready")
        xm_ready = sem("xm_ready")
        xms_ready = sem("xms_ready")
        qk_ready = sem("qk_ready")
        v_ready = sem("v_ready")
        qk_sb = sem("qk_sb")
        part1 = sem("part1")
        res1 = sem("res1")
        part2 = sem("part2")
        part3 = sem("part3")
        parts_stored = sem("parts_stored")
        vt_sb = sem("vt_sb")
        vT_ready = sem("vT_ready")
        vpx_done = sem("vpx_done")
        win_ready = sem("win_ready")
        win_sb = sem("win_sb")
        logits_ready = sem("logits_ready")
        lg_sb = sem("lg_sb")
        top_ready = sem("top_ready")
        idx_ready = sem("idx_ready")
        idx_stored = sem("idx_stored")
        k_loaded = sem("k_loaded")
        q_loaded = [sem(f"q_loaded{m}") for m in range(2)]
        mt_ready = sem("mt_ready")
        mt_copied = sem("mt_copied")
        k_gathered = sem("k_gathered")
        v_gathered = sem("v_gathered")
        s_ready = sem("s_ready")
        max_done = sem("max_done")
        m_split = sem("m_split")
        st_ready = sem("st_ready")
        exp_done = sem("exp_done")
        pv_done = sem("pv_done")
        o_copied = sem("o_copied")
        misc_ready = sem("misc_ready")
        misc_free = sem("misc_free")
        on_ready = sem("on_ready")
        tap_done = sem("tap_done")
        x2_stored = sem("x2_stored")
        u_stored = [sem(f"u_stored{k}") for k in range(2)]

        block = ctx.enter_context(nc.Block())
        LAST = NWIN - 1
        N_W = 4 + 6 * HD + 12
        UNITS = 2 * NWIN
        MISC_DUO = 5 * NWIN

        def unit_of(d, i, m):
            return d * UNITS + i * 2 + m

        def misc_no(d, i, m, what):
            order = [(0, "sum0"), (0, "sum1"), (1, "sum0"), (1, "sum1"), (1, "out")]
            return d * MISC_DUO + i * 5 + order.index((m, what))

        def tiles(eng, body):
            with eng.Fori(0, NWIN // 2) as j:
                body(j * 2, 0, False)
                body(j * 2 + 1, 1, False)
            body(LAST, 0, True)

        def u_count(d, i, k):
            return d * (64 - 16 * k) + (i - k) * 8 + 16

        def hold(eng, name, s, value):
            eng.wait_ge(s, value)
            eng.sem_inc(gate[name], 1)

        @block.sync
        def _(sp):
            sp.dma_start(ones64[:, :], mats[0]).then_inc(w_loaded, 16)
            sp.dma_start(ident[:, :], mats[1]).then_inc(w_loaded, 16)
            sp.dma_start(pick[:, :], mats[2]).then_inc(w_loaded, 16)
            sp.dma_start(each[:, :], mats[3, 0:NMAX, 0:HP * NWIN]).then_inc(w_loaded, 16)
            bias = qkv_b.rearrange("(s p h d) -> s h d p", s=3, p=HP, h=2)
            for h2 in range(2):
                q = HP * HD
                for out, s in ((bqk[q * h2:q * h2 + q, :], 0), (bqk[C + q * h2:C + q * h2 + q, :], 1),
                               (bk0[q * h2:q * h2 + q, :], 1)):
                    with nc.allow_non_contiguous_dma(reason="32 words"):
                        for e in range(HD):
                            sp.dma_start(out[HP * e:HP * e + HP], bias[s, h2, e:e + 1, :].rearrange("a p -> p a"))\
                              .then_inc(w_loaded, 16)
            for m in range(2):
                half = slice(C * m, C * m + C)
                sp.dma_start(wraw[half, :], qkv_w[:, 0:2 * C]).then_inc(w_loaded, 16)
                sp.dma_start(wv[half, :], qkv_w[:, 2 * C:3 * C]).then_inc(w_loaded, 16)
                sp.dma_start(bv[half, :], qkv_b[2 * C:3 * C].rearrange("(c a) -> c a", a=1)).then_inc(w_loaded, 16)
                sp.dma_start(taps[half, :], lepe_w.rearrange("c a i j -> c (a i j)")).then_inc(w_loaded, 16)
                sp.dma_start(wo[half, :], wo_w).then_inc(w_loaded, 16)
                sp.dma_start(wob[half, :], wo_b.rearrange("(c a) -> c a", a=1)).then_inc(w_loaded, 16)
            sp.wait_ge(init_done, 5)
            wo4 = wo_w.rearrange("(g j d) e -> j d g e", g=2, j=4)
            for j in range(4):
                sp.dma_start(woh[32 * j:32 * j + HD, :, :], wo4[j]).then_inc(woh_loaded, 16)

            def load_q(m, i, g):
                hold(sp, "sp", st_ready, g * NWIN + NWIN)
                for h2 in range(2):
                    sp.dma_start(Qbd[m][TR * h2:TR * h2 + TR, :, :, h2, :].rearrange("r p w x -> r (p w) x"),
                                 q_dram[m, :, h2][bass.ds(i, 1)].rearrange("a t (d p) (w x) -> (a t d) (p w) x", p=HP, x=PX))\
                        .then_inc(q_loaded[m], 16)

            with sp.Fori(0, duos) as d:
                hold(sp, "sp", x2_stored, d * (16 * NWIN) + 16)
                sp.dma_start(X[:, :], xv[bass.ds(d * 128, 128), :]).then_inc(x_loaded, 16)
                with sp.Fori(0, NWIN) as i:
                    for m in range(2):
                        hold(sp, "sp", part3, d * UNITS + i * 2 + (m + 1))
                        for h2 in range(2):
                            rows = slice(HD * HP * h2, HD * HP * h2 + HD * HP)
                            for part, t, nt in ((0, 0, 3), (1, 3, 2), (2, 5, 1)):
                                sp.dma_start(q_dram[m, :, h2, t:t + nt][bass.ds(i, 1)].rearrange("a t c x -> (a c) t x"),
                                             Part[m][rows, part:part + 1, :].broadcast_to([HD * HP, nt, ROW]))\
                                    .then_inc(parts_stored, 16)
                        sp.dma_start(k_dram[m].rearrange("k c x -> c k x")[:, :, bass.ds(i * ROW, ROW)],
                                     Part[m][C:2 * C]).then_inc(parts_stored, 16)
                hold(sp, "sp", parts_stored, d * (112 * UNITS) + (112 * UNITS + 16))
                for m in range(2):
                    for h2 in range(2):
                        for t, (_, part) in enumerate(TERMS):
                            r = TR * h2 + HD * t
                            src = k_dram[m, part].rearrange("(h d p) x -> h d (p x)", h=2, p=HP)[h2]
                            sp.dma_start(Kexp[m][r:r + HD].rearrange("d p x -> d (p x)"), src)\
                              .then_inc(k_loaded, 16)
                hold(sp, "sp", idx_ready, d * 2 + 2)
                for m in range(2):
                    sp.dma_start(idxrow[0:1, m, :].rearrange("a (w k) -> a w k", k=TOPK),
                                 idx[:, m, 0:TOPK].bitcast(I32)).then_inc(idx_stored, 16)
                load_q(0, 0, unit_of(d, 0, 0))

                with sp.Fori(0, LAST) as i:
                    load_q(1, i, unit_of(d, i, 1))
                    load_q(0, i + 1, unit_of(d, i, 2))
                load_q(1, LAST, unit_of(d, LAST, 1))
                def store_tile(i, k, last):
                    hold(sp, "sp", xn_ready, d * UNITS + i + (NWIN + 1))
                    sp.dma_start(x2_dram[bass.ds(d * 128, 128), bass.ds(i * ROW, ROW)],
                                 X[:, bass.ds(i * ROW, ROW)]).then_inc(x2_stored, 16)
                    sp.dma_start(u_dram[bass.ds(d * 128, 128), bass.ds(i * ROW, ROW)],
                                 Xn[k][:, :]).then_inc(u_stored[k], 16)

                tiles(sp, store_tile)
            sp.wait_ge(x2_stored, duos * 16 * NWIN + 16)
            sp.wait_ge(u_stored[0], duos * 64 + 16)
            sp.wait_ge(u_stored[1], duos * 48 + 16)

        @block.gpsimd
        def _(pool):
            for m in range(2):
                nc.gpsimd.memset(Qbd[m][:], 0.0)
            nc.gpsimd.memset(eps[:, 0:1], 1e-6)
            nc.gpsimd.memset(eps[:, 1:2], 1e-5)
            nc.gpsimd.memset(Vimg[:], 0.0)
            nc.gpsimd.memset(woh[:], 0.0).then_inc(init_done, 1)
            pool.wait_ge(init_done, 5)
            regs = [pool.alloc_register(f"pool_win{k}") for k in range(TOPK)]

            def square(i, k, tt):
                hold(pool, "pool", cen_ready, tt + 1)
                nc.gpsimd.tensor_tensor(Sq[k], Cen[k], Cen[k], ALU.mult).then_inc(sq_ready, 1)

            with pool.Fori(0, duos) as d:
                tiles(pool, lambda i, k, last: square(i, k, d * UNITS + i))
                hold(pool, "pool", k_loaded, d * (16 * 24) + 16 * 24)
                hold(pool, "pool", idx_stored, d * 32 + 32)
                with pool.Fori(0, NWIN) as i:
                    for m in range(2):
                        src = Kexp[m][:, :, :].bitcast(I32)
                        dst = Ksel[m][:, :, :, :, :].bitcast(I32)
                        for w in range(NWIN):
                            hold(pool, "pool", st_ready, unit_of(d, i, m) * NWIN + (w + 1))
                            pool.load(regs, idxrow[0:1, m, bass.ds((i * NWIN + w) * TOPK, TOPK)])
                            win = [pool.snap(r, min_val=0, max_val=WINDOWS - 1) for r in regs]
                            for k in range(TOPK):
                                nc.gpsimd.tensor_copy(dst[:, w, :, k, :],
                                                      src[:, :, bass.ds(win[k] * (PX // 2), PX // 2)])\
                                    .then_inc(k_gathered, 1)
                tiles(pool, lambda i, k, last: square(i, k, d * UNITS + i + NWIN))

        @block.scalar
        def _(act):
            act.wait_ge(w_loaded, 16 * N_W)
            nc.scalar.activation(identb[:, :], ident[:, :], ACT.Copy).then_inc(init_done, 1)
            for k in range(2):
                nc.scalar.activation(wqk[:, C * k:C * k + C].rearrange("c (h d p) -> c h d p", h=2, p=HP),
                                     wraw[:, C * k:C * k + C].rearrange("c (p h d) -> c h d p", h=2, p=HP),
                                     ACT.Copy).then_inc(init_done, 1)
            act.wait_ge(init_done, 5)
            regs = [act.alloc_register(f"act_win{k}") for k in range(TOPK)]

            def deviation(k, tt, which):
                hold(act, "act", var_ready, tt + 1)
                nc.scalar.activation(Std[k], ps[:, k, 0:ROW], ACT.Sqrt, bias=eps[:, which:which + 1])\
                    .then_inc(std_ready, 1)

            def gather_v(m, i, w):
                act.load(regs, idxrow[0:1, m, bass.ds((i * NWIN + w) * TOPK, TOPK)])
                win = [act.snap(r, min_val=0, max_val=WINDOWS - 1) for r in regs]
                for k in range(TOPK):
                    half = slice(PX * (k % 2), PX * (k % 2) + PX)
                    nc.scalar.activation(Vsel[m][half, w, k // 2], Vpx[m][half, bass.ds(win[k], 1)],
                                         ACT.Copy).then_inc(v_gathered, 1)

            with act.Fori(0, duos) as d:
                def prepare(i, k, last):
                    t = d * NWIN + i
                    for m in range(2):
                        hold(act, "act", qk_ready, t * 2 + (m + 1))
                        nc.scalar.activation(
                            Qk[:, :].rearrange("c (w a b) -> c w a b", w=NWIN, a=WS),
                            ps[:, 2 + m, 0:ROW].rearrange("c (a w b) -> c w a b", w=NWIN, a=WS),
                            ACT.Identity, bias=bqk[:, 0:1]).then_inc(qk_sb, 1)
                        hold(act, "act", qk_sb, t * 2 + (m + 1))
                        hold(act, "act", parts_stored, t * 224 + 16)
                        nc.scalar.activation(Part[m][:, 0, :], Qk[:, :], ACT.Copy).then_inc(part1, 1)
                        if m == 0:
                            hold(act, "act", v_ready, t + 1)
                            nc.scalar.activation(
                                Vimg[:, bass.ds(i * WS + 1, WS), 1:1 + SIDE],
                                ps[:, 4, 0:ROW].rearrange("c (a x) -> c a x", a=WS), ACT.Identity, bias=bv[:, 0:1])
                        elif not last:
                            deviation(1 - k, d * UNITS + i + 1, 0)
                        hold(act, "act", res1, t * 2 + (m + 1))
                        nc.scalar.activation(Part[m][:, 1, :], Res[:, :], ACT.Copy).then_inc(part2, 1)
                        if m == 0:
                            for c in range(2):
                                nc.scalar.activation(Vt[:, :, c, :].rearrange("c w (a b) -> c w a b", a=WS),
                                                     ps[:, 4, 0:ROW].rearrange("c (a w b) -> c w a b", w=NWIN, a=WS),
                                                     ACT.Identity, bias=bv[:, 0:1]).then_inc(vt_sb, 1)
                        hold(act, "act", part3, t * 2 + (m + 1))
                    for m in range(2):
                        hold(act, "act", vT_ready, t * 2 + (m + 1))
                        nc.scalar.activation(Vpx[m][:, bass.ds(i * NWIN, NWIN), :, 0:HD],
                                             ps[:, 5 + 2 * m, 0:ROW].rearrange("q (w h e) -> q w h e", w=NWIN, h=HEADS),
                                             ACT.Copy).then_inc(vpx_done, 1)

                deviation(0, d * UNITS, 0)
                tiles(act, prepare)
                hold(act, "act", idx_stored, d * 32 + 32)
                hold(act, "act", vpx_done, d * UNITS + UNITS)
                for w in range(NWIN):
                    gather_v(0, 0, w)

                def copy_o(sub, g):
                    nw = 4 - sub
                    hold(act, "act", pv_done, g * NWIN + (2 + 4 + 3 * sub))
                    hold(act, "act", on_ready, g * 2 + (sub + 1))
                    nc.scalar.activation(Osb[sub][:, 0:nw].rearrange("c w a q -> c (w a q)"),
                                         ps[:, OB, 0:nw * 128], ACT.Copy).then_inc(o_copied, 1)

                def unit(m, i, nxt, nm, ni, prev):
                    g = unit_of(d, i, m)
                    for w in range(NWIN):
                        n = g * NWIN + w
                        k = (m * NWIN + w) % 2
                        hold(act, "act", st_ready, n + (1 + 14))
                        hold(act, "act", pv_done, n + 1)
                        nc.scalar.activation(Pr[k][:].rearrange("q c p h x -> q (c p h x)"),
                                             ps[:, ST0 + 2 * k:ST0 + 2 * k + 2, :].rearrange("q a b -> q (a b)"),
                                             ACT.Exp, scale=SCALE).then_inc(exp_done, 1)
                        if w == 0 and prev:
                            copy_o(1, g - 1)
                        if w == 4:
                            copy_o(0, g)
                        if nxt:
                            if w == 0:
                                hold(act, "act", pv_done, g * NWIN + 2)
                            gather_v(nm, ni, w)

                def rows(i, first=False, last=False):
                    unit(0, i, True, 1, i, not first)
                    unit(1, i, not last, 0, i + 1, True)

                rows(0, first=True)
                with act.Fori(1, LAST) as i:
                    rows(i)
                rows(LAST, last=True)
                copy_o(1, unit_of(d, LAST, 1))
                tiles(act, lambda i, k, last: deviation(k, d * UNITS + i + NWIN, 1))

        @block.vector
        def _(dve):
            for m in range(2):
                nc.vector.memset(Vpx[m][:], 1.0)
            for n, (s, credit) in enumerate([(max_done, 2), (exp_done, 2), (pv_done, 2), (st_ready, 2 * NWIN),
                                             (o_copied, 1), (misc_free, 1), (on_ready, 2), (mt_copied, 1),
                                             (parts_stored, 16), (x2_stored, 16), (u_stored[0], 16),
                                             (u_stored[1], 16), (std_ready, 2)]):
                nc.vector.memset(nil[:, n:n + 1], 0.0).then_inc(s, credit)
            nc.vector.memset(ps[:, OB, :], 1.0).then_inc(ob_set, 1)
            nc.vector.memset(less[:], 1.0).then_inc(less_step, 1)
            dve.wait_ge(w_loaded, 16 * N_W)
            dve.wait_ge(less_step, 1)
            for n in range(HP * NWIN):
                last = nc.vector.tensor_scalar(less[:, n, :], less[:, n, :], each[:, n:n + 1], None, ALU.mult)
            last.then_inc(init_done, 1)

            def centre(i, k, tt):
                hold(dve, "dve", mean_ready, tt + 1)
                nc.vector.tensor_tensor(Cen[k], X[:, bass.ds(i * ROW, ROW)], ps[:, k, 0:ROW], ALU.subtract)\
                    .then_inc(cen_ready, 1)

            def scale(k, tt, free):
                hold(dve, "dve", std_ready, tt + 3)
                nc.vector.reciprocal(Rstd[k], Std[k]).then_inc(rstd_ready, 1)
                hold(dve, "dve", rstd_ready, tt + 1)
                hold(dve, "dve", u_stored[k], free)
                nc.vector.tensor_tensor(Xn[k][:, :], Cen[k], Rstd[k], ALU.mult).then_inc(xn_ready, 1)

            def row_max(m, w, g):
                for half in range(2):
                    hold(dve, "dve", s_ready, g * 14 + (2 * w + half + 1))
                    nc.vector.tensor_reduce(Mx[m][:, 2 * half:2 * half + 2, w],
                                            ps[:, half, :].rearrange("q (p k) -> q p k", p=2),
                                            AX.X, ALU.max).then_inc(max_done, 1)

            def split_max(m, g):
                flat = Mx[m][:].rearrange("q p w -> q (p w)")
                hold(dve, "dve", max_done, g * 14 + 16)
                nc.vector.tensor_copy(Mb[m][:, 0, :], flat).then_inc(m_split, 1)
                hold(dve, "dve", m_split, g * 4 + 1)
                nc.vector.tensor_tensor(Mr[:, :], flat, Mb[m][:, 0, :], ALU.subtract).then_inc(m_split, 1)
                hold(dve, "dve", m_split, g * 4 + 2)
                nc.vector.tensor_copy(Mb[m][:, 1, :], Mr[:, :]).then_inc(m_split, 1)
                hold(dve, "dve", m_split, g * 4 + 3)
                nc.vector.tensor_tensor(Mb[m][:, 2, :], Mr[:, :], Mb[m][:, 1, :], ALU.subtract).then_inc(m_split, 1)

            def copy_max(m, g):
                hold(dve, "dve", mt_ready, g + 1)
                nc.vector.tensor_copy(MT[m][:].rearrange("r h x -> r (h x)"),
                                      ps[:, 0, :].bitcast(BF16)[0:NMAX, 0:128]).then_inc(mt_copied, 1)

            def normalise(m, sub, on, no):
                nw = 4 - sub
                hold(dve, "dve", misc_ready, no + 1)
                hold(dve, "dve", on_ready, on + 2)
                nc.vector.reciprocal(Rc[:, 0:nw * 128], ps[:, MISC, 0:nw * 128]).then_inc(misc_free, 1)
                hold(dve, "dve", misc_free, no + 2)
                nc.vector.tensor_tensor(On[m][:, 4 * sub:4 * sub + nw].rearrange("c w a q -> c (w a q)"),
                                        Osb[sub][:, 0:nw].rearrange("c w a q -> c (w a q)"),
                                        Rc[:, 0:nw * 128], ALU.mult).then_inc(on_ready, 1)

            with dve.Fori(0, duos) as d:
                hold(dve, "dve", x_loaded, d * 16 + 16)
                def prepare(i, k, last):
                    t = d * NWIN + i
                    tt = d * UNITS + i
                    if not last:
                        centre(i + 1, 1 - k, tt + 1)
                    hold(dve, "dve", xn_ready, tt + 1)
                    nc.vector.tensor_reduce(xm[:, bass.ds(i * NWIN, NWIN)],
                                            Xn[k][:, :].rearrange("c (a w b) -> c w a b", a=WS, w=NWIN),
                                            AX.XY, ALU.add).then_inc(xm_ready, 1)
                    for m in range(2):
                        hold(dve, "dve", part1, t * 2 + (m + 1))
                        nc.vector.tensor_tensor(Res[:, :], Qk[:, :], Part[m][:, 0, :], ALU.subtract).then_inc(res1, 1)
                        hold(dve, "dve", part2, t * 2 + (m + 1))
                        nc.vector.tensor_tensor(Part[m][:, 2, :], Res[:, :], Part[m][:, 1, :], ALU.subtract)\
                            .then_inc(part3, 1)
                    if not last:
                        scale(1 - k, tt + 1, d * (48 + 16 * k) + 16)

                centre(0, 0, d * UNITS)
                scale(0, d * UNITS, d * 64 + 16)
                tiles(dve, prepare)
                hold(dve, "dve", xm_ready, d * NWIN + NWIN)
                nc.vector.tensor_scalar(xms[:, :], xm[:, :], 1.0 / PX, None, ALU.mult).then_inc(xms_ready, 1)
                hold(dve, "dve", win_ready, d + 1)
                for m in range(2):
                    bank = 2 + 2 * m
                    nc.vector.tensor_scalar(qw[:, m, :], ps[0:C, bank, 0:WINDOWS], bqk[0:C, 0:1], None, ALU.add)\
                        .then_inc(win_sb, 1)
                    nc.vector.tensor_scalar(kw[:, m, :], ps[0:C, bank, C:C + WINDOWS], bk0[:, 0:1], None,
                                            ALU.add).then_inc(win_sb, 1)
                hold(dve, "dve", logits_ready, d + 1)
                nc.vector.tensor_copy(lg[:], ps[0:WINDOWS, 3, 0:128].rearrange("a (m b) -> a m b", m=2)[:, :, 0:WINDOWS])\
                    .then_inc(lg_sb, 1)
                hold(dve, "dve", lg_sb, d + 1)
                for m in range(2):
                    nc.vector.max(top[:, m, :], lg[:, m, :]).then_inc(top_ready, 1)
                hold(dve, "dve", top_ready, d * 2 + 2)
                for m in range(2):
                    nc.vector.max_index(idx[:, m, :], top[:, m, :], lg[:, m, :]).then_inc(idx_ready, 1)

                g0 = unit_of(d, 0, 0)
                for w in range(NWIN):
                    row_max(0, w, g0)
                split_max(0, g0)
                copy_max(0, g0)

                def tap(i, k):
                    done = (d * NWIN + i) * 9
                    a, b = k // 3, k % 3
                    src = Vimg[:, bass.ds(i * WS + a, WS), b:b + SIDE]
                    out = Lp[:, :].rearrange("c (y x) -> c y x", y=WS)
                    if k == 0:
                        nc.vector.tensor_scalar(out, src, taps[:, 0:1], None, ALU.mult).then_inc(tap_done, 1)
                    else:
                        hold(dve, "dve", tap_done, done + k)
                        nc.vector.scalar_tensor_tensor(out=out, in0=src, scalar=taps[:, k:k + 1], in1=out,
                                                       op0=ALU.mult, op1=ALU.add).then_inc(tap_done, 1)

                def residual(i):
                    hold(dve, "dve", misc_ready, misc_no(d, i, 1, "out") + 1)
                    nc.vector.scalar_tensor_tensor(
                        out=X[:, bass.ds(i * ROW, ROW)], in0=ps[:, MISC, 0:ROW], scalar=wob[:, 0:1],
                        in1=X[:, bass.ds(i * ROW, ROW)], op0=ALU.add, op1=ALU.add).then_inc(misc_free, 1)

                def unit(m, i, nxt, nm, prev):
                    g = unit_of(d, i, m)
                    wa = 0
                    for w in range(NWIN):
                        if nxt:
                            for _ in range(A_AT[w]):
                                row_max(nm, wa, g + 1)
                                wa += 1
                        if w == 1 and prev:
                            normalise(*prev)
                        if w == 3 and m == 0 and prev:
                            residual(i - 1)
                        if w == LAST and nxt:
                            split_max(nm, g + 1)
                            copy_max(nm, g + 1)
                        k = w - 4 if m == 0 else w + 3
                        if 0 <= k < 9:
                            tap(i, k)
                    normalise(m, 0, g * 2, misc_no(d, i, m, "sum0"))

                def rows(i, first=False, last=False):
                    g = unit_of(d, i, 0)
                    unit(0, i, True, 1, not first and (1, 1, g * 2 - 1, misc_no(d, i - 1, 1, "sum1")))
                    unit(1, i, not last, 0, (0, 1, g * 2 + 1, misc_no(d, i, 0, "sum1")))

                rows(0, first=True)
                with dve.Fori(1, LAST) as i:
                    rows(i)
                rows(LAST, last=True)
                normalise(1, 1, unit_of(d, LAST, 1) * 2 + 1, misc_no(d, LAST, 1, "sum1"))
                residual(LAST)

                def after(i, k, last):
                    if not last:
                        hold(dve, "dve", xn_ready, d * UNITS + i + NWIN)
                        centre(i + 1, 1 - k, d * UNITS + i + (NWIN + 1))
                    scale(k, d * UNITS + i + NWIN, u_count(d, i, k))

                centre(0, 0, d * UNITS + NWIN)
                tiles(dve, after)

        @block.tensor
        def _(pe):
            mm = nc.tensor.matmul
            pe.wait_ge(w_loaded, 16 * N_W)
            pe.wait_ge(woh_loaded, 16 * 4)
            pe.wait_ge(init_done, 5)
            pe.wait_ge(ob_set, 1)

            def mean(i, k, tt):
                hold(pe, "pe", std_ready, tt + 1)
                mm(ps[:, k, 0:ROW], ones64[:, :], X[:, bass.ds(i * ROW, ROW)], start=True, stop=True)\
                    .then_inc(mean_ready, 1)

            def variance(k, tt):
                hold(pe, "pe", sq_ready, tt + 1)
                mm(ps[:, k, 0:ROW], ones64[:, :], Sq[k], start=True, stop=True).then_inc(var_ready, 1)

            def scores(m, w, g):
                hold(pe, "pe", k_gathered, (g * NWIN + w) * TOPK + TOPK)
                if w == 0:
                    hold(pe, "pe", mt_copied, g + 1)
                for half in range(2):
                    hold(pe, "pe", max_done, g * 14 + (2 * w + half + 1))
                    for p in (2 * half, 2 * half + 1):
                        last = mm(ps[:, half, (p % 2) * KEYS:(p % 2) * KEYS + KEYS], Qbd[m][0:QROWS, p, w, :, :].rearrange("r h x -> r (h x)"),
                                  Ksel[m][0:QROWS, w, p, :, :].rearrange("r k x -> r (k x)"), start=True, stop=True)
                    last.then_inc(s_ready, 1)

            def transpose_max(m, g):
                hold(pe, "pe", m_split, g * 4 + 4)
                nc.tensor.transpose(ps[:, 0, :].bitcast(BF16)[0:NMAX, 0:128],
                                    Mb[m][:].rearrange("q k n -> q (k n)"), identb[:, :]).then_inc(mt_ready, 1)

            def scores_t(m, w, g):
                n = g * NWIN + w
                k = (m * NWIN + w) % 2
                if w == 0:
                    hold(pe, "pe", mt_copied, g + 2)
                hold(pe, "pe", exp_done, n + 1)
                for c in range(2):
                    for p in range(HP):
                        out = ps[:, ST0 + 2 * k + c, p * 128:p * 128 + 128]
                        mm(out, Ksel[m][:, w, p, 2 * c:2 * c + 2, :].rearrange("r k x -> r (k x)"),
                           Qbd[m][:, p, w, :, :].rearrange("r h x -> r (h x)"), start=True, stop=False)
                        last = mm(out, less[:, p * NWIN + w, :], MT[m][:].rearrange("r h x -> r (h x)"),
                                  start=False, stop=True)
                last.then_inc(st_ready, 1)

            def weighted(m, w, g):
                n = g * NWIN + w
                k = (m * NWIN + w) % 2
                if w == 0:
                    hold(pe, "pe", v_gathered, g * 28 + 28)
                if w in (0, 4):
                    hold(pe, "pe", o_copied, g * 2 + (w // 4 + 1))
                hold(pe, "pe", exp_done, n + 3)
                col = (w % 4) * 128
                for a in range(2):
                    for c in range(2):
                        for j in range(4):
                            h = 4 * a + j
                            last = mm(ps[32 * j:32 * j + HD + 1, OB, col + 64 * a:col + 64 * a + 64],
                                      Vsel[m][:, w, c, h, :], Pr[k][:, c, h // 2, h % 2, :],
                                      start=(c == 0), stop=(c == 1))
                last.then_inc(pv_done, 1)

            def sums(sub, g, no):
                hold(pe, "pe", o_copied, g * 2 + (sub + 2))
                hold(pe, "pe", misc_free, no + 1)
                nw = 4 - sub
                mm(ps[:, MISC, 0:nw * 128], pick[:, :], Osb[sub][:, 0:nw].rearrange("c w a q -> c (w a q)"),
                   start=True, stop=True).then_inc(misc_ready, 1)

            with pe.Fori(0, duos) as d:
                hold(pe, "pe", x_loaded, d * 16 + 16)
                def prepare(i, k, last):
                    t = d * NWIN + i
                    if not last:
                        mean(i + 1, 1 - k, d * UNITS + i + 1)
                    hold(pe, "pe", xn_ready, d * UNITS + i + 1)
                    for m in range(2):
                        half = slice(C * m, C * m + C)
                        mm(ps[:, 2 + m, 0:ROW], wqk[half, :], Xn[k][half, :], start=True, stop=True).then_inc(qk_ready, 1)
                    for m in range(2):
                        half = slice(C * m, C * m + C)
                        last_mm = mm(ps[half, 4, 0:ROW], wv[half, :], Xn[k][half, :], start=True, stop=True)
                    last_mm.then_inc(v_ready, 1)
                    if not last:
                        variance(1 - k, d * UNITS + i + 1)
                    hold(pe, "pe", vt_sb, t * 2 + 2)
                    for m in range(2):
                        half = slice(C * m, C * m + C)
                        for w in range(NWIN):
                            twice = Vt[half, w].rearrange("c k x -> c (k x)")
                            last_mm = nc.tensor.transpose(ps[:, 5 + 2 * m, w * C:w * C + C], twice, ident[half, half])
                        last_mm.then_inc(vT_ready, 1)

                hold(pe, "pe", std_ready, d * UNITS + 2)
                mean(0, 0, d * UNITS)
                variance(0, d * UNITS)
                tiles(pe, prepare)
                hold(pe, "pe", xms_ready, d + 1)
                for m in range(2):
                    half = slice(C * m, C * m + C)
                    mm(ps[0:C, 2 + 2 * m, 0:WINDOWS], wqk[half, 0:C], xms[half, :], start=True, stop=True)
                    last = mm(ps[0:C, 2 + 2 * m, C:C + WINDOWS], wqk[half, C:2 * C], xms[half, :],
                              start=True, stop=True)
                last.then_inc(win_ready, 1)
                hold(pe, "pe", win_sb, d * 4 + 4)
                for m in range(2):
                    last = mm(ps[0:WINDOWS, 3, C * m:C * m + WINDOWS], qw[:, m, :], kw[:, m, :], start=True, stop=True)
                last.then_inc(logits_ready, 1)

                g0 = unit_of(d, 0, 0)
                hold(pe, "pe", vpx_done, d * UNITS + UNITS)
                hold(pe, "pe", lg_sb, d + 1)
                hold(pe, "pe", q_loaded[0], d * (32 * NWIN) + 32)
                for w in range(NWIN):
                    scores(0, w, g0)
                transpose_max(0, g0)

                def project(i):
                    hold(pe, "pe", misc_free, misc_no(d, i, 1, "out") + 1)
                    hold(pe, "pe", on_ready, (d * NWIN + i) * 4 + 6)
                    hold(pe, "pe", tap_done, (d * NWIN + i) * 9 + 9)
                    for m in range(2):
                        half = slice(C * m, C * m + C)
                        out = ps[half, MISC, 0:ROW]
                        for a in range(2):
                            mm(out, woh[:, a, :], On[m][:, :, a, :].rearrange("c w (y x) -> c y w x", y=WS),
                               start=(a == 0), stop=False)
                        last_mm = mm(out, wo[half, :], Lp[half, :], start=False, stop=True)
                    last_mm.then_inc(misc_ready, 1)

                def unit(m, i, nxt, nm, prev):
                    g = unit_of(d, i, m)
                    wa = 0
                    for w in range(NWIN):
                        scores_t(m, w, g)
                        if nxt:
                            if w == 1:
                                hold(pe, "pe", q_loaded[nm], (d * NWIN + i) * 32 + (32 if nm else 64))
                            for _ in range(A_AT[w]):
                                scores(nm, wa, g + 1)
                                wa += 1
                        if w > 0:
                            weighted(m, w - 1, g)
                        elif prev:
                            weighted(prev[0], LAST, prev[1])
                        if w == 1 and prev:
                            sums(1, prev[1], prev[2])
                        if w == 3 and m == 0 and prev:
                            project(i - 1)
                        if w == LAST and nxt:
                            transpose_max(nm, g + 1)
                    sums(0, g, misc_no(d, i, m, "sum0"))

                def rows(i, first=False, last=False):
                    g = unit_of(d, i, 0)
                    unit(0, i, True, 1, not first and (1, g - 1, misc_no(d, i - 1, 1, "sum1")))
                    unit(1, i, not last, 0, (0, g, misc_no(d, i, 0, "sum1")))

                rows(0, first=True)
                with pe.Fori(1, LAST) as i:
                    rows(i)
                rows(LAST, last=True)
                g = unit_of(d, LAST, 1)
                weighted(1, LAST, g)
                sums(1, g, misc_no(d, LAST, 1, "sum1"))
                project(LAST)
                hold(pe, "pe", misc_free, d * MISC_DUO + (MISC_DUO + 1))

                def after(i, k, last):
                    if not last:
                        mean(i + 1, 1 - k, d * UNITS + i + (NWIN + 1))
                    variance(k, d * UNITS + i + NWIN)

                hold(pe, "pe", std_ready, d * UNITS + (NWIN + 2))
                mean(0, 0, d * UNITS + NWIN)
                tiles(pe, after)


def mixer(nc, u_dram, x2_dram, sigma, phi, m_u, m_plus, m_minus, log_weights, gumbel,
          dft, fwd, inv, idft, inmask, outmask, out_dram):
    n_img = u_dram.shape[0] // C
    COLS = n_img * C
    RA = 2 * AL
    s1_dram = nc.dram_tensor("s1_dram", (2, AL, NB, COLS), F32).ap()
    sp_dram = nc.dram_tensor("sp_dram", (2, AL, NB, KAP), F32).ap()
    z_dram = nc.dram_tensor("z_dram", (AL, n_img, 4, 16 * 2 * C), F32).ap()
    y1_dram = nc.dram_tensor("y1_dram", (2, AL, NB, COLS), F32).ap()

    with ExitStack() as outer:
        def sem(name):
            return outer.enter_context(nc.semaphore(name))

        gate = {e: sem(f"mgate_{e}") for e in ("pe", "act", "dve", "pool", "sp")}

        def hold(eng, name, s, value):
            eng.wait_ge(s, value)
            eng.sem_inc(gate[name], 1)

        def in_two(n):
            return slice(0, n // 16 * 16), slice(n // 16 * 16, n)

        def tensor(ctx, name, shape, dt=F32):
            return ctx.enter_context(nc.sbuf_tensor(name, shape, dt))

        ps = outer.enter_context(nc.psum_tensor("mps", [128, 8, 512], F32))
        E4 = tensor(outer, "E4", [RA, BRANCHES, NA])
        filters = outer.enter_context(ExitStack())
        Gs = tensor(filters, "Gs", [128, 2, 2, NB, C])
        Mbd = tensor(filters, "Mbd", [128, 2, C, C])

        with ExitStack() as ctx:
            D1 = tensor(ctx, "D1", [NA, RA])
            D4 = tensor(ctx, "D4", [NA, BRANCHES, RA])
            Ei = tensor(ctx, "Ei", [RA, NA])
            z8 = tensor(ctx, "z8", [128, 8])
            gum = tensor(ctx, "gum", [128, BRANCHES])
            top = tensor(ctx, "mtop", [128, 8])
            idx = tensor(ctx, "midx", [128, 8], U32)
            idf = tensor(ctx, "idf", [128, 1])
            ex = tensor(ctx, "ex", [128, BRANCHES])
            tot = tensor(ctx, "tot", [128, 1])
            rtot = tensor(ctx, "rtot", [128, 1])
            step = tensor(ctx, "step", [128, BRANCHES])
            one = tensor(ctx, "one", [128, BRANCHES])
            wgt = tensor(ctx, "wgt", [128, BRANCHES])
            dif = tensor(ctx, "dif", [128, BRANCHES])
            inm = tensor(ctx, "inm", [NA, BRANCHES, 4])
            inms = tensor(ctx, "inms", [NA, 4])
            outm = tensor(ctx, "outm", [RA, BRANCHES, 4 * NA])
            outs = tensor(ctx, "outs", [RA, 4 * NA])
            sig = tensor(ctx, "sig", [128, KPHI])
            sq1 = tensor(ctx, "sq1", [128, KPHI])
            sk = tensor(ctx, "sk", [128, KPHI])
            pht = tensor(ctx, "pht", [NA, NB, KPHI])
            U = [tensor(ctx, f"U{k}", [NA, C, NB]) for k in range(2)]
            S1 = [tensor(ctx, f"S1{k}", [RA, NB, 2, C]) for k in range(2)]

            fil = S1[0][0:NA].rearrange("a c b d -> a (c b d)")[:, 0:KAP * NB].rearrange("a (k c) -> a k c", k=KAP)
            Sp = S1[1][:].rearrange("r c b d -> r (c b d)")[:, 0:NB * KAP].rearrange("r (c k) -> r c k", k=KAP)

            ws_loaded = sem("ws_loaded")
            m_loaded = sem("mm_loaded")
            v_step = sem("v_step")
            sk_step = sem("sk_step")
            exp_ready = sem("exp_ready")
            fil_step = sem("fil_step")
            phi_mm = sem("phi_mm")
            phi_sb = sem("phi_sb")
            phi_stored = sem("phi_stored")
            mats_ready = sem("mats_ready")
            u_in = [sem(f"u_in{j}") for j in range(2)]
            s1_mm = sem("s1_mm")
            s1_act = sem("s1_act")
            s1_dve = sem("s1_dve")
            s1_stored = [sem(f"s1_stored{k}") for k in range(2)]
            cleared = sem("cleared")

            block = ctx.enter_context(nc.Block())
            N_WS = 8

            @block.sync
            def _(sp):
                sp.dma_start(z8[:, 0:BRANCHES], log_weights.partition_broadcast(128)).then_inc(ws_loaded, 16)
                sp.dma_start(gum[:, :], gumbel.partition_broadcast(128)).then_inc(ws_loaded, 16)
                sp.dma_start(sig[:, :], sigma.partition_broadcast(128)).then_inc(ws_loaded, 16)
                sp.dma_start(pht[0:32], phi.rearrange("(a c) k -> a c k", c=NB)).then_inc(ws_loaded, 16)
                sp.dma_start(D1[:, :], dft).then_inc(ws_loaded, 16)
                sp.dma_start(Ei[:, :], idft).then_inc(ws_loaded, 16)
                sp.dma_start(inm[:, :, :], inmask).then_inc(ws_loaded, 16)
                sp.dma_start(outm[:].rearrange("r i x -> r (i x)"), outmask.partition_broadcast(RA)).then_inc(ws_loaded, 16)
                raw = Gs[:].rearrange("p a r b e -> p (a r) (b e)")
                for r in (0, C):
                    sp.dma_start(raw[r:r + KPHI], m_plus.rearrange("i k d e -> k i (d e)")).then_inc(m_loaded, 16)
                    sp.dma_start(raw[r + KPHI:r + 2 * KPHI], m_minus.rearrange("i k d e -> k i (d e)")).then_inc(m_loaded, 16)
                    sp.dma_start(raw[r + 2 * KPHI:r + KAP], m_u.rearrange("i k d e -> k i (d e)")).then_inc(m_loaded, 16)
                sp.wait_ge(cleared, 2)

                def load(j, n):
                    hold(sp, "sp", s1_mm, n * 8 + 8)
                    src = u_dram[bass.ds(n * C, C), :].rearrange("d (a c) -> a d c", c=NB)
                    for rows in in_two(NA):
                        sp.dma_start(U[j][rows], src[rows]).then_inc(u_in[j], 16)

                def store(k, p):
                    hold(sp, "sp", s1_act, p * 8 + 12)
                    hold(sp, "sp", s1_dve, p * 8 + 12)
                    dst = s1_dram.rearrange("r a c x -> (r a) c x")[:, :, bass.ds(p * 2 * C, 2 * C)]
                    for rows in in_two(RA):
                        sp.dma_start(dst[rows], S1[k][rows].rearrange("r c b d -> r c (b d)")).then_inc(s1_stored[k], 16)

                load(0, 0)
                load(1, 1)
                sp.wait_ge(phi_sb, 5)
                sp.dma_start(sp_dram.rearrange("r a c k -> (r a) (c k)"), Sp.rearrange("r c k -> r (c k)"))\
                    .then_inc(phi_stored, 16)
                with sp.Fori(0, n_img // 4 - 1) as q:
                    for k in range(2):
                        load(0, q * 4 + (2 * k + 2))
                        load(1, q * 4 + (2 * k + 3))
                        store(k, q * 2 + k)
                load(0, n_img - 2)
                load(1, n_img - 1)
                store(0, n_img // 2 - 2)
                store(1, n_img // 2 - 1)
                for k in range(2):
                    sp.wait_ge(s1_stored[k], n_img // 4 * 32 + 16)
                sp.wait_ge(phi_stored, 16)

            @block.gpsimd
            def _(pool):
                nc.gpsimd.memset(Mbd[:], 0.0).then_inc(cleared, 1)
                nc.gpsimd.memset(fil, 0.0).then_inc(cleared, 1)

            @block.scalar
            def _(act):
                act.wait_ge(ws_loaded, 16 * N_WS)
                nc.scalar.activation(sq1[:, :], sig[:, :], ACT.Sqrt).then_inc(sk_step, 1)
                act.wait_ge(sk_step, 1)
                nc.scalar.activation(sk[:, :], sq1[:, :], ACT.Sqrt).then_inc(sk_step, 1)
                act.wait_ge(v_step, 3)
                nc.scalar.activation(ex[:, :], z8[:, 4:8], ACT.Exp).then_inc(exp_ready, 1)
                for n in range(5):
                    k0, nk = 8 * n, min(8, KAP - 8 * n)
                    act.wait_ge(phi_mm, n + 1)
                    nc.scalar.activation(Sp[:, :, k0:k0 + nk].rearrange("r c k -> r k c"),
                                         ps[0:RA, n, 0:nk * NB].rearrange("r (k c) -> r k c", k=nk),
                                         ACT.Copy).then_inc(phi_sb, 1)

                def evacuate(k, j, q):
                    n = q * 4 + (2 * k + j)
                    for m in range(0, 8, 2):
                        cls, d0, nd = CUTS[m]
                        c0, w = CLASSES[cls]
                        hold(act, "act", s1_mm, n * 8 + (m + 17))
                        if m == 0:
                            hold(act, "act", s1_stored[k], q * 32 + 16)
                        nc.scalar.activation(S1[k][:, c0:c0 + w, j, d0:d0 + nd].rearrange("r c d -> r d c"),
                                             ps[0:RA, m, :].rearrange("r (d c) -> r d c", c=w),
                                             ACT.Copy).then_inc(s1_act, 1)

                act.wait_ge(phi_stored, 16)
                with act.Fori(0, n_img // 4) as q:
                    for k in range(2):
                        for j in range(2):
                            evacuate(k, j, q)

            @block.vector
            def _(dve):
                nc.vector.memset(dif[:, :], 0.0).then_inc(s1_mm, 16)
                nc.vector.memset(top[:, :], 0.0).then_inc(s1_act, 4)
                nc.vector.memset(ex[:, :], 0.0).then_inc(s1_dve, 4)
                nc.vector.memset(idf[:, :], 0.0).then_inc(s1_stored[0], 16)
                nc.vector.memset(rtot[:, :], 0.0).then_inc(s1_stored[1], 16)
                for i in range(BRANCHES):
                    nc.vector.memset(step[:, i:i + 1], float(i))
                dve.wait_ge(ws_loaded, 16 * N_WS)
                count = 0

                def step_done(ins):
                    nonlocal count
                    ins.then_inc(v_step, 1)
                    count += 1
                    dve.wait_ge(v_step, count)

                step_done(nc.vector.tensor_tensor(gum[:, :], gum[:, :], z8[:, 0:4], ALU.add))
                step_done(nc.vector.tensor_reduce(tot[:, :], gum[:, :], AX.X, ALU.max))
                step_done(nc.vector.tensor_scalar(z8[:, 4:8], gum[:, :], tot[:, 0:1], None, ALU.subtract))
                dve.wait_ge(exp_ready, 1)
                step_done(nc.vector.tensor_reduce(tot[:, :], ex[:, :], AX.X, ALU.add))
                step_done(nc.vector.reciprocal(rtot[:, :], tot[:, :]))
                step_done(nc.vector.tensor_scalar(z8[:, 0:4], ex[:, :], rtot[:, 0:1], None, ALU.mult))
                step_done(nc.vector.memset(z8[:, 4:8], -1.0))
                step_done(nc.vector.max(top[:, :], z8[:, :]))
                step_done(nc.vector.max_index(idx[:, :], top[:, :], z8[:, :]))
                step_done(nc.vector.tensor_copy(idf[:, :], idx[:, 0:1]))
                step_done(nc.vector.tensor_scalar(one[:, :], step[:, :], idf[:, 0:1], None, ALU.is_equal))
                step_done(nc.vector.tensor_tensor(dif[:, :], one[:, :], z8[:, 0:4], ALU.subtract))
                step_done(nc.vector.tensor_tensor(wgt[:, :], dif[:, :], z8[:, 0:4], ALU.add))
                dve.wait_ge(cleared, 2)
                dve.wait_ge(sk_step, 2)
                for k in range(KPHI):
                    last = nc.vector.tensor_scalar(fil[0:32, k, :], pht[0:32, :, k], sk[0:32, k:k + 1], None, ALU.mult)
                step_done(last)
                even = fil[0:32].rearrange("a k (c s) -> a k c s", s=2)
                nc.vector.tensor_scalar(even[:, KPHI:2 * KPHI, :, 0], even[:, 0:KPHI, :, 0], 1.0, None, ALU.mult)
                nc.vector.tensor_scalar(even[:, KPHI:2 * KPHI, :, 1], even[:, 0:KPHI, :, 1], -1.0, None, ALU.mult)
                for i in range(KAR):
                    last = nc.vector.memset(fil[0:1, 2 * KPHI + i, i:i + 1], 1.0)
                last.then_inc(fil_step, 1)
                for src, dst in ((inm, inms), (outm, outs)):
                    p = dst.shape[0]
                    step_done(nc.vector.tensor_scalar(dst[:, :], src[:, 0, :], one[0:p, 0:1], None, ALU.mult))
                    for i in range(1, BRANCHES):
                        step_done(nc.vector.scalar_tensor_tensor(out=dst[:, :], in0=src[:, i, :], scalar=one[0:p, i:i + 1],
                                                                 in1=dst[:, :], op0=ALU.mult, op1=ALU.add))
                for cls in range(4):
                    nc.vector.tensor_scalar(D4[:, cls, :], D1[:, :], inms[:, cls:cls + 1], None, ALU.mult)
                    last = nc.vector.tensor_tensor(E4[:, cls, :], Ei[:, :], outs[:, cls * NA:cls * NA + NA], ALU.mult)
                last.then_inc(mats_ready, 1)
                raw = Gs[:].rearrange("p a r b e -> p (a r) (b e)")
                dve.wait_ge(m_loaded, 16 * 6)
                for h in range(2):
                    rows = slice(C * h, C * h + KAP)
                    dst = Mbd[rows, h].rearrange("p d e -> p (d e)")
                    step_done(nc.vector.tensor_scalar(dst, raw[rows, 0, :], wgt[rows, 0:1], None, ALU.mult))
                    for i in range(1, BRANCHES):
                        step_done(nc.vector.scalar_tensor_tensor(out=dst, in0=raw[rows, i, :], scalar=wgt[rows, i:i + 1],
                                                                 in1=dst, op0=ALU.mult, op1=ALU.add))

                def evacuate(k, j, q):
                    n = q * 4 + (2 * k + j)
                    for m in range(1, 8, 2):
                        cls, d0, nd = CUTS[m]
                        c0, w = CLASSES[cls]
                        hold(dve, "dve", s1_mm, n * 8 + (m + 17))
                        if m == 1:
                            hold(dve, "dve", s1_stored[k], q * 32 + 16)
                        nc.vector.tensor_copy(S1[k][:, c0:c0 + w, j, d0:d0 + nd].rearrange("r c d -> r d c"),
                                              ps[0:RA, m, :].rearrange("r (d c) -> r d c", c=w)).then_inc(s1_dve, 1)

                dve.wait_ge(phi_stored, 16)
                with dve.Fori(0, n_img // 4) as q:
                    for k in range(2):
                        for j in range(2):
                            evacuate(k, j, q)

            @block.tensor
            def _(pe):
                mm = nc.tensor.matmul
                pe.wait_ge(fil_step, 1)
                for n in range(5):
                    k0, nk = 8 * n, min(8, KAP - 8 * n)
                    mm(ps[0:RA, n, 0:nk * NB], D1[:, :], fil[:, k0:k0 + nk, :].rearrange("a k c -> a (k c)"),
                       start=True, stop=True).then_inc(phi_mm, 1)
                pe.wait_ge(phi_sb, 5)
                pe.wait_ge(mats_ready, 1)
                with pe.Fori(0, n_img // 2) as q:
                    for j in range(2):
                        n = q * 2 + j
                        hold(pe, "pe", u_in[j], q * 32 + 32)
                        for m, (cls, d0, nd) in enumerate(CUTS):
                            c0, w = CLASSES[cls]
                            hold(pe, "pe", s1_dve if m % 2 else s1_act, n * 4 + (m // 2 + 1))
                            mm(ps[0:RA, m, :], D4[:, cls, :], U[j][:, d0:d0 + nd, c0:c0 + w],
                               start=True, stop=True).then_inc(s1_mm, 1)

        with ExitStack() as ctx:
            Fw = tensor(ctx, "Fw", [128, 2, 3 * NB])
            Iv = tensor(ctx, "Iv", [128, 2, 2 * NB])
            Sf = tensor(ctx, "Sf", [128, 2, KAP])
            Sin = tensor(ctx, "Sin", [128, 2, COLS])
            Uh = [tensor(ctx, f"Uh{k}", [128, n_img, NB]) for k in range(2)]
            Vh = tensor(ctx, "Vh", [128, 2, 2 * NB])
            Zs = [tensor(ctx, f"Zs{k}", [128, 4, 4 * 2 * C]) for k in range(2)]
            Zr = [tensor(ctx, f"Zr{k}", [128, n_img, C]) for k in range(2)]
            Ys = [tensor(ctx, f"Ys{k}", [128, COLS]) for k in range(2)]
            nil = tensor(ctx, "mnil", [1, 16])

            in_loaded = sem("in_loaded")
            iv_loaded = sem("iv_loaded")
            v_mm = sem("v_mm")
            v_sb = sem("v_sb")
            g_mm = sem("g_mm")
            g_act = sem("g_act")
            g_dve = sem("g_dve")
            uh_mm = sem("uh_mm")
            uh_act = sem("uh_act")
            uh_dve = sem("uh_dve")
            z_mm = sem("z_mm")
            z_act = sem("z_act")
            z_dve = sem("z_dve")
            z_stored = [sem(f"z_stored{k}") for k in range(2)]
            z_loaded = [sem(f"z_loaded{k}") for k in range(2)]
            i_mm = sem("i_mm")
            i_act = sem("i_act")
            i_dve = sem("i_dve")
            y_stored = [sem(f"y_stored{k}") for k in range(2)]
            b_init = sem("b_init")

            block = ctx.enter_context(nc.Block())
            Z_BANK, I_BANK = 4, 6

            @block.sync
            def _(sp):
                def load_in(p):
                    for r in range(2):
                        half = slice(NB * r, NB * r + NB)
                        sp.dma_start(Sin[half], s1_dram[r].rearrange("a c x -> c a x")[:, bass.ds(p * 2, 2), :])\
                            .then_inc(in_loaded, 16)
                        sp.dma_start(Sf[half], sp_dram[r].rearrange("a c k -> c a k")[:, bass.ds(p * 2, 2), :])\
                            .then_inc(in_loaded, 16)
                    sp.dma_start(Fw[:], fwd[:, bass.ds(p * 2, 2), :]).then_inc(in_loaded, 16)

                def load_inverse(p):
                    sp.dma_start(Iv[:], inv[:, bass.ds(p * 2, 2), :]).then_inc(iv_loaded, 16)

                def store_inverse(p):
                    for k in range(2):
                        hold(sp, "sp", i_act, p * 2 + (k + 2))
                        hold(sp, "sp", i_dve, p * 2 + (k + 2))
                        for r in range(2):
                            half = slice(NB * r, NB * r + NB)
                            sp.dma_start(y1_dram[r].rearrange("a c x -> c a x")[:, bass.ds(p * 2 + k, 1), :]
                                         .rearrange("c a x -> c (a x)"), Ys[k][half, :]).then_inc(y_stored[k], 16)

                def turn(p):
                    for k in range(2):
                        hold(sp, "sp", z_act, p * 4 + (2 * k + 3))
                        hold(sp, "sp", z_dve, p * 4 + (2 * k + 3))
                        for q in range(4):
                            sp.dma_start(z_dram.rearrange("a b q x -> q a b x")[q][bass.ds(p * 2 + k, 1)]
                                         .rearrange("a b x -> (a b) x"),
                                         Zs[k][32 * q:32 * q + n_img].rearrange("b j x -> b (j x)")).then_inc(z_stored[k], 16)
                    for k in range(2):
                        hold(sp, "sp", z_stored[k], p * 64 + 80)
                        hold(sp, "sp", i_mm, p * 4 + 4)
                        sp.dma_start(Zr[k][:, :, :], z_dram[bass.ds(p * 2 + k, 1)]
                                     .rearrange("a b q (j e) -> (a q j) b e", e=C)).then_inc(z_loaded[k], 16)

                sp.wait_ge(b_init, 1)
                load_in(0)
                load_inverse(0)
                sp.wait_ge(uh_mm, 4)
                load_in(1)
                turn(0)

                def step(p, last):
                    store_inverse(p - 1)
                    load_inverse(p)
                    if not last:
                        hold(sp, "sp", uh_mm, p * 4 + 4)
                        load_in(p + 1)
                    turn(p)

                with sp.Fori(1, PAIRS - 1) as p:
                    step(p, False)
                step(PAIRS - 1, True)
                store_inverse(PAIRS - 1)
                for k in range(2):
                    sp.wait_ge(y_stored[k], PAIRS * 32 + 16)

            def copy_g(eng, name, copy, s, odd, p):
                hold(eng, name, z_mm, p * 8 + 1)
                for n in range(odd, 32, 2):
                    hold(eng, name, g_mm, p * 32 + (n + 1))
                    copy(Gs[:, :, :, :, 2 * n:2 * n + 2].rearrange("p a r b e -> p (a r) b e"),
                         ps[:, n % 4, :].rearrange("p (e x b) -> p x b e", e=2, b=NB)).then_inc(s, 1)

            def copy_uh(eng, name, copy, s, odd, p):
                for k in range(2):
                    hold(eng, name, uh_mm, p * 4 + (2 * k + odd + 1))
                    copy(Uh[k][:, 8 * odd:8 * odd + 8].rearrange("p b x -> p (b x)"), ps[:, 2 * k + odd, :]).then_inc(s, 1)

            def copy_z(eng, name, copy, s, odd, p):
                for t in range(odd, 8, 2):
                    if t < 4:
                        hold(eng, name, z_stored[0], p * 64 + 16)
                    else:
                        hold(eng, name, z_stored[1], p * 64 + 16)
                    hold(eng, name, z_mm, p * 8 + (t + 2))
                    copy(Zs[t // 4][:, t % 4, :], ps[:, Z_BANK + odd, :]).then_inc(s, 1)

            def copy_inverse(eng, name, copy, s, odd, p):
                for k in range(2):
                    hold(eng, name, i_mm, p * 4 + (2 * k + odd + 5))
                    hold(eng, name, y_stored[k], p * 32 + 16)
                    copy(Ys[k][:, 512 * odd:512 * odd + 512], ps[:, I_BANK + odd, :]).then_inc(s, 1)

            @block.scalar
            def _(act):
                def copy(out, in_):
                    return nc.scalar.activation(out, in_, ACT.Copy)

                act.wait_ge(b_init, 1)

                def step(p, first):
                    hold(act, "act", v_mm, p + 1)
                    copy(Vh[0:KAP].rearrange("k a x -> k (a x)"), ps[0:KAP, I_BANK, 0:256]).then_inc(v_sb, 1)
                    copy_g(act, "act", copy, g_act, 0, p)
                    if not first:
                        copy_inverse(act, "act", copy, i_act, 0, p - 1)
                    copy_uh(act, "act", copy, uh_act, 0, p)
                    copy_z(act, "act", copy, z_act, 0, p)

                step(0, True)
                with act.Fori(1, PAIRS) as p:
                    step(p, False)
                copy_inverse(act, "act", copy, i_act, 0, PAIRS - 1)

            @block.vector
            def _(dve):
                copy = nc.vector.tensor_copy
                nc.vector.memset(ps[:, Z_BANK:Z_BANK + 2, :], 0.0)
                nc.vector.memset(Vh[:], 0.0)
                for n, (s, credit) in enumerate([(g_act, 2), (g_dve, 2), (z_mm, 1), (z_act, 1), (z_dve, 1), (i_mm, 4),
                                                 (i_act, 1), (i_dve, 1), (z_stored[0], 16), (z_stored[1], 16),
                                                 (y_stored[0], 16), (y_stored[1], 16), (b_init, 1)]):
                    nc.vector.memset(nil[:, n:n + 1], 0.0).then_inc(s, credit)

                def step(p, first):
                    hold(dve, "dve", v_mm, p + 1)
                    copy(Vh[C:C + KAP].rearrange("k a x -> k (a x)"), ps[C:C + KAP, I_BANK, 0:256]).then_inc(v_sb, 1)
                    copy_g(dve, "dve", copy, g_dve, 1, p)
                    if not first:
                        copy_inverse(dve, "dve", copy, i_dve, 1, p - 1)
                    copy_uh(dve, "dve", copy, uh_dve, 1, p)
                    copy_z(dve, "dve", copy, z_dve, 1, p)

                dve.wait_ge(b_init, 1)
                step(0, True)
                with dve.Fori(1, PAIRS) as p:
                    step(p, False)
                copy_inverse(dve, "dve", copy, i_dve, 1, PAIRS - 1)

            @block.tensor
            def _(pe):
                mm = nc.tensor.matmul
                pe.wait_ge(b_init, 1)

                def inverse(p):
                    hold(pe, "pe", iv_loaded, p * 16 + 16)
                    for k in range(2):
                        hold(pe, "pe", z_loaded[k], p * 16 + 16)
                        for h in range(2):
                            hold(pe, "pe", i_dve if h else i_act, p * 2 + (k + 1))
                            mm(ps[:, I_BANK + h, :], Iv[:, k, :], Zr[k][:, 8 * h:8 * h + 8, :].rearrange("x b e -> x (b e)"),
                               start=True, stop=True).then_inc(i_mm, 1)

                def step(p, first):
                    hold(pe, "pe", in_loaded, p * 80 + 80)
                    if not first:
                        hold(pe, "pe", i_act, p * 2 - 1)
                    for k in range(2):
                        mm(ps[0:KAP, I_BANK, 128 * k:128 * k + 128], Sf[:, k, :], Fw[:, k, NB:3 * NB], start=True, stop=True)
                        last = mm(ps[C:C + KAP, I_BANK, 128 * k:128 * k + 128], Sf[:, k, :], Fw[:, k, 0:2 * NB],
                                  start=True, stop=True)
                    last.then_inc(v_mm, 1)
                    hold(pe, "pe", v_sb, p * 2 + 2)
                    for n in range(32):
                        hold(pe, "pe", g_dve if n % 2 else g_act, p * 16 + (n // 2 + 1))
                        for e in range(2):
                            last = mm(ps[:, n % 4, 256 * e:256 * e + 256],
                                      Mbd[:, :, :, 2 * n + e].rearrange("k h d -> k (h d)"),
                                      Vh[:].rearrange("k a x -> k (a x)"), start=True, stop=True)
                        last.then_inc(g_mm, 1)
                    if not first:
                        inverse(p - 1)
                    hold(pe, "pe", g_act, p * 16 + 18)
                    hold(pe, "pe", g_dve, p * 16 + 18)
                    for k in range(2):
                        for b in range(n_img):
                            bank, col = 2 * k + b // 8, (b % 8) * NB
                            mm(ps[0:C, bank, col:col + NB], Sin[:, k, b * C:b * C + C], Fw[:, k, NB:2 * NB],
                               start=True, stop=True)
                            last = mm(ps[C:2 * C, bank, col:col + NB], Sin[:, k, b * C:b * C + C], Fw[:, k, 2 * NB:3 * NB],
                                      start=True, stop=True)
                            if b % 8 == 7:
                                last.then_inc(uh_mm, 1)
                    for k in range(2):
                        hold(pe, "pe", uh_act, p * 2 + (k + 1))
                        hold(pe, "pe", uh_dve, p * 2 + (k + 1))
                        for jj in range(4):
                            t = 4 * k + jj
                            hold(pe, "pe", z_dve if t % 2 else z_act, p * 4 + (t // 2 + 1))
                            for j in range(4):
                                for q in range(4):
                                    be = 16 * q + 4 * jj + j
                                    last = mm(ps[32 * q:32 * q + n_img, Z_BANK + t % 2, 128 * j:128 * j + 128],
                                              Uh[k][:, :, be], Gs[:, k, :, be, :], start=True, stop=True)
                            last.then_inc(z_mm, 1)

                step(0, True)
                with pe.Fori(1, PAIRS) as p:
                    step(p, False)
                inverse(PAIRS - 1)

        filters.close()

        with ExitStack() as ctx:
            Y1 = [tensor(ctx, f"Y1{k}", [RA, NB, 2, C]) for k in range(2)]
            Xr = [tensor(ctx, f"Xr{k}", [NA, C, NB]) for k in range(4)]
            nil = tensor(ctx, "nil2", [1, 5])
            c_in = [sem(f"c_in{k}") for k in range(2)]
            c_mm = sem("c_mm")
            c_dve = sem("c_dve")
            c_stored = [sem(f"c_stored{k}") for k in range(2)]
            c_init = sem("c_init")
            block = ctx.enter_context(nc.Block())

            @block.sync
            def _(sp):
                sp.wait_ge(c_init, 1)

                def load(k, q):
                    p = q * 2 + k
                    hold(sp, "sp", c_mm, p * 16 + 16)
                    src = y1_dram.rearrange("r a c x -> (r a) c x")[:, :, bass.ds(p * 2 * C, 2 * C)]
                    for rows in in_two(RA):
                        sp.dma_start(Y1[k][rows].rearrange("r c b e -> r c (b e)"), src[rows]).then_inc(c_in[k], 16)
                    hold(sp, "sp", c_stored[k], q * 64 + 16)
                    for j in range(2):
                        src = x2_dram[bass.ds((p * 2 + j) * C, C), :].rearrange("e (a c) -> a e c", c=NB)
                        for rows in in_two(NA):
                            sp.dma_start(Xr[2 * k + j][rows], src[rows]).then_inc(c_in[k], 16)

                def store(k, q):
                    for j in range(2):
                        n = q * 4 + (2 * k + j)
                        hold(sp, "sp", c_dve, n * 8 + 16)
                        dst = out_dram[bass.ds(n * C, C), :].rearrange("e (a c) -> a e c", c=NB)
                        for rows in in_two(NA):
                            sp.dma_start(dst[rows], Xr[2 * k + j][rows]).then_inc(c_stored[k], 16)

                load(0, 0)
                with sp.Fori(0, n_img // 4 - 1) as q:
                    load(1, q)
                    store(0, q)
                    load(0, q + 1)
                    store(1, q)
                load(1, n_img // 4 - 1)
                store(0, n_img // 4 - 1)
                store(1, n_img // 4 - 1)
                for k in range(2):
                    sp.wait_ge(c_stored[k], n_img // 4 * 64 + 16)

            @block.vector
            def _(dve):
                for n, (s, credit) in enumerate([(c_mm, 32), (c_dve, 8), (c_stored[0], 16), (c_stored[1], 16)]):
                    nc.vector.memset(nil[:, n:n + 1], 0.0).then_inc(s, credit)
                nc.vector.memset(nil[:, 4:5], 0.0).then_inc(c_init, 1)
                with dve.Fori(0, n_img // 4) as q:
                    for k in range(2):
                        hold(dve, "dve", c_in[k], q * 96 + 96)
                        for j in range(2):
                            n = q * 4 + (2 * k + j)
                            for m, (cls, e0, ne) in enumerate(CUTS):
                                c0, w = CLASSES[cls]
                                part = Xr[2 * k + j][:, e0:e0 + ne, c0:c0 + w]
                                hold(dve, "dve", c_mm, n * 8 + (m + 33))
                                nc.vector.tensor_tensor(part, ps[0:NA, m, :].rearrange("a (e c) -> a e c", c=w), part,
                                                        ALU.add).then_inc(c_dve, 1)

            @block.tensor
            def _(pe):
                pe.wait_ge(c_init, 1)
                with pe.Fori(0, n_img // 4) as q:
                    for k in range(2):
                        hold(pe, "pe", c_in[k], q * 96 + 96)
                        for j in range(2):
                            n = q * 4 + (2 * k + j)
                            for m, (cls, e0, ne) in enumerate(CUTS):
                                c0, w = CLASSES[cls]
                                hold(pe, "pe", c_dve, n * 8 + (m + 1))
                                nc.tensor.matmul(ps[0:NA, m, :], E4[:, cls, :],
                                                 Y1[k][:, c0:c0 + w, j, e0:e0 + ne].rearrange("r c e -> r e c"),
                                                 start=True, stop=True).then_inc(c_mm, 1)


def dft_mats():
    import numpy as np
    al = np.arange(AL)
    a, c, be = np.arange(NB), np.arange(NB), np.arange(NB)
    t1 = 2 * np.pi * ((a[:NA, None] * al[None, :]) % NB) / NB
    dft = np.concatenate([np.cos(t1), -np.sin(t1)], 1)
    t2 = 2 * np.pi * ((c[:, None, None] * (al[None, :, None] + NB * be[None, None, :])) % NF) / NF
    re, im = np.cos(t2), -np.sin(t2)
    fwd = np.concatenate([np.concatenate([-im, re, im], 2), np.concatenate([-re, -im, re], 2)], 0)
    ce, se = np.cos(t2), np.sin(t2)
    inv = np.empty((NB, 2, AL, 2, NB))
    inv[:, 0, :, 0], inv[:, 1, :, 0] = ce.transpose(2, 1, 0), -se.transpose(2, 1, 0)
    inv[:, 0, :, 1], inv[:, 1, :, 1] = se.transpose(2, 1, 0), ce.transpose(2, 1, 0)
    weight = np.where((al == 0) | (al == 32), 1.0, 2.0) * (al < 33) / NF
    idft = np.concatenate([np.cos(t1) * weight, -np.sin(t1) * weight], 1).T
    cut = TOKENS // 2 ** np.arange(BRANCHES)
    first = np.array([c0 for c0, _ in CLASSES])
    inside = NB * a[:NA, None, None] + first[None, None, :] < cut[None, :, None]
    inmask = inside
    outmask = inside.transpose(1, 2, 0).reshape(-1)
    return [np.ascontiguousarray(m, np.float32) for m in (dft, fwd, inv.reshape(2 * NB, AL, 2 * NB), idft, inmask, outmask)]


def const_mats():
    import numpy as np
    mats = np.zeros((4, 128, 128), np.float32)
    for m in range(2):
        mats[0, C * m:C * m + C, C * m:C * m + C] = 1.0 / C
    mats[1] = np.eye(128, dtype=np.float32)
    for j in range(4):
        mats[2, 32 * j + HD, 32 * j:32 * j + 32] = 1.0
    for part in range(3):
        mats[3, HP * NWIN * part:HP * NWIN * (part + 1), 0:HP * NWIN] = -np.eye(HP * NWIN)
    return mats


_INPUTS = ["x", "L0_conv_qkv_w", "L0_conv_qkv_b", "L0_conv_lepe_w", "L0_conv_wo_w", "L0_conv_wo_b",
           "L0_ffn_sigma", "L0_ffn_phi", "L0_ffn_M_u", "L0_ffn_M_phi_plus", "L0_ffn_M_phi_minus",
           "L0_ffn_log_weights", "L0_ffn_gumbel"]


def kernel(**inputs):
    import numpy as np
    import concourse.bacc as _bacc
    from concourse import mybir as _mybir
    from concourse.bass_utils import run_bass_kernel_spmd as _run
    nc = _bacc.Bacc("TRN2", target_bir_lowering=False, num_devices=1)
    arrays = {}

    def given(name, array):
        arrays[name] = np.ascontiguousarray(array)
        return nc.dram_tensor(name, arrays[name].shape, _mybir.dt.from_np(arrays[name].dtype),
                              kind="ExternalInput").ap()

    x, qkv_w, qkv_b, lepe_w, wo_w, wo_b, *ffn = [given(f"in_{n}", inputs[n]) for n in _INPUTS]
    mats = given("att_mats", const_mats())
    dfts = [given(f"dft_mats{n}", m) for n, m in enumerate(dft_mats())]
    out = nc.dram_tensor("out0", x.shape, F32, kind="ExternalOutput").ap()
    rows = x.shape[0] * C
    x2_dram = nc.dram_tensor("x2_dram", (rows, TOKENS), F32).ap()
    u_dram = nc.dram_tensor("u_dram", (rows, TOKENS), F32).ap()
    attention(nc, x, qkv_w, qkv_b, lepe_w, wo_w, wo_b, mats, x2_dram, u_dram)
    mixer(nc, u_dram, x2_dram, *ffn, *dfts, out.rearrange("n c h w -> (n c) (h w)"))
    result = _run(nc, [arrays], core_ids=[0])
    return result.results[0]["out0"]
```

```python
from contextlib import ExitStack

import concourse.bass as bass
from concourse import mybir

F32 = mybir.dt.float32
BF16 = mybir.dt.bfloat16
I32 = mybir.dt.int32
U32 = mybir.dt.uint32
ALU = mybir.AluOpType
ACT = mybir.ActivationFunctionType
AX = mybir.AxisListType

C = 64
SIDE = 56
TOKENS = SIDE * SIDE
NWIN = 7
WINDOWS = NWIN * NWIN
WS = SIDE // NWIN
PX = WS * WS
ROW = NWIN * PX
HEADS, HD = 8, 8
HP = HEADS // 2
TOPK = 4
KEYS = TOPK * PX
PAD = SIDE + 2
TERMS = [(0, 0), (0, 1), (0, 2), (1, 0), (1, 1), (2, 0)]
TR = len(TERMS) * HD
QROWS = 2 * TR
NMAX = 3 * HP * NWIN
SCALE = float(C) ** -0.5
SUMS = HEADS * ROW
TAPS_AT = [(0, 1, 5, 6, 6), (0, 0, 1, 5)]
SPLIT_AT = 5
A_AT = [0, 1, 2, 2, 2, 0, 0]


NF = 4096
NA, NB = 49, 64
AL = 34
PAIRS = AL // 2
KPHI = 16
KAR = 3
KAP = 2 * KPHI + KAR
BRANCHES = 4
CLASSES = [(0, 8), (8, 8), (16, 16), (32, 32)]
CUTS = [(3, 0, 16), (3, 16, 16), (3, 32, 16), (3, 48, 16), (2, 0, 32), (2, 32, 32), (1, 0, 64), (0, 0, 64)]



def attention(nc, x, qkv_w, qkv_b, lepe_w, wo_w, wo_b, mats, x2_dram, u_dram):
    n_img = x.shape[0]
    duos = n_img // 2
    xv = x.rearrange("n c h w -> (n c) (h w)")
    with ExitStack() as ctx:
        def sb(name, shape, dt=F32):
            return ctx.enter_context(nc.sbuf_tensor(name, shape, dt))

        def sem(name):
            return ctx.enter_context(nc.semaphore(name))

        q_dram = nc.dram_tensor("q_dram", (2, NWIN, 2, len(TERMS), HD * HP, ROW), BF16).ap()
        k_dram = nc.dram_tensor("k_dram", (2, 3, C, TOKENS), BF16).ap()

        sums_dram = nc.dram_tensor("sums_dram", (2, 4, SUMS // 4), F32).ap()
        rsums_dram = nc.dram_tensor("rsums_dram", (2, 4, SUMS // 4), F32).ap()

        ones64 = sb("ones64", [128, 128])
        ident = sb("ident", [128, 128])
        identb = sb("identb", [128, 128], BF16)
        each = sb("each", [NMAX, HP * NWIN])
        less = sb("less", [NMAX, HP * NWIN, 2 * PX], BF16)
        wqk = sb("wqk", [128, 2 * C])
        wraw = sb("wraw", [128, 2 * C])
        wv = sb("wv", [128, C])
        bqk = sb("bqk", [128, 1])
        bk0 = sb("bk0", [C, 1])
        bv = sb("bv", [128, 1])
        taps = sb("taps", [128, 9])
        wo = sb("wo", [128, C])
        woh = sb("woh", [128, 2, C])
        wob = sb("wob", [128, 1])
        X = sb("X", [128, TOKENS])
        Vimg = sb("Vimg", [128, PAD, PAD])
        Kexp = [sb(f"Kexp{m}", [QROWS, HP, TOKENS], BF16) for m in range(2)]
        Vpx = [sb(f"Vpx{m}", [128, WINDOWS, HEADS, HD + 1]) for m in range(2)]
        idxrow = sb("idxrow", [1, 2, WINDOWS * TOPK], I32)
        Lp = sb("Lp", [128, ROW])
        nil = sb("nil", [1, 16])
        eps = sb("eps", [128, 2])
        Xn = [sb(f"Xn{k}", [128, ROW]) for k in range(2)]
        Res = [sb(f"Res{m}", [128, ROW]) for m in range(2)]
        part0 = [sb(f"Part{m}", [128, 3, ROW], BF16) for m in range(2)]
        Vt = sb("Vt", [128, NWIN, 2, PX])
        xm = sb("xm", [128, WINDOWS])
        xms = sb("xms", [128, WINDOWS])
        qw = sb("qw", [C, 2, WINDOWS])
        kw = sb("kw", [C, 2, WINDOWS])
        lg = sb("lg", [WINDOWS, 2, WINDOWS])
        top = sb("top", [WINDOWS, 2, 8])
        idx = sb("idx", [WINDOWS, 2, 8], U32)
        Qbd = [sb(f"Qbd{m}", [QROWS, HP, NWIN, 2, PX], BF16) for m in range(2)]
        Ksel = [sb(f"Ksel{m}", [QROWS, NWIN, HP, TOPK, PX], BF16) for m in range(2)]
        Vsel = [sb(f"Vsel{m}", [128, NWIN, 2, HEADS, HD + 1]) for m in range(2)]
        Mx = [sb(f"Mx{m}", [128, HP, NWIN]) for m in range(2)]
        Mr = sb("Mr", [128, HP * NWIN])
        Mb = [sb(f"Mb{m}", [128, 3, HP * NWIN], BF16) for m in range(2)]
        MT = [sb(f"MT{m}", [NMAX, 2, PX], BF16) for m in range(2)]
        Pr = [sb(f"Pr{k}", [128, 2, HP, 2, PX]) for k in range(2)]
        O = [sb(f"O{m}", [128, NWIN, 2, PX]) for m in range(2)]
        Rb = sb("Rb", [128, NWIN * 2 * PX])
        sums = sb("sums", [128, SUMS // 128])
        rsums = sb("rsums", [128, SUMS // 128])
        Qk = [Rb[:, ROW * m:ROW * m + ROW] for m in range(2)]
        Part = [[part0[m][:] for m in range(2)],
                [Vsel[m][:].rearrange("p w c h e -> p (w c h e)").bitcast(BF16)[:, 0:3 * ROW]
                 .rearrange("p (k x) -> p k x", k=3) for m in range(2)]]
        Cen = [O[k][:].rearrange("c w a q -> c (w a q)")[:, 0:ROW] for k in range(2)]
        Sq = [O[k][:].rearrange("c w a q -> c (w a q)")[:, ROW:2 * ROW] for k in range(2)]
        Std = [Pr[k][:].rearrange("q c p h x -> q (c p h x)")[:, 0:ROW] for k in range(2)]
        Rstd = [Pr[k][:].rearrange("q c p h x -> q (c p h x)")[:, 512:512 + ROW] for k in range(2)]

        ps = ctx.enter_context(nc.psum_tensor("ps", [128, 8, 512], F32))
        ST0, OB, MISC = 2, 6, 7

        gate = {e: sem(f"gate_{e}") for e in ("pe", "act", "dve", "pool", "sp")}
        w_loaded = sem("w_loaded")
        less_step = sem("less_step")
        ob_set = sem("ob_set")
        init_done = sem("init_done")
        woh_loaded = sem("woh_loaded")
        x_loaded = [sem(f"x_loaded{k}") for k in range(2)]
        mean_ready = sem("mean_ready")
        cen_ready = sem("cen_ready")
        sq_ready = sem("sq_ready")
        var_ready = sem("var_ready")
        std_ready = sem("std_ready")
        rstd_ready = sem("rstd_ready")
        xn_ready = sem("xn_ready")
        xm_ready = sem("xm_ready")
        xms_ready = sem("xms_ready")
        qk_ready = sem("qk_ready")
        v_ready = sem("v_ready")
        qk_sb = sem("qk_sb")
        part1 = sem("part1")
        res1 = sem("res1")
        part2 = sem("part2")
        part3 = sem("part3")
        parts_stored = [sem(f"parts_stored{k}") for k in range(2)]
        vt_sb = sem("vt_sb")
        vT_ready = sem("vT_ready")
        vpx_done = sem("vpx_done")
        win_ready = sem("win_ready")
        win_sb = sem("win_sb")
        logits_ready = sem("logits_ready")
        lg_sb = sem("lg_sb")
        top_ready = sem("top_ready")
        idx_ready = sem("idx_ready")
        idx_stored = sem("idx_stored")
        k_loaded = sem("k_loaded")
        q_loaded = [sem(f"q_loaded{m}") for m in range(2)]
        mt_ready = sem("mt_ready")
        mt_copied = sem("mt_copied")
        k_gathered = sem("k_gathered")
        v_gathered = sem("v_gathered")
        s_ready = sem("s_ready")
        max_done = sem("max_done")
        m_split = sem("m_split")
        st_ready = sem("st_ready")
        exp_done = sem("exp_done")
        pv_done = sem("pv_done")
        o_copied = sem("o_copied")
        misc_ready = sem("misc_ready")
        misc_free = sem("misc_free")
        sums_out = sem("sums_out")
        sums_in = sem("sums_in")
        rsums_ready = sem("rsums_ready")
        rsums_out = sem("rsums_out")
        rb_loaded = sem("rb_loaded")
        on_ready = sem("on_ready")
        tap_done = sem("tap_done")
        x2_stored = sem("x2_stored")
        u_stored = [sem(f"u_stored{k}") for k in range(2)]

        block = ctx.enter_context(nc.Block())
        LAST = NWIN - 1
        N_W = 3 + 6 * HD + 12
        UNITS = 2 * NWIN
        MISC_DUO = 3 * NWIN

        def unit_of(d, i, m):
            return d * UNITS + i * 2 + m

        def misc_no(d, i, what):
            return d * MISC_DUO + i * 3 + ("conv", 0, 1).index(what)

        def tiles(eng, body):
            with eng.Fori(0, NWIN // 2) as j:
                body(j * 2, 0, False)
                body(j * 2 + 1, 1, False)
            body(LAST, 0, True)

        def u_count(d, i, k):
            return d * (64 - 16 * k) + (i - k) * 8 + 16

        def parts_count(d, i, k):
            return d * (112 * (8 - 2 * k)) + (i - k) * 112 + 16

        def hold(eng, name, s, value):
            eng.wait_ge(s, value)
            eng.sem_inc(gate[name], 1)

        @block.sync
        def _(sp):
            sp.dma_start(ones64[:, :], mats[0]).then_inc(w_loaded, 16)
            sp.dma_start(ident[:, :], mats[1]).then_inc(w_loaded, 16)
            sp.dma_start(each[:, :], mats[2, 0:NMAX, 0:HP * NWIN]).then_inc(w_loaded, 16)
            bias = qkv_b.rearrange("(s p h d) -> s h d p", s=3, p=HP, h=2)
            for h2 in range(2):
                q = HP * HD
                for out, s in ((bqk[q * h2:q * h2 + q, :], 0), (bqk[C + q * h2:C + q * h2 + q, :], 1),
                               (bk0[q * h2:q * h2 + q, :], 1)):
                    with nc.allow_non_contiguous_dma(reason="32 words"):
                        for e in range(HD):
                            sp.dma_start(out[HP * e:HP * e + HP], bias[s, h2, e:e + 1, :].rearrange("a p -> p a"))\
                              .then_inc(w_loaded, 16)
            for m in range(2):
                half = slice(C * m, C * m + C)
                sp.dma_start(wraw[half, :], qkv_w[:, 0:2 * C]).then_inc(w_loaded, 16)
                sp.dma_start(wv[half, :], qkv_w[:, 2 * C:3 * C]).then_inc(w_loaded, 16)
                sp.dma_start(bv[half, :], qkv_b[2 * C:3 * C].rearrange("(c a) -> c a", a=1)).then_inc(w_loaded, 16)
                sp.dma_start(taps[half, :], lepe_w.rearrange("c a i j -> c (a i j)")).then_inc(w_loaded, 16)
                sp.dma_start(wo[half, :], wo_w).then_inc(w_loaded, 16)
                sp.dma_start(wob[half, :], wo_b.rearrange("(c a) -> c a", a=1)).then_inc(w_loaded, 16)
            sp.wait_ge(ob_set, 2)
            sp.wait_ge(init_done, 5)
            wo4 = wo_w.rearrange("(g j d) e -> j d g e", g=2, j=4)
            for j in range(4):
                sp.dma_start(woh[32 * j:32 * j + HD, :, :], wo4[j]).then_inc(woh_loaded, 16)

            def load_q(m, i, g):
                hold(sp, "sp", st_ready, g * NWIN + NWIN)
                for h2 in range(2):
                    sp.dma_start(Qbd[m][TR * h2:TR * h2 + TR, :, :, h2, :].rearrange("r p w x -> r (p w) x"),
                                 q_dram[m, :, h2][bass.ds(i, 1)].rearrange("a t (d p) (w x) -> (a t d) (p w) x", p=HP, x=PX))\
                        .then_inc(q_loaded[m], 16)

            def turn_sums(m, g):
                hold(sp, "sp", o_copied, g * 2 + 3)
                sp.dma_start(sums_dram[m], O[m][HD:128:32].rearrange("j w a q -> j (w a q)")).then_inc(sums_out, 16)
                hold(sp, "sp", sums_out, g * 16 + 16)
                sp.dma_start(sums[:, :], sums_dram[m].rearrange("j (p x) -> (j p) x", p=32)).then_inc(sums_in, 16)
                hold(sp, "sp", rsums_ready, g + 1)
                sp.dma_start(rsums_dram[m].rearrange("j (p x) -> (j p) x", p=32), rsums[:, :]).then_inc(rsums_out, 16)
                hold(sp, "sp", rsums_out, g * 16 + 16)
                hold(sp, "sp", on_ready, g + 1)
                for j in range(4):
                    sp.dma_start(Rb[32 * j:32 * j + HD, :], rsums_dram[m, j].partition_broadcast(HD))\
                        .then_inc(rb_loaded, 16)

            with sp.Fori(0, duos) as d:
                hold(sp, "sp", x2_stored, d * (16 * NWIN) + 16)
                for k, cols in enumerate((slice(0, ROW), slice(ROW, TOKENS))):
                    sp.dma_start(X[:, cols], xv[bass.ds(d * 128, 128), cols]).then_inc(x_loaded[k], 16)
                def store_parts(i, k, last):
                    for m in range(2):
                        hold(sp, "sp", part3, d * UNITS + i * 2 + (m + 1))
                        for h2 in range(2):
                            rows = slice(HD * HP * h2, HD * HP * h2 + HD * HP)
                            for part, t, nt in ((0, 0, 3), (1, 3, 2), (2, 5, 1)):
                                sp.dma_start(q_dram[m, :, h2, t:t + nt][bass.ds(i, 1)].rearrange("a t c x -> (a c) t x"),
                                             Part[k][m][rows, part:part + 1, :].broadcast_to([HD * HP, nt, ROW]))\
                                    .then_inc(parts_stored[k], 16)
                        sp.dma_start(k_dram[m].rearrange("k c x -> c k x")[:, :, bass.ds(i * ROW, ROW)],
                                     Part[k][m][C:2 * C]).then_inc(parts_stored[k], 16)

                tiles(sp, store_parts)
                hold(sp, "sp", parts_stored[0], parts_count(d, 8, 0))
                hold(sp, "sp", parts_stored[1], parts_count(d, 7, 1))
                for m in range(2):
                    for h2 in range(2):
                        for t, (_, part) in enumerate(TERMS):
                            r = TR * h2 + HD * t
                            src = k_dram[m, part].rearrange("(h d p) x -> h d (p x)", h=2, p=HP)[h2]
                            sp.dma_start(Kexp[m][r:r + HD].rearrange("d p x -> d (p x)"), src)\
                              .then_inc(k_loaded, 16)
                hold(sp, "sp", idx_ready, d * 2 + 2)
                for m in range(2):
                    sp.dma_start(idxrow[0:1, m, :].rearrange("a (w k) -> a w k", k=TOPK),
                                 idx[:, m, 0:TOPK].bitcast(I32)).then_inc(idx_stored, 16)
                load_q(0, 0, unit_of(d, 0, 0))

                def rows(i, first=False, last=False):
                    load_q(1, i, unit_of(d, i, 1))
                    if not first:
                        turn_sums(1, unit_of(d, i - 1, 1))
                    if not last:
                        load_q(0, i + 1, unit_of(d, i, 2))
                    turn_sums(0, unit_of(d, i, 0))

                rows(0, first=True)
                with sp.Fori(1, LAST) as i:
                    rows(i)
                rows(LAST, last=True)
                turn_sums(1, unit_of(d, LAST, 1))
                def store_tile(i, k, last):
                    hold(sp, "sp", xn_ready, d * UNITS + i + (NWIN + 1))
                    sp.dma_start(x2_dram[bass.ds(d * 128, 128), bass.ds(i * ROW, ROW)],
                                 X[:, bass.ds(i * ROW, ROW)]).then_inc(x2_stored, 16)
                    sp.dma_start(u_dram[bass.ds(d * 128, 128), bass.ds(i * ROW, ROW)],
                                 Xn[k][:, :]).then_inc(u_stored[k], 16)

                tiles(sp, store_tile)
            sp.wait_ge(x2_stored, duos * 16 * NWIN + 16)
            sp.wait_ge(u_stored[0], duos * 64 + 16)
            sp.wait_ge(u_stored[1], duos * 48 + 16)

        @block.gpsimd
        def _(pool):
            for m in range(2):
                nc.gpsimd.memset(Qbd[m][:], 0.0)
            nc.gpsimd.memset(eps[:, 0:1], 1e-6)
            nc.gpsimd.memset(eps[:, 1:2], 1e-5)
            nc.gpsimd.memset(Vimg[:], 0.0)
            nc.gpsimd.memset(woh[:], 0.0).then_inc(init_done, 1)
            pool.wait_ge(init_done, 5)
            regs = [pool.alloc_register(f"pool_win{k}") for k in range(TOPK)]

            def square(i, k, tt):
                hold(pool, "pool", cen_ready, tt + 1)
                nc.gpsimd.tensor_tensor(Sq[k], Cen[k], Cen[k], ALU.mult).then_inc(sq_ready, 1)

            with pool.Fori(0, duos) as d:
                tiles(pool, lambda i, k, last: square(i, k, d * UNITS + i))
                hold(pool, "pool", k_loaded, d * (16 * 24) + 16 * 24)
                hold(pool, "pool", idx_stored, d * 32 + 32)
                with pool.Fori(0, NWIN) as i:
                    for m in range(2):
                        src = Kexp[m][:, :, :].bitcast(I32)
                        dst = Ksel[m][:, :, :, :, :].bitcast(I32)
                        for w in range(NWIN):
                            hold(pool, "pool", st_ready, unit_of(d, i, m) * NWIN + (w + 1))
                            pool.load(regs, idxrow[0:1, m, bass.ds((i * NWIN + w) * TOPK, TOPK)])
                            win = [pool.snap(r, min_val=0, max_val=WINDOWS - 1) for r in regs]
                            for k in range(TOPK):
                                nc.gpsimd.tensor_copy(dst[:, w, :, k, :],
                                                      src[:, :, bass.ds(win[k] * (PX // 2), PX // 2)])\
                                    .then_inc(k_gathered, 1)
                tiles(pool, lambda i, k, last: square(i, k, d * UNITS + i + NWIN))

        @block.scalar
        def _(act):
            act.wait_ge(w_loaded, 16 * N_W)
            nc.scalar.activation(identb[:, :], ident[:, :], ACT.Copy).then_inc(init_done, 1)
            for k in range(2):
                nc.scalar.activation(wqk[:, C * k:C * k + C].rearrange("c (h d p) -> c h d p", h=2, p=HP),
                                     wraw[:, C * k:C * k + C].rearrange("c (p h d) -> c h d p", h=2, p=HP),
                                     ACT.Copy).then_inc(init_done, 1)
            act.wait_ge(init_done, 5)
            regs = [act.alloc_register(f"act_win{k}") for k in range(TOPK)]

            def deviation(k, tt, which):
                hold(act, "act", var_ready, tt + 1)
                nc.scalar.activation(Std[k], ps[:, k, 0:ROW], ACT.Sqrt, bias=eps[:, which:which + 1])\
                    .then_inc(std_ready, 1)

            def gather_v(m, i, w):
                act.load(regs, idxrow[0:1, m, bass.ds((i * NWIN + w) * TOPK, TOPK)])
                win = [act.snap(r, min_val=0, max_val=WINDOWS - 1) for r in regs]
                for k in range(TOPK):
                    half = slice(PX * (k % 2), PX * (k % 2) + PX)
                    nc.scalar.activation(Vsel[m][half, w, k // 2], Vpx[m][half, bass.ds(win[k], 1)],
                                         ACT.Copy).then_inc(v_gathered, 1)

            with act.Fori(0, duos) as d:
                def prepare(i, k, last):
                    t = d * NWIN + i
                    for m in range(2):
                        hold(act, "act", qk_ready, t * 2 + (m + 1))
                        nc.scalar.activation(
                            Qk[m].rearrange("c (w a b) -> c w a b", w=NWIN, a=WS),
                            ps[:, 2 + m, 0:ROW].rearrange("c (a w b) -> c w a b", w=NWIN, a=WS),
                            ACT.Identity, bias=bqk[:, 0:1]).then_inc(qk_sb, 1)
                    for m in range(2):
                        hold(act, "act", qk_sb, t * 2 + (m + 1))
                        hold(act, "act", parts_stored[k], parts_count(d, i, k))
                        nc.scalar.activation(Part[k][m][:, 0, :], Qk[m], ACT.Copy).then_inc(part1, 1)
                    hold(act, "act", v_ready, t + 1)
                    nc.scalar.activation(
                        Vimg[:, bass.ds(i * WS + 1, WS), 1:1 + SIDE],
                        ps[:, 4, 0:ROW].rearrange("c (a x) -> c a x", a=WS), ACT.Identity, bias=bv[:, 0:1])
                    if not last:
                        deviation(1 - k, d * UNITS + i + 1, 0)
                    for m in range(2):
                        hold(act, "act", res1, t * 2 + (m + 1))
                        nc.scalar.activation(Part[k][m][:, 1, :], Res[m][:, :], ACT.Copy).then_inc(part2, 1)
                    for c in range(2):
                        nc.scalar.activation(Vt[:, :, c, :].rearrange("c w (a b) -> c w a b", a=WS),
                                             ps[:, 4, 0:ROW].rearrange("c (a w b) -> c w a b", w=NWIN, a=WS),
                                             ACT.Identity, bias=bv[:, 0:1]).then_inc(vt_sb, 1)
                    for m in range(2):
                        hold(act, "act", vT_ready, t * 2 + (m + 1))
                        nc.scalar.activation(Vpx[m][:, bass.ds(i * NWIN, NWIN), :, 0:HD],
                                             ps[:, 5 + 2 * m, 0:ROW].rearrange("q (w h e) -> q w h e", w=NWIN, h=HEADS),
                                             ACT.Copy).then_inc(vpx_done, 1)

                deviation(0, d * UNITS, 0)
                tiles(act, prepare)
                hold(act, "act", idx_stored, d * 32 + 32)
                hold(act, "act", vpx_done, d * UNITS + UNITS)
                hold(act, "act", parts_stored[1], parts_count(d, 7, 1))
                for w in range(NWIN):
                    gather_v(0, 0, w)

                def copy_o(m, sub, g):
                    nw = 4 - sub
                    hold(act, "act", pv_done, g * NWIN + (2 + 4 + 3 * sub))
                    nc.scalar.activation(O[m][:, 4 * sub:4 * sub + nw].rearrange("c w a q -> c (w a q)"),
                                         ps[:, OB, 0:nw * 128], ACT.Copy).then_inc(o_copied, 1)

                def unit(m, i, nxt, nm, ni, prev, first):
                    g = unit_of(d, i, m)
                    for w in range(NWIN):
                        n = g * NWIN + w
                        k = (m * NWIN + w) % 2
                        hold(act, "act", st_ready, n + (1 + 14))
                        hold(act, "act", pv_done, n + 1)
                        nc.scalar.activation(Pr[k][:].rearrange("q c p h x -> q (c p h x)"),
                                             ps[:, ST0 + 2 * k:ST0 + 2 * k + 2, :].rearrange("q a b -> q (a b)"),
                                             ACT.Exp, scale=SCALE).then_inc(exp_done, 1)
                        if w == 0 and prev:
                            copy_o(1 - m, 1, g - 1)
                        if w == 4:
                            if not first:
                                hold(act, "act", misc_ready, misc_no(d, i - 1, m) + 1)
                            copy_o(m, 0, g)
                        if nxt:
                            if w == 0:
                                hold(act, "act", pv_done, g * NWIN + 2)
                            gather_v(nm, ni, w)

                def rows(i, first=False, last=False):
                    unit(0, i, True, 1, i, not first, first)
                    unit(1, i, not last, 0, i + 1, True, first)

                rows(0, first=True)
                with act.Fori(1, LAST) as i:
                    rows(i)
                rows(LAST, last=True)
                copy_o(1, 1, unit_of(d, LAST, 1))
                tiles(act, lambda i, k, last: deviation(k, d * UNITS + i + NWIN, 1))

        @block.vector
        def _(dve):
            for m in range(2):
                nc.vector.memset(Vpx[m][:], 1.0)
            for n, (s, credit) in enumerate([(max_done, 2), (exp_done, 2), (pv_done, 2), (st_ready, 2 * NWIN),
                                             (o_copied, 1), (misc_free, 1), (on_ready, 1), (mt_copied, 1),
                                             (parts_stored[0], 16), (parts_stored[1], 16), (x2_stored, 16), (u_stored[0], 16),
                                             (u_stored[1], 16), (std_ready, 2)]):
                nc.vector.memset(nil[:, n:n + 1], 0.0).then_inc(s, credit)
            nc.vector.memset(ps[:, OB, :], 1.0).then_inc(ob_set, 1)
            nc.vector.memset(Rb[:, :], 1.0).then_inc(ob_set, 1)
            nc.vector.memset(less[:], 1.0).then_inc(less_step, 1)
            dve.wait_ge(w_loaded, 16 * N_W)
            dve.wait_ge(less_step, 1)
            for n in range(HP * NWIN):
                last = nc.vector.tensor_scalar(less[:, n, :], less[:, n, :], each[:, n:n + 1], None, ALU.mult)
            last.then_inc(init_done, 1)

            def centre(i, k, tt):
                hold(dve, "dve", mean_ready, tt + 1)
                nc.vector.tensor_tensor(Cen[k], X[:, bass.ds(i * ROW, ROW)], ps[:, k, 0:ROW], ALU.subtract)\
                    .then_inc(cen_ready, 1)

            def scale(k, tt, free):
                hold(dve, "dve", std_ready, tt + 3)
                nc.vector.reciprocal(Rstd[k], Std[k]).then_inc(rstd_ready, 1)
                hold(dve, "dve", rstd_ready, tt + 1)
                hold(dve, "dve", u_stored[k], free)
                nc.vector.tensor_tensor(Xn[k][:, :], Cen[k], Rstd[k], ALU.mult).then_inc(xn_ready, 1)

            def row_max(m, w, g):
                for half in range(2):
                    hold(dve, "dve", s_ready, g * 14 + (2 * w + half + 1))
                    nc.vector.tensor_reduce(Mx[m][:, 2 * half:2 * half + 2, w],
                                            ps[:, half, :].rearrange("q (p k) -> q p k", p=2),
                                            AX.X, ALU.max).then_inc(max_done, 1)

            def split_max(m, g):
                flat = Mx[m][:].rearrange("q p w -> q (p w)")
                hold(dve, "dve", max_done, g * 14 + 16)
                nc.vector.tensor_copy(Mb[m][:, 0, :], flat).then_inc(m_split, 1)
                hold(dve, "dve", m_split, g * 4 + 1)
                nc.vector.tensor_tensor(Mr[:, :], flat, Mb[m][:, 0, :], ALU.subtract).then_inc(m_split, 1)
                hold(dve, "dve", m_split, g * 4 + 2)
                nc.vector.tensor_copy(Mb[m][:, 1, :], Mr[:, :]).then_inc(m_split, 1)
                hold(dve, "dve", m_split, g * 4 + 3)
                nc.vector.tensor_tensor(Mb[m][:, 2, :], Mr[:, :], Mb[m][:, 1, :], ALU.subtract).then_inc(m_split, 1)

            def copy_max(m, g):
                hold(dve, "dve", mt_ready, g + 1)
                nc.vector.tensor_copy(MT[m][:].rearrange("r h x -> r (h x)"),
                                      ps[:, 0, :].bitcast(BF16)[0:NMAX, 0:128]).then_inc(mt_copied, 1)

            def invert(g):
                hold(dve, "dve", sums_in, g * 16 + 16)
                nc.vector.reciprocal(rsums[:, :], sums[:, :]).then_inc(rsums_ready, 1)

            def normalise(m, g):
                hold(dve, "dve", rb_loaded, g * 64 + 64)
                flat = O[m][:].rearrange("c w a q -> c (w a q)")
                nc.vector.tensor_tensor(flat, flat, Rb[:, :], ALU.mult).then_inc(on_ready, 1)

            with dve.Fori(0, duos) as d:
                hold(dve, "dve", x_loaded[0], d * 16 + 16)
                def prepare(i, k, last):
                    t = d * NWIN + i
                    tt = d * UNITS + i
                    if not last:
                        centre(i + 1, 1 - k, tt + 1)
                    hold(dve, "dve", xn_ready, tt + 1)
                    nc.vector.tensor_reduce(xm[:, bass.ds(i * NWIN, NWIN)],
                                            Xn[k][:, :].rearrange("c (a w b) -> c w a b", a=WS, w=NWIN),
                                            AX.XY, ALU.add).then_inc(xm_ready, 1)
                    for m in range(2):
                        hold(dve, "dve", part1, t * 2 + (m + 1))
                        nc.vector.tensor_tensor(Res[m][:, :], Qk[m], Part[k][m][:, 0, :], ALU.subtract).then_inc(res1, 1)
                    if not last:
                        scale(1 - k, tt + 1, d * (48 + 16 * k) + 16)
                    for m in range(2):
                        hold(dve, "dve", part2, t * 2 + (m + 1))
                        nc.vector.tensor_tensor(Part[k][m][:, 2, :], Res[m][:, :], Part[k][m][:, 1, :], ALU.subtract)\
                            .then_inc(part3, 1)
                    hold(dve, "dve", part3, t * 2 + 2)

                centre(0, 0, d * UNITS)
                scale(0, d * UNITS, d * 64 + 16)
                hold(dve, "dve", x_loaded[1], d * 16 + 16)
                tiles(dve, prepare)
                hold(dve, "dve", xm_ready, d * NWIN + NWIN)
                nc.vector.tensor_scalar(xms[:, :], xm[:, :], 1.0 / PX, None, ALU.mult).then_inc(xms_ready, 1)
                hold(dve, "dve", win_ready, d + 1)
                for m in range(2):
                    bank = 2 + 2 * m
                    nc.vector.tensor_scalar(qw[:, m, :], ps[0:C, bank, 0:WINDOWS], bqk[0:C, 0:1], None, ALU.add)\
                        .then_inc(win_sb, 1)
                    nc.vector.tensor_scalar(kw[:, m, :], ps[0:C, bank, C:C + WINDOWS], bk0[:, 0:1], None,
                                            ALU.add).then_inc(win_sb, 1)
                hold(dve, "dve", logits_ready, d + 1)
                nc.vector.tensor_copy(lg[:], ps[0:WINDOWS, 3, 0:128].rearrange("a (m b) -> a m b", m=2)[:, :, 0:WINDOWS])\
                    .then_inc(lg_sb, 1)
                hold(dve, "dve", lg_sb, d + 1)
                for m in range(2):
                    nc.vector.max(top[:, m, :], lg[:, m, :]).then_inc(top_ready, 1)
                hold(dve, "dve", top_ready, d * 2 + 2)
                for m in range(2):
                    nc.vector.max_index(idx[:, m, :], top[:, m, :], lg[:, m, :]).then_inc(idx_ready, 1)

                g0 = unit_of(d, 0, 0)
                for w in range(NWIN):
                    row_max(0, w, g0)
                split_max(0, g0)
                copy_max(0, g0)

                def tap(i, k):
                    done = (d * NWIN + i) * 9
                    a, b = k // 3, k % 3
                    src = Vimg[:, bass.ds(i * WS + a, WS), b:b + SIDE]
                    out = Lp[:, :].rearrange("c (y x) -> c y x", y=WS)
                    if k == 0:
                        nc.vector.tensor_scalar(out, src, taps[:, 0:1], None, ALU.mult).then_inc(tap_done, 1)
                    else:
                        hold(dve, "dve", tap_done, done + k)
                        nc.vector.scalar_tensor_tensor(out=out, in0=src, scalar=taps[:, k:k + 1], in1=out,
                                                       op0=ALU.mult, op1=ALU.add).then_inc(tap_done, 1)

                def add(i, what, rows, bias):
                    hold(dve, "dve", misc_ready, misc_no(d, i, what) + 1)
                    part = X[rows, bass.ds(i * ROW, ROW)]
                    if bias:
                        ins = nc.vector.scalar_tensor_tensor(out=part, in0=ps[rows, MISC, 0:ROW], scalar=wob[:, 0:1],
                                                             in1=part, op0=ALU.add, op1=ALU.add)
                    else:
                        hold(dve, "dve", misc_free, misc_no(d, i, what) + 1)
                        ins = nc.vector.tensor_tensor(part, part, ps[rows, MISC, 0:ROW], ALU.add)
                    ins.then_inc(misc_free, 1)

                def unit(m, i, nxt, prev, first):
                    g = unit_of(d, i, m)
                    wa = 0
                    for w in range(NWIN):
                        if nxt:
                            for _ in range(A_AT[w]):
                                row_max(1 - m, wa, g + 1)
                                wa += 1
                        if w == 2 and not first:
                            add(i - 1, m, slice(C * m, C * m + C), False)
                        if w == 3 and prev:
                            invert(g - 1)
                        if w == SPLIT_AT and nxt:
                            split_max(1 - m, g + 1)
                            copy_max(1 - m, g + 1)
                        if w == LAST and prev:
                            normalise(1 - m, g - 1)
                        for k, at in enumerate(TAPS_AT[m]):
                            if w == at:
                                tap(i, k + 5 * m)
                        if w == LAST and m == 1:
                            add(i, "conv", slice(0, 128), True)
                def rows(i, first=False, last=False):
                    unit(0, i, True, not first, first)
                    unit(1, i, not last, True, first)

                rows(0, first=True)
                with dve.Fori(1, LAST) as i:
                    rows(i)
                rows(LAST, last=True)
                g = unit_of(d, LAST, 1)
                add(LAST, 0, slice(0, C), False)
                invert(g)
                normalise(1, g)
                add(LAST, 1, slice(C, 2 * C), False)

                def after(i, k, last):
                    if not last:
                        hold(dve, "dve", xn_ready, d * UNITS + i + NWIN)
                        centre(i + 1, 1 - k, d * UNITS + i + (NWIN + 1))
                    scale(k, d * UNITS + i + NWIN, u_count(d, i, k))

                centre(0, 0, d * UNITS + NWIN)
                tiles(dve, after)

        @block.tensor
        def _(pe):
            mm = nc.tensor.matmul
            pe.wait_ge(w_loaded, 16 * N_W)
            pe.wait_ge(woh_loaded, 16 * 4)
            pe.wait_ge(init_done, 5)
            pe.wait_ge(ob_set, 2)

            def mean(i, k, tt):
                hold(pe, "pe", std_ready, tt + 1)
                mm(ps[:, k, 0:ROW], ones64[:, :], X[:, bass.ds(i * ROW, ROW)], start=True, stop=True)\
                    .then_inc(mean_ready, 1)

            def variance(k, tt):
                hold(pe, "pe", sq_ready, tt + 1)
                mm(ps[:, k, 0:ROW], ones64[:, :], Sq[k], start=True, stop=True).then_inc(var_ready, 1)

            def scores(m, w, g, halves=(0, 1)):
                if 0 in halves:
                    hold(pe, "pe", k_gathered, (g * NWIN + w) * TOPK + TOPK)
                if w == 0:
                    hold(pe, "pe", mt_copied, g + 1)
                for half in halves:
                    hold(pe, "pe", max_done, g * 14 + (2 * w + half + 1))
                    for p in (2 * half, 2 * half + 1):
                        last = mm(ps[:, half, (p % 2) * KEYS:(p % 2) * KEYS + KEYS], Qbd[m][0:QROWS, p, w, :, :].rearrange("r h x -> r (h x)"),
                                  Ksel[m][0:QROWS, w, p, :, :].rearrange("r k x -> r (k x)"), start=True, stop=True)
                    last.then_inc(s_ready, 1)

            def transpose_max(m, g):
                hold(pe, "pe", m_split, g * 4 + 4)
                nc.tensor.transpose(ps[:, 0, :].bitcast(BF16)[0:NMAX, 0:128],
                                    Mb[m][:].rearrange("q k n -> q (k n)"), identb[:, :]).then_inc(mt_ready, 1)

            def scores_t(m, w, g):
                n = g * NWIN + w
                k = (m * NWIN + w) % 2
                if w == 0:
                    hold(pe, "pe", mt_copied, g + 2)
                hold(pe, "pe", exp_done, n + 1)
                for c in range(2):
                    for p in range(HP):
                        out = ps[:, ST0 + 2 * k + c, p * 128:p * 128 + 128]
                        mm(out, Ksel[m][:, w, p, 2 * c:2 * c + 2, :].rearrange("r k x -> r (k x)"),
                           Qbd[m][:, p, w, :, :].rearrange("r h x -> r (h x)"), start=True, stop=False)
                        last = mm(out, less[:, p * NWIN + w, :], MT[m][:].rearrange("r h x -> r (h x)"),
                                  start=False, stop=True)
                last.then_inc(st_ready, 1)

            def weighted(m, w, g):
                n = g * NWIN + w
                k = (m * NWIN + w) % 2
                if w == 0:
                    hold(pe, "pe", v_gathered, g * 28 + 28)
                if w in (0, 4):
                    hold(pe, "pe", o_copied, g * 2 + (w // 4 + 1))
                hold(pe, "pe", exp_done, n + 3)
                col = (w % 4) * 128
                for a in range(2):
                    for c in range(2):
                        for j in range(4):
                            h = 4 * a + j
                            last = mm(ps[32 * j:32 * j + HD + 1, OB, col + 64 * a:col + 64 * a + 64],
                                      Vsel[m][:, w, c, h, :], Pr[k][:, c, h // 2, h % 2, :],
                                      start=(c == 0), stop=(c == 1))
                last.then_inc(pv_done, 1)

            with pe.Fori(0, duos) as d:
                hold(pe, "pe", x_loaded[0], d * 16 + 16)
                def prepare(i, k, last):
                    t = d * NWIN + i
                    if not last:
                        mean(i + 1, 1 - k, d * UNITS + i + 1)
                    hold(pe, "pe", xn_ready, d * UNITS + i + 1)
                    for m in range(2):
                        half = slice(C * m, C * m + C)
                        mm(ps[:, 2 + m, 0:ROW], wqk[half, :], Xn[k][half, :], start=True, stop=True).then_inc(qk_ready, 1)
                    for m in range(2):
                        half = slice(C * m, C * m + C)
                        last_mm = mm(ps[half, 4, 0:ROW], wv[half, :], Xn[k][half, :], start=True, stop=True)
                    last_mm.then_inc(v_ready, 1)
                    if not last:
                        variance(1 - k, d * UNITS + i + 1)
                    hold(pe, "pe", vt_sb, t * 2 + 2)
                    for m in range(2):
                        half = slice(C * m, C * m + C)
                        for w in range(NWIN):
                            twice = Vt[half, w].rearrange("c k x -> c (k x)")
                            last_mm = nc.tensor.transpose(ps[:, 5 + 2 * m, w * C:w * C + C], twice, ident[half, half])
                        last_mm.then_inc(vT_ready, 1)

                hold(pe, "pe", std_ready, d * UNITS + 2)
                mean(0, 0, d * UNITS)
                variance(0, d * UNITS)
                hold(pe, "pe", x_loaded[1], d * 16 + 16)
                tiles(pe, prepare)
                hold(pe, "pe", xms_ready, d + 1)
                for m in range(2):
                    half = slice(C * m, C * m + C)
                    mm(ps[0:C, 2 + 2 * m, 0:WINDOWS], wqk[half, 0:C], xms[half, :], start=True, stop=True)
                    last = mm(ps[0:C, 2 + 2 * m, C:C + WINDOWS], wqk[half, C:2 * C], xms[half, :],
                              start=True, stop=True)
                last.then_inc(win_ready, 1)
                hold(pe, "pe", win_sb, d * 4 + 4)
                for m in range(2):
                    last = mm(ps[0:WINDOWS, 3, C * m:C * m + WINDOWS], qw[:, m, :], kw[:, m, :], start=True, stop=True)
                last.then_inc(logits_ready, 1)

                g0 = unit_of(d, 0, 0)
                hold(pe, "pe", vpx_done, d * UNITS + UNITS)
                hold(pe, "pe", lg_sb, d + 1)
                hold(pe, "pe", q_loaded[0], d * (32 * NWIN) + 32)
                for w in range(NWIN):
                    scores(0, w, g0)
                transpose_max(0, g0)

                def project(i, m):
                    hold(pe, "pe", misc_free, misc_no(d, i, m) + 1)
                    hold(pe, "pe", on_ready, unit_of(d, i, m) + 2)
                    for a in range(2):
                        last_mm = mm(ps[C * m:C * m + C, MISC, 0:ROW], woh[:, a, :],
                                     O[m][:, :, a, :].rearrange("c w (y x) -> c y w x", y=WS),
                                     start=(a == 0), stop=(a == 1))
                    last_mm.then_inc(misc_ready, 1)

                def project_conv(i):
                    hold(pe, "pe", misc_free, misc_no(d, i, "conv") + 1)
                    hold(pe, "pe", tap_done, (d * NWIN + i) * 9 + 9)
                    for m in range(2):
                        half = slice(C * m, C * m + C)
                        last_mm = mm(ps[half, MISC, 0:ROW], wo[half, :], Lp[half, :], start=True, stop=True)
                    last_mm.then_inc(misc_ready, 1)

                def unit(m, i, nxt, prev, first):
                    g = unit_of(d, i, m)
                    wa = 0
                    for w in range(NWIN):
                        if nxt and w == 1:
                            hold(pe, "pe", q_loaded[1 - m], (d * NWIN + i) * 32 + (32 + 32 * m))
                        if nxt and A_AT[w] == 2:
                            scores(1 - m, wa, g + 1)
                            wa += 1
                        scores_t(m, w, g)
                        if nxt and A_AT[w]:
                            scores(1 - m, wa, g + 1, (0,))
                        if w > 0:
                            weighted(m, w - 1, g)
                        elif prev:
                            weighted(1 - m, LAST, g - 1)
                        if nxt and A_AT[w]:
                            scores(1 - m, wa, g + 1, (1,))
                            wa += 1
                        if w == 1 and not first:
                            project(i - 1, m)
                        if w == SPLIT_AT and nxt:
                            transpose_max(1 - m, g + 1)
                        if w == LAST and m == 1:
                            project_conv(i)

                def rows(i, first=False, last=False):
                    unit(0, i, True, not first, first)
                    unit(1, i, not last, True, first)

                rows(0, first=True)
                with pe.Fori(1, LAST) as i:
                    rows(i)
                rows(LAST, last=True)
                weighted(1, LAST, unit_of(d, LAST, 1))
                project(LAST, 0)
                project(LAST, 1)
                hold(pe, "pe", misc_free, d * MISC_DUO + (MISC_DUO + 1))

                def after(i, k, last):
                    if not last:
                        mean(i + 1, 1 - k, d * UNITS + i + (NWIN + 1))
                    variance(k, d * UNITS + i + NWIN)

                hold(pe, "pe", std_ready, d * UNITS + (NWIN + 2))
                mean(0, 0, d * UNITS + NWIN)
                tiles(pe, after)


def mixer(nc, u_dram, x2_dram, sigma, phi, m_u, m_plus, m_minus, log_weights, gumbel,
          dft, fwd, inv, idft, inmask, outmask, out_dram):
    n_img = u_dram.shape[0] // C
    COLS = n_img * C
    RA = 2 * AL
    s1_dram = nc.dram_tensor("s1_dram", (2, AL, NB, COLS), F32).ap()
    sp_dram = nc.dram_tensor("sp_dram", (2, AL, NB, KAP), F32).ap()
    z_dram = nc.dram_tensor("z_dram", (AL, n_img, 4, 16 * 2 * C), F32).ap()
    y1_dram = nc.dram_tensor("y1_dram", (2, AL, NB, COLS), F32).ap()

    with ExitStack() as outer:
        def sem(name):
            return outer.enter_context(nc.semaphore(name))

        gate = {e: sem(f"mgate_{e}") for e in ("pe", "act", "dve", "pool", "sp")}

        def hold(eng, name, s, value):
            eng.wait_ge(s, value)
            eng.sem_inc(gate[name], 1)

        def in_two(n):
            return slice(0, n // 16 * 16), slice(n // 16 * 16, n)

        def tensor(ctx, name, shape, dt=F32):
            return ctx.enter_context(nc.sbuf_tensor(name, shape, dt))

        ps = outer.enter_context(nc.psum_tensor("mps", [128, 8, 512], F32))
        E4 = tensor(outer, "E4", [RA, BRANCHES, NA])
        filters = outer.enter_context(ExitStack())
        Gs = tensor(filters, "Gs", [128, 2, 2, NB, C])
        Mbd = tensor(filters, "Mbd", [128, 2, C, C])

        with ExitStack() as ctx:
            D1 = tensor(ctx, "D1", [NA, RA])
            D4 = tensor(ctx, "D4", [NA, BRANCHES, RA])
            Ei = tensor(ctx, "Ei", [RA, NA])
            z8 = tensor(ctx, "z8", [128, 8])
            gum = tensor(ctx, "gum", [128, BRANCHES])
            top = tensor(ctx, "mtop", [128, 8])
            idx = tensor(ctx, "midx", [128, 8], U32)
            idf = tensor(ctx, "idf", [128, 1])
            ex = tensor(ctx, "ex", [128, BRANCHES])
            tot = tensor(ctx, "tot", [128, 1])
            rtot = tensor(ctx, "rtot", [128, 1])
            step = tensor(ctx, "step", [128, BRANCHES])
            one = tensor(ctx, "one", [128, BRANCHES])
            wgt = tensor(ctx, "wgt", [128, BRANCHES])
            dif = tensor(ctx, "dif", [128, BRANCHES])
            inm = tensor(ctx, "inm", [NA, BRANCHES, 4])
            inms = tensor(ctx, "inms", [NA, 4])
            outm = tensor(ctx, "outm", [RA, BRANCHES, 4 * NA])
            outs = tensor(ctx, "outs", [RA, 4 * NA])
            sig = tensor(ctx, "sig", [128, KPHI])
            sq1 = tensor(ctx, "sq1", [128, KPHI])
            sk = tensor(ctx, "sk", [128, KPHI])
            pht = tensor(ctx, "pht", [NA, NB, KPHI])
            U = [tensor(ctx, f"U{k}", [NA, C, NB]) for k in range(2)]
            S1 = [tensor(ctx, f"S1{k}", [RA, NB, 2, C]) for k in range(2)]

            fil = S1[0][0:NA].rearrange("a c b d -> a (c b d)")[:, 0:KAP * NB].rearrange("a (k c) -> a k c", k=KAP)
            Sp = S1[1][:].rearrange("r c b d -> r (c b d)")[:, 0:NB * KAP].rearrange("r (c k) -> r c k", k=KAP)

            ws_loaded = sem("ws_loaded")
            m_loaded = sem("mm_loaded")
            v_step = sem("v_step")
            sk_step = sem("sk_step")
            exp_ready = sem("exp_ready")
            fil_step = sem("fil_step")
            phi_mm = sem("phi_mm")
            phi_sb = sem("phi_sb")
            phi_stored = sem("phi_stored")
            mats_ready = sem("mats_ready")
            u_in = [sem(f"u_in{j}") for j in range(2)]
            s1_mm = sem("s1_mm")
            s1_act = sem("s1_act")
            s1_dve = sem("s1_dve")
            s1_stored = [sem(f"s1_stored{k}") for k in range(2)]
            cleared = sem("cleared")

            block = ctx.enter_context(nc.Block())
            N_WS = 8

            @block.sync
            def _(sp):
                sp.dma_start(z8[:, 0:BRANCHES], log_weights.partition_broadcast(128)).then_inc(ws_loaded, 16)
                sp.dma_start(gum[:, :], gumbel.partition_broadcast(128)).then_inc(ws_loaded, 16)
                sp.dma_start(sig[:, :], sigma.partition_broadcast(128)).then_inc(ws_loaded, 16)
                sp.dma_start(pht[0:32], phi.rearrange("(a c) k -> a c k", c=NB)).then_inc(ws_loaded, 16)
                sp.dma_start(D1[:, :], dft).then_inc(ws_loaded, 16)
                sp.dma_start(Ei[:, :], idft).then_inc(ws_loaded, 16)
                sp.dma_start(inm[:, :, :], inmask).then_inc(ws_loaded, 16)
                sp.dma_start(outm[:].rearrange("r i x -> r (i x)"), outmask.partition_broadcast(RA)).then_inc(ws_loaded, 16)
                raw = Gs[:].rearrange("p a r b e -> p (a r) (b e)")
                for r in (0, C):
                    sp.dma_start(raw[r:r + KPHI], m_plus.rearrange("i k d e -> k i (d e)")).then_inc(m_loaded, 16)
                    sp.dma_start(raw[r + KPHI:r + 2 * KPHI], m_minus.rearrange("i k d e -> k i (d e)")).then_inc(m_loaded, 16)
                    sp.dma_start(raw[r + 2 * KPHI:r + KAP], m_u.rearrange("i k d e -> k i (d e)")).then_inc(m_loaded, 16)
                sp.wait_ge(cleared, 2)

                def load(j, n):
                    hold(sp, "sp", s1_mm, n * 8 + 8)
                    src = u_dram[bass.ds(n * C, C), :].rearrange("d (a c) -> a d c", c=NB)
                    for rows in in_two(NA):
                        sp.dma_start(U[j][rows], src[rows]).then_inc(u_in[j], 16)

                def store(k, p):
                    hold(sp, "sp", s1_act, p * 8 + 12)
                    hold(sp, "sp", s1_dve, p * 8 + 12)
                    dst = s1_dram.rearrange("r a c x -> (r a) c x")[:, :, bass.ds(p * 2 * C, 2 * C)]
                    for rows in in_two(RA):
                        sp.dma_start(dst[rows], S1[k][rows].rearrange("r c b d -> r c (b d)")).then_inc(s1_stored[k], 16)

                load(0, 0)
                load(1, 1)
                sp.wait_ge(phi_sb, 5)
                sp.dma_start(sp_dram.rearrange("r a c k -> (r a) (c k)"), Sp.rearrange("r c k -> r (c k)"))\
                    .then_inc(phi_stored, 16)
                with sp.Fori(0, n_img // 4 - 1) as q:
                    for k in range(2):
                        load(0, q * 4 + (2 * k + 2))
                        load(1, q * 4 + (2 * k + 3))
                        store(k, q * 2 + k)
                load(0, n_img - 2)
                load(1, n_img - 1)
                store(0, n_img // 2 - 2)
                store(1, n_img // 2 - 1)
                for k in range(2):
                    sp.wait_ge(s1_stored[k], n_img // 4 * 32 + 16)
                sp.wait_ge(phi_stored, 16)

            @block.gpsimd
            def _(pool):
                nc.gpsimd.memset(Mbd[:], 0.0).then_inc(cleared, 1)
                nc.gpsimd.memset(fil, 0.0).then_inc(cleared, 1)

            @block.scalar
            def _(act):
                act.wait_ge(ws_loaded, 16 * N_WS)
                nc.scalar.activation(sq1[:, :], sig[:, :], ACT.Sqrt).then_inc(sk_step, 1)
                act.wait_ge(sk_step, 1)
                nc.scalar.activation(sk[:, :], sq1[:, :], ACT.Sqrt).then_inc(sk_step, 1)
                act.wait_ge(v_step, 3)
                nc.scalar.activation(ex[:, :], z8[:, 4:8], ACT.Exp).then_inc(exp_ready, 1)
                for n in range(5):
                    k0, nk = 8 * n, min(8, KAP - 8 * n)
                    act.wait_ge(phi_mm, n + 1)
                    nc.scalar.activation(Sp[:, :, k0:k0 + nk].rearrange("r c k -> r k c"),
                                         ps[0:RA, n, 0:nk * NB].rearrange("r (k c) -> r k c", k=nk),
                                         ACT.Copy).then_inc(phi_sb, 1)

                def evacuate(k, j, q):
                    n = q * 4 + (2 * k + j)
                    for m in range(0, 8, 2):
                        cls, d0, nd = CUTS[m]
                        c0, w = CLASSES[cls]
                        hold(act, "act", s1_mm, n * 8 + (m + 17))
                        if m == 0:
                            hold(act, "act", s1_stored[k], q * 32 + 16)
                        nc.scalar.activation(S1[k][:, c0:c0 + w, j, d0:d0 + nd].rearrange("r c d -> r d c"),
                                             ps[0:RA, m, :].rearrange("r (d c) -> r d c", c=w),
                                             ACT.Copy).then_inc(s1_act, 1)

                act.wait_ge(phi_stored, 16)
                with act.Fori(0, n_img // 4) as q:
                    for k in range(2):
                        for j in range(2):
                            evacuate(k, j, q)

            @block.vector
            def _(dve):
                nc.vector.memset(dif[:, :], 0.0).then_inc(s1_mm, 16)
                nc.vector.memset(top[:, :], 0.0).then_inc(s1_act, 4)
                nc.vector.memset(ex[:, :], 0.0).then_inc(s1_dve, 4)
                nc.vector.memset(idf[:, :], 0.0).then_inc(s1_stored[0], 16)
                nc.vector.memset(rtot[:, :], 0.0).then_inc(s1_stored[1], 16)
                for i in range(BRANCHES):
                    nc.vector.memset(step[:, i:i + 1], float(i))
                dve.wait_ge(ws_loaded, 16 * N_WS)
                count = 0

                def step_done(ins):
                    nonlocal count
                    ins.then_inc(v_step, 1)
                    count += 1
                    dve.wait_ge(v_step, count)

                step_done(nc.vector.tensor_tensor(gum[:, :], gum[:, :], z8[:, 0:4], ALU.add))
                step_done(nc.vector.tensor_reduce(tot[:, :], gum[:, :], AX.X, ALU.max))
                step_done(nc.vector.tensor_scalar(z8[:, 4:8], gum[:, :], tot[:, 0:1], None, ALU.subtract))
                dve.wait_ge(exp_ready, 1)
                step_done(nc.vector.tensor_reduce(tot[:, :], ex[:, :], AX.X, ALU.add))
                step_done(nc.vector.reciprocal(rtot[:, :], tot[:, :]))
                step_done(nc.vector.tensor_scalar(z8[:, 0:4], ex[:, :], rtot[:, 0:1], None, ALU.mult))
                step_done(nc.vector.memset(z8[:, 4:8], -1.0))
                step_done(nc.vector.max(top[:, :], z8[:, :]))
                step_done(nc.vector.max_index(idx[:, :], top[:, :], z8[:, :]))
                step_done(nc.vector.tensor_copy(idf[:, :], idx[:, 0:1]))
                step_done(nc.vector.tensor_scalar(one[:, :], step[:, :], idf[:, 0:1], None, ALU.is_equal))
                step_done(nc.vector.tensor_tensor(dif[:, :], one[:, :], z8[:, 0:4], ALU.subtract))
                step_done(nc.vector.tensor_tensor(wgt[:, :], dif[:, :], z8[:, 0:4], ALU.add))
                dve.wait_ge(cleared, 2)
                dve.wait_ge(sk_step, 2)
                for k in range(KPHI):
                    last = nc.vector.tensor_scalar(fil[0:32, k, :], pht[0:32, :, k], sk[0:32, k:k + 1], None, ALU.mult)
                step_done(last)
                even = fil[0:32].rearrange("a k (c s) -> a k c s", s=2)
                nc.vector.tensor_scalar(even[:, KPHI:2 * KPHI, :, 0], even[:, 0:KPHI, :, 0], 1.0, None, ALU.mult)
                nc.vector.tensor_scalar(even[:, KPHI:2 * KPHI, :, 1], even[:, 0:KPHI, :, 1], -1.0, None, ALU.mult)
                for i in range(KAR):
                    last = nc.vector.memset(fil[0:1, 2 * KPHI + i, i:i + 1], 1.0)
                last.then_inc(fil_step, 1)
                for src, dst in ((inm, inms), (outm, outs)):
                    p = dst.shape[0]
                    step_done(nc.vector.tensor_scalar(dst[:, :], src[:, 0, :], one[0:p, 0:1], None, ALU.mult))
                    for i in range(1, BRANCHES):
                        step_done(nc.vector.scalar_tensor_tensor(out=dst[:, :], in0=src[:, i, :], scalar=one[0:p, i:i + 1],
                                                                 in1=dst[:, :], op0=ALU.mult, op1=ALU.add))
                for cls in range(4):
                    nc.vector.tensor_scalar(D4[:, cls, :], D1[:, :], inms[:, cls:cls + 1], None, ALU.mult)
                    last = nc.vector.tensor_tensor(E4[:, cls, :], Ei[:, :], outs[:, cls * NA:cls * NA + NA], ALU.mult)
                last.then_inc(mats_ready, 1)
                raw = Gs[:].rearrange("p a r b e -> p (a r) (b e)")

                def choose(h, i):
                    rows = slice(C * h, C * h + KAP)
                    dst = Mbd[rows, h].rearrange("p d e -> p (d e)")
                    if i == 0:
                        step_done(nc.vector.tensor_scalar(dst, raw[rows, 0, :], wgt[rows, 0:1], None, ALU.mult))
                    else:
                        step_done(nc.vector.scalar_tensor_tensor(out=dst, in0=raw[rows, i, :], scalar=wgt[rows, i:i + 1],
                                                                 in1=dst, op0=ALU.mult, op1=ALU.add))

                def evacuate(k, j, q):
                    n = q * 4 + (2 * k + j)
                    for m in range(1, 8, 2):
                        cls, d0, nd = CUTS[m]
                        c0, w = CLASSES[cls]
                        hold(dve, "dve", s1_mm, n * 8 + (m + 17))
                        if m == 1:
                            hold(dve, "dve", s1_stored[k], q * 32 + 16)
                        nc.vector.tensor_copy(S1[k][:, c0:c0 + w, j, d0:d0 + nd].rearrange("r c d -> r d c"),
                                              ps[0:RA, m, :].rearrange("r (d c) -> r d c", c=w)).then_inc(s1_dve, 1)

                dve.wait_ge(phi_stored, 16)
                dve.wait_ge(m_loaded, 16 * 6)
                for q in range(2):
                    for n in range(4):
                        evacuate(n // 2, n % 2, q)
                        choose(q, n)
                with dve.Fori(2, n_img // 4) as q:
                    for k in range(2):
                        for j in range(2):
                            evacuate(k, j, q)

            @block.tensor
            def _(pe):
                mm = nc.tensor.matmul
                pe.wait_ge(fil_step, 1)
                for n in range(5):
                    k0, nk = 8 * n, min(8, KAP - 8 * n)
                    mm(ps[0:RA, n, 0:nk * NB], D1[:, :], fil[:, k0:k0 + nk, :].rearrange("a k c -> a (k c)"),
                       start=True, stop=True).then_inc(phi_mm, 1)
                pe.wait_ge(phi_sb, 5)
                pe.wait_ge(mats_ready, 1)
                with pe.Fori(0, n_img // 2) as q:
                    for j in range(2):
                        n = q * 2 + j
                        hold(pe, "pe", u_in[j], q * 32 + 32)
                        for m, (cls, d0, nd) in enumerate(CUTS):
                            c0, w = CLASSES[cls]
                            hold(pe, "pe", s1_dve if m % 2 else s1_act, n * 4 + (m // 2 + 1))
                            mm(ps[0:RA, m, :], D4[:, cls, :], U[j][:, d0:d0 + nd, c0:c0 + w],
                               start=True, stop=True).then_inc(s1_mm, 1)

        with ExitStack() as ctx:
            Fw = tensor(ctx, "Fw", [128, 2, 3 * NB])
            Iv = tensor(ctx, "Iv", [128, 2, 2 * NB])
            Sf = tensor(ctx, "Sf", [128, 2, KAP])
            Sin = tensor(ctx, "Sin", [128, 2, COLS])
            Uh = [tensor(ctx, f"Uh{k}", [128, n_img, NB]) for k in range(2)]
            Vh = tensor(ctx, "Vh", [128, 2, 2 * NB])
            Zs = [tensor(ctx, f"Zs{k}", [128, 4, 4 * 2 * C]) for k in range(2)]
            Zr = [tensor(ctx, f"Zr{k}", [128, n_img, C]) for k in range(2)]
            Ys = [tensor(ctx, f"Ys{k}", [128, COLS]) for k in range(2)]
            nil = tensor(ctx, "mnil", [1, 16])

            in_loaded = sem("in_loaded")
            iv_loaded = sem("iv_loaded")
            v_mm = sem("v_mm")
            v_sb = sem("v_sb")
            g_mm = sem("g_mm")
            g_act = sem("g_act")
            g_dve = sem("g_dve")
            uh_mm = sem("uh_mm")
            uh_act = sem("uh_act")
            uh_dve = sem("uh_dve")
            z_mm = sem("z_mm")
            z_act = sem("z_act")
            z_dve = sem("z_dve")
            z_stored = [sem(f"z_stored{k}") for k in range(2)]
            z_loaded = [sem(f"z_loaded{k}") for k in range(2)]
            i_mm = sem("i_mm")
            i_act = sem("i_act")
            i_dve = sem("i_dve")
            y_stored = [sem(f"y_stored{k}") for k in range(2)]
            b_init = sem("b_init")

            block = ctx.enter_context(nc.Block())
            Z_BANK, I_BANK = 4, 6

            @block.sync
            def _(sp):
                def load_in(p):
                    for r in range(2):
                        half = slice(NB * r, NB * r + NB)
                        sp.dma_start(Sin[half], s1_dram[r].rearrange("a c x -> c a x")[:, bass.ds(p * 2, 2), :])\
                            .then_inc(in_loaded, 16)
                        sp.dma_start(Sf[half], sp_dram[r].rearrange("a c k -> c a k")[:, bass.ds(p * 2, 2), :])\
                            .then_inc(in_loaded, 16)
                    sp.dma_start(Fw[:], fwd[:, bass.ds(p * 2, 2), :]).then_inc(in_loaded, 16)

                def load_inverse(p):
                    sp.dma_start(Iv[:], inv[:, bass.ds(p * 2, 2), :]).then_inc(iv_loaded, 16)

                def store_inverse(p):
                    for k in range(2):
                        hold(sp, "sp", i_act, p * 2 + (k + 2))
                        hold(sp, "sp", i_dve, p * 2 + (k + 2))
                        for r in range(2):
                            half = slice(NB * r, NB * r + NB)
                            sp.dma_start(y1_dram[r].rearrange("a c x -> c a x")[:, bass.ds(p * 2 + k, 1), :]
                                         .rearrange("c a x -> c (a x)"), Ys[k][half, :]).then_inc(y_stored[k], 16)

                def turn(p):
                    for k in range(2):
                        hold(sp, "sp", z_act, p * 4 + (2 * k + 3))
                        hold(sp, "sp", z_dve, p * 4 + (2 * k + 3))
                        for q in range(4):
                            sp.dma_start(z_dram.rearrange("a b q x -> q a b x")[q][bass.ds(p * 2 + k, 1)]
                                         .rearrange("a b x -> (a b) x"),
                                         Zs[k][32 * q:32 * q + n_img].rearrange("b j x -> b (j x)")).then_inc(z_stored[k], 16)
                    for k in range(2):
                        hold(sp, "sp", z_stored[k], p * 64 + 80)
                        hold(sp, "sp", i_mm, p * 4 + 4)
                        sp.dma_start(Zr[k][:, :, :], z_dram[bass.ds(p * 2 + k, 1)]
                                     .rearrange("a b q (j e) -> (a q j) b e", e=C)).then_inc(z_loaded[k], 16)

                sp.wait_ge(b_init, 1)
                load_in(0)
                load_inverse(0)
                sp.wait_ge(uh_mm, 4)
                load_in(1)
                turn(0)

                def step(p, last):
                    store_inverse(p - 1)
                    load_inverse(p)
                    if not last:
                        hold(sp, "sp", uh_mm, p * 4 + 4)
                        load_in(p + 1)
                    turn(p)

                with sp.Fori(1, PAIRS - 1) as p:
                    step(p, False)
                step(PAIRS - 1, True)
                store_inverse(PAIRS - 1)
                for k in range(2):
                    sp.wait_ge(y_stored[k], PAIRS * 32 + 16)

            def copy_g(eng, name, copy, s, odd, p):
                hold(eng, name, z_mm, p * 8 + 1)
                for n in range(odd, 32, 2):
                    hold(eng, name, g_mm, p * 32 + (n + 1))
                    copy(Gs[:, :, :, :, 2 * n:2 * n + 2].rearrange("p a r b e -> p (a r) b e"),
                         ps[:, n % 4, :].rearrange("p (e x b) -> p x b e", e=2, b=NB)).then_inc(s, 1)

            def copy_uh(eng, name, copy, s, odd, p):
                for k in range(2):
                    hold(eng, name, uh_mm, p * 4 + (2 * k + odd + 1))
                    copy(Uh[k][:, 8 * odd:8 * odd + 8].rearrange("p b x -> p (b x)"), ps[:, 2 * k + odd, :]).then_inc(s, 1)

            def copy_z(eng, name, copy, s, odd, p):
                for t in range(odd, 8, 2):
                    if t < 4:
                        hold(eng, name, z_stored[0], p * 64 + 16)
                    else:
                        hold(eng, name, z_stored[1], p * 64 + 16)
                    hold(eng, name, z_mm, p * 8 + (t + 2))
                    copy(Zs[t // 4][:, t % 4, :], ps[:, Z_BANK + odd, :]).then_inc(s, 1)

            def copy_inverse(eng, name, copy, s, odd, p):
                for k in range(2):
                    hold(eng, name, i_mm, p * 4 + (2 * k + odd + 5))
                    hold(eng, name, y_stored[k], p * 32 + 16)
                    copy(Ys[k][:, 512 * odd:512 * odd + 512], ps[:, I_BANK + odd, :]).then_inc(s, 1)

            @block.scalar
            def _(act):
                def copy(out, in_):
                    return nc.scalar.activation(out, in_, ACT.Copy)

                act.wait_ge(b_init, 1)

                def step(p, first):
                    hold(act, "act", v_mm, p + 1)
                    copy(Vh[0:KAP].rearrange("k a x -> k (a x)"), ps[0:KAP, I_BANK, 0:256]).then_inc(v_sb, 1)
                    copy_g(act, "act", copy, g_act, 0, p)
                    if not first:
                        copy_inverse(act, "act", copy, i_act, 0, p - 1)
                    copy_uh(act, "act", copy, uh_act, 0, p)
                    copy_z(act, "act", copy, z_act, 0, p)

                step(0, True)
                with act.Fori(1, PAIRS) as p:
                    step(p, False)
                copy_inverse(act, "act", copy, i_act, 0, PAIRS - 1)

            @block.vector
            def _(dve):
                copy = nc.vector.tensor_copy
                nc.vector.memset(ps[:, Z_BANK:Z_BANK + 2, :], 0.0)
                nc.vector.memset(Vh[:], 0.0)
                for n, (s, credit) in enumerate([(g_act, 2), (g_dve, 2), (z_mm, 1), (z_act, 1), (z_dve, 1), (i_mm, 4),
                                                 (i_act, 1), (i_dve, 1), (z_stored[0], 16), (z_stored[1], 16),
                                                 (y_stored[0], 16), (y_stored[1], 16), (b_init, 1)]):
                    nc.vector.memset(nil[:, n:n + 1], 0.0).then_inc(s, credit)

                def step(p, first):
                    hold(dve, "dve", v_mm, p + 1)
                    copy(Vh[C:C + KAP].rearrange("k a x -> k (a x)"), ps[C:C + KAP, I_BANK, 0:256]).then_inc(v_sb, 1)
                    copy_g(dve, "dve", copy, g_dve, 1, p)
                    if not first:
                        copy_inverse(dve, "dve", copy, i_dve, 1, p - 1)
                    copy_uh(dve, "dve", copy, uh_dve, 1, p)
                    copy_z(dve, "dve", copy, z_dve, 1, p)

                dve.wait_ge(b_init, 1)
                step(0, True)
                with dve.Fori(1, PAIRS) as p:
                    step(p, False)
                copy_inverse(dve, "dve", copy, i_dve, 1, PAIRS - 1)

            @block.tensor
            def _(pe):
                mm = nc.tensor.matmul
                pe.wait_ge(b_init, 1)

                def inverse(p):
                    hold(pe, "pe", iv_loaded, p * 16 + 16)
                    for k in range(2):
                        hold(pe, "pe", z_loaded[k], p * 16 + 16)
                        for h in range(2):
                            hold(pe, "pe", i_dve if h else i_act, p * 2 + (k + 1))
                            mm(ps[:, I_BANK + h, :], Iv[:, k, :], Zr[k][:, 8 * h:8 * h + 8, :].rearrange("x b e -> x (b e)"),
                               start=True, stop=True).then_inc(i_mm, 1)

                def step(p, first):
                    hold(pe, "pe", in_loaded, p * 80 + 80)
                    if not first:
                        hold(pe, "pe", i_act, p * 2 - 1)
                    for k in range(2):
                        mm(ps[0:KAP, I_BANK, 128 * k:128 * k + 128], Sf[:, k, :], Fw[:, k, NB:3 * NB], start=True, stop=True)
                        last = mm(ps[C:C + KAP, I_BANK, 128 * k:128 * k + 128], Sf[:, k, :], Fw[:, k, 0:2 * NB],
                                  start=True, stop=True)
                    last.then_inc(v_mm, 1)
                    hold(pe, "pe", v_sb, p * 2 + 2)
                    for n in range(32):
                        hold(pe, "pe", g_dve if n % 2 else g_act, p * 16 + (n // 2 + 1))
                        for e in range(2):
                            last = mm(ps[:, n % 4, 256 * e:256 * e + 256],
                                      Mbd[:, :, :, 2 * n + e].rearrange("k h d -> k (h d)"),
                                      Vh[:].rearrange("k a x -> k (a x)"), start=True, stop=True)
                        last.then_inc(g_mm, 1)
                    if not first:
                        inverse(p - 1)
                    hold(pe, "pe", g_act, p * 16 + 18)
                    hold(pe, "pe", g_dve, p * 16 + 18)
                    for k in range(2):
                        for b in range(n_img):
                            bank, col = 2 * k + b // 8, (b % 8) * NB
                            mm(ps[0:C, bank, col:col + NB], Sin[:, k, b * C:b * C + C], Fw[:, k, NB:2 * NB],
                               start=True, stop=True)
                            last = mm(ps[C:2 * C, bank, col:col + NB], Sin[:, k, b * C:b * C + C], Fw[:, k, 2 * NB:3 * NB],
                                      start=True, stop=True)
                            if b % 8 == 7:
                                last.then_inc(uh_mm, 1)
                    for k in range(2):
                        hold(pe, "pe", uh_act, p * 2 + (k + 1))
                        hold(pe, "pe", uh_dve, p * 2 + (k + 1))
                        for jj in range(4):
                            t = 4 * k + jj
                            hold(pe, "pe", z_dve if t % 2 else z_act, p * 4 + (t // 2 + 1))
                            for j in range(4):
                                for q in range(4):
                                    be = 16 * q + 4 * jj + j
                                    last = mm(ps[32 * q:32 * q + n_img, Z_BANK + t % 2, 128 * j:128 * j + 128],
                                              Uh[k][:, :, be], Gs[:, k, :, be, :], start=True, stop=True)
                            last.then_inc(z_mm, 1)

                step(0, True)
                with pe.Fori(1, PAIRS) as p:
                    step(p, False)
                inverse(PAIRS - 1)

        filters.close()

        with ExitStack() as ctx:
            Y1 = [tensor(ctx, f"Y1{k}", [RA, NB, 2, C]) for k in range(2)]
            Xr = [tensor(ctx, f"Xr{k}", [NA, C, NB]) for k in range(4)]
            nil = tensor(ctx, "nil2", [1, 5])
            c_in = [sem(f"c_in{k}") for k in range(2)]
            c_mm = sem("c_mm")
            c_dve = sem("c_dve")
            c_stored = [sem(f"c_stored{k}") for k in range(2)]
            c_init = sem("c_init")
            block = ctx.enter_context(nc.Block())

            @block.sync
            def _(sp):
                sp.wait_ge(c_init, 1)

                def load(k, q):
                    p = q * 2 + k
                    hold(sp, "sp", c_mm, p * 16 + 16)
                    src = y1_dram.rearrange("r a c x -> (r a) c x")[:, :, bass.ds(p * 2 * C, 2 * C)]
                    for rows in in_two(RA):
                        sp.dma_start(Y1[k][rows].rearrange("r c b e -> r c (b e)"), src[rows]).then_inc(c_in[k], 16)
                    hold(sp, "sp", c_stored[k], q * 64 + 16)
                    for j in range(2):
                        src = x2_dram[bass.ds((p * 2 + j) * C, C), :].rearrange("e (a c) -> a e c", c=NB)
                        for rows in in_two(NA):
                            sp.dma_start(Xr[2 * k + j][rows], src[rows]).then_inc(c_in[k], 16)

                def store(k, q):
                    for j in range(2):
                        n = q * 4 + (2 * k + j)
                        hold(sp, "sp", c_dve, n * 8 + 16)
                        dst = out_dram[bass.ds(n * C, C), :].rearrange("e (a c) -> a e c", c=NB)
                        for rows in in_two(NA):
                            sp.dma_start(dst[rows], Xr[2 * k + j][rows]).then_inc(c_stored[k], 16)

                load(0, 0)
                with sp.Fori(0, n_img // 4 - 1) as q:
                    load(1, q)
                    store(0, q)
                    load(0, q + 1)
                    store(1, q)
                load(1, n_img // 4 - 1)
                store(0, n_img // 4 - 1)
                store(1, n_img // 4 - 1)
                for k in range(2):
                    sp.wait_ge(c_stored[k], n_img // 4 * 64 + 16)

            @block.vector
            def _(dve):
                for n, (s, credit) in enumerate([(c_mm, 32), (c_dve, 8), (c_stored[0], 16), (c_stored[1], 16)]):
                    nc.vector.memset(nil[:, n:n + 1], 0.0).then_inc(s, credit)
                nc.vector.memset(nil[:, 4:5], 0.0).then_inc(c_init, 1)
                with dve.Fori(0, n_img // 4) as q:
                    for k in range(2):
                        hold(dve, "dve", c_in[k], q * 96 + 96)
                        for j in range(2):
                            n = q * 4 + (2 * k + j)
                            for m, (cls, e0, ne) in enumerate(CUTS):
                                c0, w = CLASSES[cls]
                                part = Xr[2 * k + j][:, e0:e0 + ne, c0:c0 + w]
                                hold(dve, "dve", c_mm, n * 8 + (m + 33))
                                nc.vector.tensor_tensor(part, ps[0:NA, m, :].rearrange("a (e c) -> a e c", c=w), part,
                                                        ALU.add).then_inc(c_dve, 1)

            @block.tensor
            def _(pe):
                pe.wait_ge(c_init, 1)
                with pe.Fori(0, n_img // 4) as q:
                    for k in range(2):
                        hold(pe, "pe", c_in[k], q * 96 + 96)
                        for j in range(2):
                            n = q * 4 + (2 * k + j)
                            for m, (cls, e0, ne) in enumerate(CUTS):
                                c0, w = CLASSES[cls]
                                hold(pe, "pe", c_dve, n * 8 + (m + 1))
                                nc.tensor.matmul(ps[0:NA, m, :], E4[:, cls, :],
                                                 Y1[k][:, c0:c0 + w, j, e0:e0 + ne].rearrange("r c e -> r e c"),
                                                 start=True, stop=True).then_inc(c_mm, 1)


def dft_mats():
    import numpy as np
    al = np.arange(AL)
    a, c, be = np.arange(NB), np.arange(NB), np.arange(NB)
    t1 = 2 * np.pi * ((a[:NA, None] * al[None, :]) % NB) / NB
    dft = np.concatenate([np.cos(t1), -np.sin(t1)], 1)
    t2 = 2 * np.pi * ((c[:, None, None] * (al[None, :, None] + NB * be[None, None, :])) % NF) / NF
    re, im = np.cos(t2), -np.sin(t2)
    fwd = np.concatenate([np.concatenate([-im, re, im], 2), np.concatenate([-re, -im, re], 2)], 0)
    ce, se = np.cos(t2), np.sin(t2)
    inv = np.empty((NB, 2, AL, 2, NB))
    inv[:, 0, :, 0], inv[:, 1, :, 0] = ce.transpose(2, 1, 0), -se.transpose(2, 1, 0)
    inv[:, 0, :, 1], inv[:, 1, :, 1] = se.transpose(2, 1, 0), ce.transpose(2, 1, 0)
    weight = np.where((al == 0) | (al == 32), 1.0, 2.0) * (al < 33) / NF
    idft = np.concatenate([np.cos(t1) * weight, -np.sin(t1) * weight], 1).T
    cut = TOKENS // 2 ** np.arange(BRANCHES)
    first = np.array([c0 for c0, _ in CLASSES])
    inside = NB * a[:NA, None, None] + first[None, None, :] < cut[None, :, None]
    inmask = inside
    outmask = inside.transpose(1, 2, 0).reshape(-1)
    return [np.ascontiguousarray(m, np.float32) for m in (dft, fwd, inv.reshape(2 * NB, AL, 2 * NB), idft, inmask, outmask)]


def const_mats():
    import numpy as np
    mats = np.zeros((3, 128, 128), np.float32)
    for m in range(2):
        mats[0, C * m:C * m + C, C * m:C * m + C] = 1.0 / C
    mats[1] = np.eye(128, dtype=np.float32)
    for part in range(3):
        mats[2, HP * NWIN * part:HP * NWIN * (part + 1), 0:HP * NWIN] = -np.eye(HP * NWIN)
    return mats


_INPUTS = ["x", "L0_conv_qkv_w", "L0_conv_qkv_b", "L0_conv_lepe_w", "L0_conv_wo_w", "L0_conv_wo_b",
           "L0_ffn_sigma", "L0_ffn_phi", "L0_ffn_M_u", "L0_ffn_M_phi_plus", "L0_ffn_M_phi_minus",
           "L0_ffn_log_weights", "L0_ffn_gumbel"]


def kernel(**inputs):
    import numpy as np
    import concourse.bacc as _bacc
    from concourse import mybir as _mybir
    from concourse.bass_utils import run_bass_kernel_spmd as _run
    nc = _bacc.Bacc("TRN2", target_bir_lowering=False, num_devices=1)
    arrays = {}

    def given(name, array):
        arrays[name] = np.ascontiguousarray(array)
        return nc.dram_tensor(name, arrays[name].shape, _mybir.dt.from_np(arrays[name].dtype),
                              kind="ExternalInput").ap()

    x, qkv_w, qkv_b, lepe_w, wo_w, wo_b, *ffn = [given(f"in_{n}", inputs[n]) for n in _INPUTS]
    mats = given("att_mats", const_mats())
    dfts = [given(f"dft_mats{n}", m) for n, m in enumerate(dft_mats())]
    out = nc.dram_tensor("out0", x.shape, F32, kind="ExternalOutput").ap()
    rows = x.shape[0] * C
    x2_dram = nc.dram_tensor("x2_dram", (rows, TOKENS), F32).ap()
    u_dram = nc.dram_tensor("u_dram", (rows, TOKENS), F32).ap()
    attention(nc, x, qkv_w, qkv_b, lepe_w, wo_w, wo_b, mats, x2_dram, u_dram)
    mixer(nc, u_dram, x2_dram, *ffn, *dfts, out.rearrange("n c h w -> (n c) (h w)"))
    result = _run(nc, [arrays], core_ids=[0])
    return result.results[0]["out0"]
```
